# Optimizing a Trainium2 kernel written in Bass

```python
import numpy as np
import jax
import jax.numpy as jnp

def _softmax(x, axis=-1):
    return jax.nn.softmax(x, axis=axis)

def _gelu(x):
    return jax.nn.gelu(x, approximate=True)

def _silu(x):
    return jax.nn.silu(x)

def _sigmoid(x):
    return jax.nn.sigmoid(x)

def _layernorm(x, axis=-1, eps=1e-05):
    m = jnp.mean(x, axis=axis, keepdims=True)
    v = jnp.var(x, axis=axis, keepdims=True)
    return (x - m) / jnp.sqrt(v + eps)

def _scatter_add(tgt, idx, src, axis=0):
    return tgt.at[idx].add(src)

def _segment_sum(src, seg, n):
    return jax.ops.segment_sum(src, seg, n)
kernel_name = 'mk_seq_preln_d1_jaxref_r8_a20de1'

def setup_inputs(seed: int=0):
    np.random.seed(seed)
    _w = jnp.asarray

    def _L0_attn_setup():
        import jax, jax.numpy as jnp
        import numpy as np
        B, S, E, H = (4, 256, 128, 16)
        HD = E // H
        key = jax.random.key(seed)
        ks = jax.random.split(key, 9)
        s_in = 1.0 / np.sqrt(E)
        return {'x': jax.random.normal(ks[0], (B, S, E), dtype=jnp.float32), 'Wq': jax.random.normal(ks[1], (E, E), dtype=jnp.float32) * s_in, 'bq': jax.random.normal(ks[2], (E,), dtype=jnp.float32) * 0.01, 'Wk': jax.random.normal(ks[3], (E, E), dtype=jnp.float32) * s_in, 'bk': jax.random.normal(ks[4], (E,), dtype=jnp.float32) * 0.01, 'Wv': jax.random.normal(ks[5], (E, E), dtype=jnp.float32) * s_in, 'bv': jax.random.normal(ks[6], (E,), dtype=jnp.float32) * 0.01, 'Wo': jax.random.normal(ks[7], (E, E), dtype=jnp.float32) * s_in, 'bo': jax.random.normal(ks[8], (E,), dtype=jnp.float32) * 0.01}
    _L0_attn_in = _L0_attn_setup()

    def _L0_ffn_setup():
        import jax, jax.numpy as jnp
        import numpy as np
        DIM = 128
        DEPTH = 6
        HEADS = 16
        DIM_HEAD = 64
        WINDOW = 32
        INNER = HEADS * DIM_HEAD
        DIM_INNER = int(DIM * 4 * 2 / 3)
        QK_SCALE = 8.0

        def shift_tokens(t):
            a, s = jnp.split(t, 2, -1)
            s = jnp.pad(s, ((0, 0), (1, 0), (0, 0)))[:, :-1]
            return jnp.concatenate([a, s], -1)

        def l2norm(t):
            return t / jnp.maximum(jnp.linalg.norm(t, axis=-1, keepdims=True), 1e-12)

        def rotate_half(x):
            x1, x2 = jnp.split(x, 2, -1)
            return jnp.concatenate([-x2, x1], -1)

        def rotary_tables(n):
            half = jnp.arange(0, DIM_HEAD, 2, dtype=jnp.float32)
            inv_freq = 1.0 / 10000.0 ** (half / DIM_HEAD)
            t = jnp.arange(n, dtype=jnp.float32)
            freqs = t[:, None] * inv_freq[None, :]
            freqs = jnp.concatenate([freqs, freqs], -1)
            base_scale = (half + 0.4 * DIM_HEAD) / (1.4 * DIM_HEAD)
            power = (t - n // 2) / (WINDOW // 2)
            scale = base_scale[None, :] ** power[:, None]
            scale = jnp.concatenate([scale, scale], -1)
            return (freqs, scale)

        def local_attention(q, k, v):
            b, h, n, d = q.shape
            w = WINDOW
            nw = n // w
            bq = q.reshape(b, h, nw, w, d)
            bk = k.reshape(b, h, nw, w, d)
            bv = v.reshape(b, h, nw, w, d)

            def look(t):
                p = jnp.pad(t, ((0, 0), (0, 0), (1, 0), (0, 0), (0, 0)))
                return jnp.concatenate([p[:, :, :nw], p[:, :, 1:]], axis=3)
            bk2, bv2 = (look(bk), look(bv))
            seq = jnp.arange(n).reshape(nw, w)
            seq_p = jnp.pad(seq, ((1, 0), (0, 0)), constant_values=-1)
            jt = jnp.concatenate([seq_p[:nw], seq_p[1:]], axis=1)
            it = seq[:, :, None]
            jb = jt[:, None, :]
            mask = (it < jb) | (it > jb + w) | (jb == -1)
            sim = jnp.einsum('bhwie,bhwje->bhwij', bq, bk2) * QK_SCALE
            sim = jnp.where(mask, -jnp.finfo(sim.dtype).max, sim)
            attn = jax.nn.softmax(sim, -1)
            out = jnp.einsum('bhwij,bhwje->bhwie', attn, bv2)
            return out.reshape(b, h, n, d)

        def attn_layer(x, Wqkv, qs, ksc, Wo):
            b, n, _ = x.shape
            qkv = x @ Wqkv
            q, k, v = jnp.split(qkv, 3, -1)
            sh = lambda t: t.reshape(b, n, HEADS, DIM_HEAD).transpose(0, 2, 1, 3)
            q, k, v = (sh(q), sh(k), sh(v))
            q = l2norm(q) * qs
            k = l2norm(k) * ksc
            freqs, scale = rotary_tables(n)
            cos, sin = (jnp.cos(freqs), jnp.sin(freqs))
            q = q * cos * scale + rotate_half(q) * sin * scale
            inv = 1.0 / scale
            k = k * cos * inv + rotate_half(k) * sin * inv
            out = local_attention(q, k, v)
            out = out.transpose(0, 2, 1, 3).reshape(b, n, INNER)
            return out @ Wo

        def ffn_layer(x, g, bln, W1, b1, W2, b2):
            mu = x.mean(-1, keepdims=True)
            var = ((x - mu) ** 2).mean(-1, keepdims=True)
            xn = (x - mu) / jnp.sqrt(var + 1e-05) * g + bln
            hg = xn @ W1 + b1
            a, gate = jnp.split(hg, 2, -1)
            return a * jax.nn.gelu(gate, approximate=False) @ W2 + b2
        key = jax.random.key(seed)
        ks = jax.random.split(key, 8)
        B, N = (2, 256)
        init = lambda k, shape: jax.random.normal(k, shape, jnp.float32) * 0.02
        return {'x': jax.random.normal(ks[0], (B, N, DIM), jnp.float32), 'Wqkv': init(ks[1], (DEPTH, DIM, 3 * INNER)), 'q_scale': jnp.ones((DEPTH, DIM_HEAD), jnp.float32), 'k_scale': jnp.ones((DEPTH, DIM_HEAD), jnp.float32), 'Wo': init(ks[2], (DEPTH, INNER, DIM)), 'ln_g': jnp.ones((DEPTH, DIM), jnp.float32), 'ln_b': jnp.zeros((DEPTH, DIM), jnp.float32), 'W1': init(ks[3], (DEPTH, DIM, 2 * DIM_INNER)), 'b1': jnp.zeros((DEPTH, 2 * DIM_INNER), jnp.float32), 'W2': init(ks[4], (DEPTH, DIM_INNER, DIM)), 'b2': jnp.zeros((DEPTH, DIM), jnp.float32)}
    _L0_ffn_in = _L0_ffn_setup()
    _d = {'L0_attn_x': _L0_attn_in['x'], 'L0_attn_Wq': _L0_attn_in['Wq'], 'L0_attn_bq': _L0_attn_in['bq'], 'L0_attn_Wk': _L0_attn_in['Wk'], 'L0_attn_bk': _L0_attn_in['bk'], 'L0_attn_Wv': _L0_attn_in['Wv'], 'L0_attn_bv': _L0_attn_in['bv'], 'L0_attn_Wo': _L0_attn_in['Wo'], 'L0_attn_bo': _L0_attn_in['bo'], 'L0_ffn_Wqkv': _L0_ffn_in['Wqkv'], 'L0_ffn_q_scale': _L0_ffn_in['q_scale'], 'L0_ffn_k_scale': _L0_ffn_in['k_scale'], 'L0_ffn_Wo': _L0_ffn_in['Wo'], 'L0_ffn_ln_g': _L0_ffn_in['ln_g'], 'L0_ffn_ln_b': _L0_ffn_in['ln_b'], 'L0_ffn_W1': _L0_ffn_in['W1'], 'L0_ffn_b1': _L0_ffn_in['b1'], 'L0_ffn_W2': _L0_ffn_in['W2'], 'L0_ffn_b2': _L0_ffn_in['b2']}
    _x0 = _d['L0_attn_x']
    _d['L0_attn_x'] = jax.random.normal(jax.random.fold_in(jax.random.key(seed), 1), (8, 512, 128), dtype=_x0.dtype)
    del _x0
    return _d

def reference(L0_attn_x, L0_attn_Wq, L0_attn_bq, L0_attn_Wk, L0_attn_bk, L0_attn_Wv, L0_attn_bv, L0_attn_Wo, L0_attn_bo, L0_ffn_Wqkv, L0_ffn_q_scale, L0_ffn_k_scale, L0_ffn_Wo, L0_ffn_ln_g, L0_ffn_ln_b, L0_ffn_W1, L0_ffn_b1, L0_ffn_W2, L0_ffn_b2):

    def _L0_attn_ref(x, Wq, bq, Wk, bk, Wv, bv, Wo, bo):
        import jax, jax.numpy as jnp
        import numpy as np
        B, S, E, H = (4, 256, 128, 16)
        HD = E // H
        b, s, e = x.shape
        q = x @ Wq + bq
        k = x @ Wk + bk
        v = x @ Wv + bv

        def split(t):
            return t.reshape(b, s, H, HD).transpose(0, 2, 1, 3)
        q, k, v = (split(q), split(k), split(v))
        scale = 1.0 / np.sqrt(HD)
        attn = jnp.einsum('bhqd,bhkd->bhqk', q, k) * scale
        causal = jnp.tril(jnp.ones((s, s), dtype=bool))
        attn = jnp.where(causal[None, None], attn, -jnp.inf)
        attn = jax.nn.softmax(attn, axis=-1)
        y = jnp.einsum('bhqk,bhkd->bhqd', attn, v)
        y = y.transpose(0, 2, 1, 3).reshape(b, s, e)
        return y @ Wo + bo

    def _L0_ffn_ref(x, Wqkv, q_scale, k_scale, Wo, ln_g, ln_b, W1, b1, W2, b2):
        import jax, jax.numpy as jnp
        import numpy as np
        DIM = 128
        DEPTH = 6
        HEADS = 16
        DIM_HEAD = 64
        WINDOW = 32
        INNER = HEADS * DIM_HEAD
        DIM_INNER = int(DIM * 4 * 2 / 3)
        QK_SCALE = 8.0

        def shift_tokens(t):
            a, s = jnp.split(t, 2, -1)
            s = jnp.pad(s, ((0, 0), (1, 0), (0, 0)))[:, :-1]
            return jnp.concatenate([a, s], -1)

        def l2norm(t):
            return t / jnp.maximum(jnp.linalg.norm(t, axis=-1, keepdims=True), 1e-12)

        def rotate_half(x):
            x1, x2 = jnp.split(x, 2, -1)
            return jnp.concatenate([-x2, x1], -1)

        def rotary_tables(n):
            half = jnp.arange(0, DIM_HEAD, 2, dtype=jnp.float32)
            inv_freq = 1.0 / 10000.0 ** (half / DIM_HEAD)
            t = jnp.arange(n, dtype=jnp.float32)
            freqs = t[:, None] * inv_freq[None, :]
            freqs = jnp.concatenate([freqs, freqs], -1)
            base_scale = (half + 0.4 * DIM_HEAD) / (1.4 * DIM_HEAD)
            power = (t - n // 2) / (WINDOW // 2)
            scale = base_scale[None, :] ** power[:, None]
            scale = jnp.concatenate([scale, scale], -1)
            return (freqs, scale)

        def local_attention(q, k, v):
            b, h, n, d = q.shape
            w = WINDOW
            nw = n // w
            bq = q.reshape(b, h, nw, w, d)
            bk = k.reshape(b, h, nw, w, d)
            bv = v.reshape(b, h, nw, w, d)

            def look(t):
                p = jnp.pad(t, ((0, 0), (0, 0), (1, 0), (0, 0), (0, 0)))
                return jnp.concatenate([p[:, :, :nw], p[:, :, 1:]], axis=3)
            bk2, bv2 = (look(bk), look(bv))
            seq = jnp.arange(n).reshape(nw, w)
            seq_p = jnp.pad(seq, ((1, 0), (0, 0)), constant_values=-1)
            jt = jnp.concatenate([seq_p[:nw], seq_p[1:]], axis=1)
            it = seq[:, :, None]
            jb = jt[:, None, :]
            mask = (it < jb) | (it > jb + w) | (jb == -1)
            sim = jnp.einsum('bhwie,bhwje->bhwij', bq, bk2) * QK_SCALE
            sim = jnp.where(mask, -jnp.finfo(sim.dtype).max, sim)
            attn = jax.nn.softmax(sim, -1)
            out = jnp.einsum('bhwij,bhwje->bhwie', attn, bv2)
            return out.reshape(b, h, n, d)

        def attn_layer(x, Wqkv, qs, ksc, Wo):
            b, n, _ = x.shape
            qkv = x @ Wqkv
            q, k, v = jnp.split(qkv, 3, -1)
            sh = lambda t: t.reshape(b, n, HEADS, DIM_HEAD).transpose(0, 2, 1, 3)
            q, k, v = (sh(q), sh(k), sh(v))
            q = l2norm(q) * qs
            k = l2norm(k) * ksc
            freqs, scale = rotary_tables(n)
            cos, sin = (jnp.cos(freqs), jnp.sin(freqs))
            q = q * cos * scale + rotate_half(q) * sin * scale
            inv = 1.0 / scale
            k = k * cos * inv + rotate_half(k) * sin * inv
            out = local_attention(q, k, v)
            out = out.transpose(0, 2, 1, 3).reshape(b, n, INNER)
            return out @ Wo

        def ffn_layer(x, g, bln, W1, b1, W2, b2):
            mu = x.mean(-1, keepdims=True)
            var = ((x - mu) ** 2).mean(-1, keepdims=True)
            xn = (x - mu) / jnp.sqrt(var + 1e-05) * g + bln
            hg = xn @ W1 + b1
            a, gate = jnp.split(hg, 2, -1)
            return a * jax.nn.gelu(gate, approximate=False) @ W2 + b2
        for i in range(DEPTH):
            x = attn_layer(shift_tokens(x), Wqkv[i], q_scale[i], k_scale[i], Wo[i]) + x
            x = ffn_layer(shift_tokens(x), ln_g[i], ln_b[i], W1[i], b1[i], W2[i], b2[i]) + x
        return x
    x = L0_attn_x
    x = x + _L0_attn_ref(_layernorm(x, axis=-1), L0_attn_Wq, L0_attn_bq, L0_attn_Wk, L0_attn_bk, L0_attn_Wv, L0_attn_bv, L0_attn_Wo, L0_attn_bo)
    x = x + _L0_ffn_ref(_layernorm(x, axis=-1), L0_ffn_Wqkv, L0_ffn_q_scale, L0_ffn_k_scale, L0_ffn_Wo, L0_ffn_ln_g, L0_ffn_ln_b, L0_ffn_W1, L0_ffn_b1, L0_ffn_W2, L0_ffn_b2)
    return x

_drawn_inputs = setup_inputs


def setup_inputs(seed=0):
    import zlib

    import numpy as np

    out = dict(_drawn_inputs(seed))
    spreads = {'L0_ffn_q_scale': (1.0, 0.6),
     'L0_ffn_k_scale': (1.0, 0.6),
     'L0_ffn_ln_g': (1.0, 0.6),
     'L0_ffn_ln_b': (0.0, 0.8),
     'L0_ffn_b1': (0.0, 0.8),
     'L0_ffn_b2': (0.0, 0.1)}
    factors = {'L0_attn_bq': 29.791,
     'L0_attn_bk': 64.0,
     'L0_attn_bv': 4.838,
     'L0_attn_bo': 5.476,
     'L0_ffn_W1': 3.666,
     'L0_ffn_W2': 3.6}
    for name, (base, spread) in spreads.items():
        noise = np.random.default_rng([zlib.crc32(name.encode()), seed]).standard_normal(out[name].shape)
        drawn = base * np.exp(spread * noise) if base else spread * noise
        out[name] = jnp.asarray(drawn.astype(out[name].dtype))
    for name, factor in factors.items():
        out[name] = (out[name] * factor).astype(out[name].dtype)
    return out
```

```python
from contextlib import ExitStack

import numpy as np

import concourse.bass as bass
from concourse import mybir

F32 = mybir.dt.float32
BF16 = mybir.dt.bfloat16
ACT = mybir.ActivationFunctionType
ALU = mybir.AluOpType
AX = mybir.AxisListType.X

P = 128
NSEQ, SEQ, DIM = 8, 512, 128
TOK = NSEQ * SEQ
HEADS = 16
EPS = 1e-5

HD1, PADH = 8, 32
GROUPS = HEADS * PADH // P
HPG = P // PADH
QB = SEQ // P
UNITS = GROUPS * QB * HPG
UNIT_LIST = [(g, b, i) for g in range(GROUPS) for b in range(QB) for i in range(HPG)]

DEPTH, HD, WIN = 6, 64, 32
INNER = HEADS * HD
PAIRS = HEADS // 2
BLK = 64
NBLK = SEQ // BLK
KEYS = BLK + WIN
HALF = NBLK // 2
QK_SCALE = 8.0
DIM_INNER = int(DIM * 4 * 2 / 3)
CHUNKS = [(c, min(P, DIM_INNER - c)) for c in range(0, DIM_INNER, P)]
NC = len(CHUNKS)

MASKED = 1e30


def wait(eng, sem, value):
    if not (isinstance(value, int) and value <= 0):
        eng.wait_ge(sem, value)


def build_stage1(nc, d, res_sb, u_sb):
    with ExitStack() as st:
        def sb(name, shape, dt=F32):
            return st.enter_context(nc.sbuf_tensor(name, shape, dt))

        def sem(name):
            return st.enter_context(nc.semaphore(name))

        bank = [st.enter_context(nc.psum_tensor(f"s1_bank{i}", [P, 512], F32)) for i in range(8)]
        stat_bank, proj_bank = bank[0], bank[1]
        score_bank = [bank[2], bank[3], bank[4]]
        tr_bank = [bank[5], bank[0]]
        y_bank = [bank[6], bank[7]]

        x_sb = sb("s1_x", [P, TOK])
        wq = sb("s1_wq", [P, GROUPS * P])
        wk = sb("s1_wk", [P, GROUPS * P])
        wv = sb("s1_wv", [P, GROUPS * P])
        wo = sb("s1_wo", [P, GROUPS, DIM])
        bq = sb("s1_bq", [P, GROUPS])
        bk = sb("s1_bk", [P, GROUPS])
        bv = sb("s1_bv", [P, GROUPS * P])
        bo = sb("s1_bo", [P, 1])
        mean_w = sb("s1_mean_w", [P, P])
        eps = sb("s1_eps", [P, 1])
        ident = sb("s1_ident", [P, P])
        ident_b = sb("s1_ident_b", [P, P], BF16)
        causal = sb("s1_causal", [P, P])
        causal_b = sb("s1_causal_b", [P, P], BF16)
        xc = sb("s1_xc", [P, SEQ])
        sq = sb("s1_sq", [P, SEQ])
        std = sb("s1_std", [P, SEQ])
        rstd = sb("s1_rstd", [P, SEQ])
        xn = sb("s1_xn", [P, SEQ])
        q_t = sb("s1_q", [P, GROUPS, SEQ])
        k_t = sb("s1_k", [P, GROUPS, SEQ])
        v = sb("s1_v", [P, QB, GROUPS * P])
        neg_max = sb("s1_neg_max", [P, UNITS])
        den = sb("s1_den", [P, UNITS])
        rden = sb("s1_rden", [P, UNITS])
        NP = 4
        probs = sb("s1_probs", [P, NP, SEQ])
        probs_t = sb("s1_probs_t", [P, 2, QB, P])
        y_t = sb("s1_y", [P, GROUPS, SEQ])

        loaded = sem("s1_loaded")
        const_ready, mask_ready = sem("s1_const_ready"), sem("s1_mask_ready")
        ln_mean, ln_xc, ln_sq = sem("s1_ln_mean"), sem("s1_ln_xc"), sem("s1_ln_sq")
        ln_var, ln_std, ln_rstd, ln_out = sem("s1_ln_var"), sem("s1_ln_std"), sem("s1_ln_rstd"), sem("s1_ln_out")
        proj_done = sem("s1_proj_done")
        qv_ready, k_ready = sem("s1_qv_ready"), sem("s1_k_ready")
        score_done, max_done, exp_done = sem("s1_score_done"), sem("s1_max_done"), sem("s1_exp_done")
        rden_done, probs_done = sem("s1_rden_done"), sem("s1_probs_done")
        tr_done, pt_even, pt_odd = sem("s1_tr_done"), sem("s1_pt_even"), sem("s1_pt_odd")
        pv_done, y_ready = sem("s1_pv_done"), sem("s1_y_ready")
        wo_done, res_done = sem("s1_wo_done"), sem("s1_res_done")

        loads = [(x_sb[:, :], d["x"]), (wq[:, :], d["a_wq"]), (wk[:, :], d["a_wk"]), (wv[:, :], d["a_wv"]),
                 (wo[:, :, :], d["a_wo"]), (bq[:, :], d["a_bq"]), (bk[:, :], d["a_bk"]),
                 (bv[:, :], d["a_bv"].partition_broadcast(P)), (bo[:, :], d["a_bo"]),
                 (ident[:, :], d["c_ident"]), (causal[:, :], d["c_causal"])]
        n_loaded = 16 * len(loads)
        block = st.enter_context(nc.Block())

        def seq_of(t, s):
            return t[:, bass.ds(s * SEQ, SEQ)]

        def pt_sem(u):
            return pt_even if u % 2 == 0 else pt_odd

        def pt_count(s, u):
            return s * (UNITS // 2) + u // 2 + 1

        @block.sync
        def _(sp):
            for dst, src in loads:
                sp.dma_start(dst, src).then_inc(loaded, 16)

        @block.gpsimd
        def _(pool):
            pool.memset(mean_w[:, :], 1.0 / DIM).then_inc(const_ready, 1)
            pool.memset(eps[:, :], EPS).then_inc(const_ready, 1)
            with pool.Fori(0, NSEQ) as s:
                for u, (g, b, i) in enumerate(UNIT_LIST):
                    n = P * (b + 1)
                    pool.wait_ge(rden_done, s * UNITS + (u + 1))
                    row = probs[:, u % NP, 0:n]
                    nc.gpsimd.tensor_tensor(row, row, rden[:, u:u + 1].to_broadcast([P, n]), ALU.mult)\
                      .then_inc(probs_done, 1)

        @block.scalar
        def _(act):
            act.wait_ge(const_ready, 2)

            def norm(k):
                act.wait_ge(ln_xc, k + 1)
                nc.scalar.activation(sq[:, :], xc[:, :], ACT.Square).then_inc(ln_sq, 1)
                act.wait_ge(ln_var, k + 1)
                nc.scalar.activation(std[:, :], stat_bank[:, :], ACT.Sqrt, bias=eps[:, 0:1]).then_inc(ln_std, 1)

            with act.Fori(0, NSEQ) as s:
                norm(2 * s)
                for g in range(GROUPS):
                    act.wait_ge(proj_done, s * (2 * GROUPS + QB) + (2 * g + 2))
                    nc.scalar.activation(k_t[:, g, :], proj_bank[:, :], ACT.Identity, bias=bk[:, g:g + 1])\
                      .then_inc(k_ready, 1)
                for t in range(UNITS + 4):
                    if t < UNITS:
                        n = P * (UNIT_LIST[t][1] + 1)
                        act.wait_ge(max_done, s * UNITS + (t + 1))
                        if t >= NP:
                            act.wait_ge(tr_done, s * UNITS + (t - NP + 1))
                        nc.scalar.activation(probs[:, t % NP, 0:n], score_bank[t % 3][:, 0:n], ACT.Exp, scale=-1.0,
                                             bias=neg_max[:, t:t + 1], accum_out=den[:, t:t + 1])\
                          .then_inc(exp_done, 1)
                    u = t - 3
                    if 0 <= u < UNITS and u % 2:
                        nb = UNIT_LIST[u][1] + 1
                        act.wait_ge(tr_done, s * UNITS + (u + 1))
                        if u >= 2:
                            act.wait_ge(pv_done, s * UNITS + (u - 1))
                        nc.scalar.activation(probs_t[:, u % 2, 0:nb, :], tr_bank[u % 2][:, 0:nb * P], ACT.Copy)\
                          .then_inc(pt_odd, 1)
                    u = t - 4
                    if u >= 0 and (u + 1) % (QB * HPG) == 0:
                        g = u // (QB * HPG)
                        act.wait_ge(pv_done, s * UNITS + (u + 1))
                        nc.scalar.activation(y_t[:, g, :], y_bank[g % 2][:, :], ACT.Copy).then_inc(y_ready, 1)
                norm(2 * s + 1)

        @block.vector
        def _(dve):
            dve.wait_ge(loaded, n_loaded)
            nc.vector.tensor_copy(ident_b[:, :], ident[:, :]).then_inc(mask_ready, 1)
            nc.vector.tensor_copy(causal_b[:, :], causal[:, :]).then_inc(mask_ready, 1)

            def norm(k, src, dst):
                dve.wait_ge(ln_mean, k + 1)
                nc.vector.tensor_tensor(xc[:, :], src, stat_bank[:, :], ALU.subtract).then_inc(ln_xc, 1)
                dve.wait_ge(ln_std, k + 1)
                nc.vector.reciprocal(rstd[:, :], std[:, :]).then_inc(ln_rstd, 1)
                dve.wait_ge(ln_rstd, k + 1)
                nc.vector.tensor_tensor(dst, xc[:, :], rstd[:, :], ALU.mult).then_inc(ln_out, 1)

            with dve.Fori(0, NSEQ) as s:
                norm(2 * s, seq_of(x_sb, s), xn[:, :])
                for g in range(GROUPS):
                    dve.wait_ge(proj_done, s * (2 * GROUPS + QB) + (2 * g + 1))
                    nc.vector.tensor_scalar(q_t[:, g, :], stat_bank[:, :], bq[:, g:g + 1], -float(HD1) ** -0.5,
                                            ALU.add, ALU.mult).then_inc(qv_ready, 1)
                for b in range(QB):
                    dve.wait_ge(proj_done, s * (2 * GROUPS + QB) + (2 * GROUPS + b + 1))
                    nc.vector.tensor_tensor(v[:, b, :], (stat_bank, proj_bank)[b % 2][:, :], bv[:, :], ALU.add)\
                      .then_inc(qv_ready, 1)
                for t in range(UNITS + 4):
                    if t < UNITS:
                        n = P * (UNIT_LIST[t][1] + 1)
                        dve.wait_ge(score_done, s * UNITS + (t + 1))
                        nc.vector.tensor_reduce(neg_max[:, t:t + 1], score_bank[t % 3][:, 0:n], AX, ALU.min)\
                          .then_inc(max_done, 1)
                    u = t - 1
                    if 0 <= u < UNITS:
                        dve.wait_ge(exp_done, s * UNITS + (u + 1))
                        nc.vector.reciprocal(rden[:, u:u + 1], den[:, u:u + 1]).then_inc(rden_done, 1)
                    u = t - 3
                    if 0 <= u < UNITS and u % 2 == 0:
                        nb = UNIT_LIST[u][1] + 1
                        dve.wait_ge(tr_done, s * UNITS + (u + 1))
                        if u >= 2:
                            dve.wait_ge(pv_done, s * UNITS + (u - 1))
                        nc.vector.tensor_copy(probs_t[:, u % 2, 0:nb, :], tr_bank[u % 2][:, 0:nb * P])\
                          .then_inc(pt_even, 1)
                dve.wait_ge(wo_done, s + 1)
                nc.vector.scalar_tensor_tensor(seq_of(res_sb, s), proj_bank[:, :], bo[:, 0:1], seq_of(x_sb, s),
                                               ALU.add, ALU.add).then_inc(res_done, 1)
                dve.wait_ge(res_done, s + 1)
                norm(2 * s + 1, seq_of(res_sb, s), seq_of(u_sb, s))

        @block.tensor
        def _(pe):
            pe.wait_ge(loaded, n_loaded)
            pe.wait_ge(const_ready, 2)
            pe.wait_ge(mask_ready, 2)

            def norm(k, src):
                nc.tensor.matmul(stat_bank[:, :], mean_w[:, :], src, start=True, stop=True).then_inc(ln_mean, 1)
                pe.wait_ge(ln_sq, k + 1)
                nc.tensor.matmul(stat_bank[:, :], mean_w[:, :], sq[:, :], start=True, stop=True).then_inc(ln_var, 1)

            with pe.Fori(0, NSEQ) as s:
                norm(2 * s, seq_of(x_sb, s))
                pe.wait_ge(ln_out, 2 * s + 1)
                for g in range(GROUPS):
                    if g:
                        pe.wait_ge(qv_ready, s * (GROUPS + QB) + g)
                    nc.tensor.matmul(stat_bank[:, :], wq[:, g * P:(g + 1) * P], xn[:, :], start=True, stop=True)\
                      .then_inc(proj_done, 1)
                    if g:
                        pe.wait_ge(k_ready, s * GROUPS + g)
                    nc.tensor.matmul(proj_bank[:, :], wk[:, g * P:(g + 1) * P], xn[:, :], start=True, stop=True)\
                      .then_inc(proj_done, 1)
                for b in range(QB):
                    if b != 1:
                        pe.wait_ge(qv_ready, s * (GROUPS + QB) + (GROUPS + max(0, b - 1)))
                    else:
                        pe.wait_ge(k_ready, s * GROUPS + GROUPS)
                    nc.tensor.matmul((stat_bank, proj_bank)[b % 2][:, :], xn[:, b * P:(b + 1) * P], wv[:, :],
                                     start=True, stop=True).then_inc(proj_done, 1)
                pe.wait_ge(qv_ready, s * (GROUPS + QB) + (GROUPS + QB))
                for t in range(UNITS + 4):
                    if t < UNITS:
                        g, b, i = UNIT_LIST[t]
                        n = P * (b + 1)
                        rows = slice(PADH * i, PADH * i + HD1)
                        if t >= 3:
                            pe.wait_ge(exp_done, s * UNITS + (t - 2))
                        nc.tensor.matmul(score_bank[t % 3][:, 0:n], q_t[rows, g, b * P:(b + 1) * P], k_t[rows, g, 0:n],
                                         start=True, stop=False, tile_position=(PADH * i, 0), skip_group_check=True)
                        nc.tensor.matmul(score_bank[t % 3][:, n - P:n], ident_b[:, :], causal_b[:, :],
                                         start=False, stop=True, skip_group_check=True).then_inc(score_done, 1)
                    u = t - 3
                    if 0 <= u < UNITS:
                        nb = UNIT_LIST[u][1] + 1
                        pe.wait_ge(probs_done, s * UNITS + (u + 1))
                        if u >= 2:
                            pe.wait_ge(pt_sem(u), pt_count(s, u - 2))
                        for kb in range(nb):
                            last = nc.tensor.transpose(tr_bank[u % 2][:, kb * P:(kb + 1) * P],
                                                       probs[:, u % NP, kb * P:(kb + 1) * P], ident[:, :])
                        last.then_inc(tr_done, 1)
                    u = t - 4
                    if 0 <= u < UNITS:
                        g, b, i = UNIT_LIST[u]
                        pe.wait_ge(pt_sem(u), pt_count(s, u))
                        if b == 0 and i == 0 and g >= 2:
                            pe.wait_ge(y_ready, s * GROUPS + (g - 1))
                        for kb in range(b + 1):
                            last = nc.tensor.matmul(
                                y_bank[g % 2][PADH * i:PADH * (i + 1), b * P:(b + 1) * P],
                                v[:, kb, g * P + PADH * i:g * P + PADH * (i + 1)], probs_t[:, u % 2, kb, :],
                                start=(kb == 0), stop=(kb == b), tile_position=(0, PADH * i))
                        last.then_inc(pv_done, 1)
                pe.wait_ge(y_ready, s * GROUPS + GROUPS)
                for g in range(GROUPS):
                    last = nc.tensor.matmul(proj_bank[:, :], wo[:, g, :], y_t[:, g, :],
                                            start=(g == 0), stop=(g == GROUPS - 1))
                last.then_inc(wo_done, 1)
                pe.wait_ge(res_done, s + 1)
                norm(2 * s + 1, seq_of(res_sb, s))
                pe.wait_ge(ln_out, 2 * s + 2)


V_UNITS = [(half, j) for half in range(2) for j in range(NBLK)]
V_SLOTS = {0: {"a": 0, "b": 1, "c": 2}, 1: {"a": 3, "b": 4, "c": 5}, 2: {"b": 6, "c": 7}, 3: {"b": 8, "c": 9},
           4: {"b": 10, "c": 11}, 5: {"b": 12, "c": 13}, 6: {"b": 14, "c": 15}, 7: {}}
LAG_NORM, LAG_SCORE, LAG_VALUE = 1, 2, 3
WO_STEP = LAG_VALUE
LN_SCALE = 2.0 ** 16
NORM_FLOOR = 1e-24


def build_stage2(nc, d, res_sb, u_sb, out, depth):
    with ExitStack() as st:
        def sb(name, shape, dt=F32):
            return st.enter_context(nc.sbuf_tensor(name, shape, dt))

        def sem(name):
            return st.enter_context(nc.semaphore(name))

        bank = [st.enter_context(nc.psum_tensor(f"s2_bank{i}", [P, 512], F32)) for i in range(4, 8)]
        proj_ps = st.enter_context(nc.psum_tensor("s2_proj", [P, 4, SEQ], F32))
        ss_bank, score_bank, misc_bank = bank[0], [bank[1], bank[2]], bank[3]
        up_bank = [(proj_ps[:, 0, :], proj_ps[:, 1, :]), (proj_ps[:, 2, :], proj_ps[:, 3, :]),
                   (bank[1][:, :], bank[2][:, :])]

        wqk = sb("s2_wqk", [P, PAIRS, 4, P])
        wv = sb("s2_wv", [P, INNER])
        wo = sb("s2_wo", [P, PAIRS, DIM])
        qk_scale = sb("s2_qk_scale", [P, 4])
        w1 = sb("s2_w1", [P, 2 * DIM_INNER])
        w2 = sb("s2_w2", [P, NC, DIM])
        vec = sb("s2_vec", [P, 2 + 2 * NC + 1])
        ln_g, ln_b, b2 = vec[:, 0:1], vec[:, 1:2], vec[:, 2 + 2 * NC:3 + 2 * NC]
        rot_cos = sb("s2_cos", [P, 2, SEQ])
        rot_sin = sb("s2_sin", [P, 2, SEQ])
        ident = sb("s2_ident", [P, P])
        ident_b = sb("s2_ident_b", [P, P], BF16)
        band_b = sb("s2_band_b", [P, NBLK * KEYS], BF16)
        same_head = sb("s2_same_head", [P, P])
        mean_w = sb("s2_mean_w", [P, P])
        eps = sb("s2_eps", [P, 1])
        ln_shift = sb("s2_ln_shift", [P, 1])
        xs = sb("s2_xs", [P, WIN + SEQ])
        v = sb("s2_v", [P, 2, NBLK, INNER // 2])
        sq = sb("s2_sq", [P, 2, 2, SEQ])
        by_cos = sb("s2_by_cos", [P, 2, SEQ])
        by_sin = sb("s2_by_sin", [P, 2, SEQ])
        rotated = sb("s2_rotated", [P, 2, 2, SEQ])
        inv_norm = sb("s2_inv_norm", [P, 2, SEQ])
        q_diag = sb("s2_q_diag", [P, 2, NBLK, 2, BLK])
        k_t = sb("s2_k", [P, 2, WIN + SEQ])
        neg_max = sb("s2_neg_max", [P, 2, NBLK])
        den = sb("s2_den", [P, 2, NBLK])
        rden = sb("s2_rden", [P, 2, NBLK])
        probs = sb("s2_probs", [P, 2, NBLK, KEYS])
        probs_t = sb("s2_probs_t", [P, 2, HALF, 2, BLK])
        y_t = sb("s2_y", [P, PAIRS, SEQ])
        xf = sb("s2_xf", [P, SEQ])
        xc = sb("s2_xc", [P, SEQ])
        fsq = sb("s2_fsq", [P, SEQ])
        rstd = sb("s2_rstd", [P, SEQ])
        xa = sb("s2_xa", [P, 2, SEQ])
        gate = sb("s2_gate", [P, NC, SEQ])
        hid = sb("s2_hid", [P, NC, SEQ])

        names = ("const_in consts cast zeroed attn_w ffn_w tables xs_in proj_qk proj_rot sq_done rot_done cos_done "
                 "add_done ss_done guard_done log_done inv_done norm_done score_done max_done exp_done rden_done "
                 "probs_done tr_done pt0 pt1 v_mm v_done pv_done y_done wo_done attn_res "
                 "xf_in f_mean f_xc f_sq f_var f_std f_rstd f_xn f_xa f_up f_gate f_hid f_down ffn_res "
                 "sum_done stored").split()
        S = {n: sem("s2_" + n) for n in names}
        N_ATTN_DMA, N_FFN_DMA = 6, 3

        block = st.enter_context(nc.Block())

        def seq_of(t, s):
            return t[:, bass.ds(s * SEQ, SEQ)]

        def steps(eng, l, body):
            for p in range(PAIRS):
                body(l, 0, p, True)
            with eng.Fori(1, NSEQ) as s:
                for p in range(PAIRS):
                    body(l, s, p, False)
            for p in range(WO_STEP + 1):
                body(l, NSEQ, p, False)

        def live(s, p, lag, first):
            if first:
                return p >= lag
            return p < lag if isinstance(s, int) else True

        def pair_no(l, s, p):
            return l * (NSEQ * PAIRS) + s * PAIRS + p

        @block.sync
        def _(sp):
            sp.dma_start(ident[:, :], d["c_ident"]).then_inc(S["const_in"], 16)
            sp.dma_start(by_cos[:, :, :].rearrange("p a t -> p (a t)")[:, 0:NBLK * KEYS], d["c_band"])\
              .then_inc(S["const_in"], 16)
            sp.dma_start(same_head[:, :], d["c_same_head"]).then_inc(S["const_in"], 16)
            sp.wait_ge(S["zeroed"], 3)
            def layer(l, first):
                def of_layer(name):
                    a = d[name]
                    return (a[0:1] if first else a[bass.ds(l, 1)]).rearrange("o p n -> (o p) n")

                if not first:
                    sp.wait_ge(S["attn_res"], l * NSEQ)
                for dst, src in ((wqk[:, :, :, :].rearrange("p a b n -> p (a b n)"), of_layer("f_wqk")),
                                 (wv[:, :], of_layer("f_wv")),
                                 (wo[:, :, :].rearrange("p a n -> p (a n)"), of_layer("f_wo")),
                                 (qk_scale[:, :], of_layer("f_qk_scale")),
                                 (rot_cos[:, :, :], d["c_cos"]), (rot_sin[:, :, :], d["c_sin"])):
                    sp.dma_start(dst, src).then_inc(S["attn_w"], 16)
                if not first:
                    sp.wait_ge(S["ffn_res"], l * NSEQ)

                def shifted(s):
                    at = s * SEQ if isinstance(s, int) else sp.snap(s * SEQ)
                    if not isinstance(s, int):
                        sp.wait_ge(S["cos_done"], pair_no(l, s, 0))
                    sp.dma_start(xs[0:64, WIN:WIN + SEQ], u_sb[0:64, bass.ds(at, SEQ)]).then_inc(S["xs_in"], 16)
                    sp.dma_start(xs[64:128, WIN + 1:WIN + SEQ], u_sb[64:128, bass.ds(at, SEQ - 1)])\
                      .then_inc(S["xs_in"], 16)

                shifted(0)
                for dst, src in ((w1[:, :], of_layer("f_w1")),
                                 (w2[:, :, :].rearrange("p a n -> p (a n)"), of_layer("f_w2")),
                                 (vec[:, :], of_layer("f_vec"))):
                    sp.dma_start(dst, src).then_inc(S["ffn_w"], 16)
                with sp.Fori(1, NSEQ) as s:
                    shifted(s)

                def shifted_ffn(s):
                    at = s * SEQ if isinstance(s, int) else sp.snap(s * SEQ)
                    sp.wait_ge(S["attn_res"], l * NSEQ + s + 1)
                    if not isinstance(s, int):
                        sp.wait_ge(S["f_xc"], l * NSEQ + s)
                    sp.dma_start(xf[0:64, :], u_sb[0:64, bass.ds(at, SEQ)]).then_inc(S["xf_in"], 16)
                    sp.dma_start(xf[64:128, 1:SEQ], u_sb[64:128, bass.ds(at, SEQ - 1)]).then_inc(S["xf_in"], 16)

                shifted_ffn(0)
                with sp.Fori(1, NSEQ) as s:
                    shifted_ffn(s)

            layer(0, True)
            if depth > 1:
                with sp.Fori(1, depth) as l:
                    layer(l, False)
            sp.wait_ge(S["sum_done"], 1)
            sp.dma_start(out, res_sb[:, :]).then_inc(S["stored"], 16)
            sp.wait_ge(S["stored"], 16)

        @block.gpsimd
        def _(pool):
            pool.memset(xs[:, 0:WIN + 1], 0.0).then_inc(S["zeroed"], 1)
            pool.memset(xf[:, 0:1], 0.0).then_inc(S["zeroed"], 1)
            pool.memset(k_t[:, :, 0:WIN], 0.0).then_inc(S["zeroed"], 1)
            pool.memset(q_diag[:, :, :, :, :], 0.0).then_inc(S["consts"], 1)
            pool.memset(mean_w[:, :], 1.0 / DIM).then_inc(S["consts"], 1)
            pool.memset(eps[:, :], EPS).then_inc(S["consts"], 1)
            pool.memset(ln_shift[:, :], 0.5 * float(np.log(LN_SCALE))).then_inc(S["consts"], 1)

            def step(l, s, p, first):
                n = pair_no(l, s, p)
                if live(s, p, 0, first):
                    pool.wait_ge(S["cos_done"], n + 1)
                    if not (first and p < 1):
                        pool.wait_ge(S["norm_done"], n - 1)
                    nc.gpsimd.tensor_tensor(rotated[:, p % 2, :, :], by_cos[:, :, :], by_sin[:, :, :], ALU.add)\
                      .then_inc(S["add_done"], 1)
                if live(s, p, LAG_SCORE, first):
                    m = n - LAG_SCORE
                    for h in range(2):
                        pool.wait_ge(S["rden_done"], 2 * m + (h + 1))
                        blk = slice(h * HALF, (h + 1) * HALF)
                        part = probs[:, p % 2, blk, :]
                        nc.gpsimd.tensor_tensor(part, part, rden[:, p % 2, blk].unsqueeze(2).to_broadcast([P, HALF, KEYS]),
                                                ALU.mult).then_inc(S["probs_done"], 1)

            with pool.Fori(0, depth) as l:
                steps(pool, l, step)

        @block.scalar
        def _(act):
            act.wait_ge(S["consts"], 4)

            def v_unit(l, s, p, slot):
                q = V_SLOTS[p].get(slot)
                if q is None:
                    return
                half, j = V_UNITS[q]
                act.wait_ge(S["v_mm"], (l * NSEQ + s) * len(V_UNITS) + (q + 1))
                nc.scalar.activation(v[0:KEYS, half, j, :], misc_bank[0:KEYS, :], ACT.Copy).then_inc(S["v_done"], 1)

            def step(l, s, p, first):
                n = pair_no(l, s, p)
                full = live(s, p, 0, first)
                if full:
                    v_unit(l, s, p, "a")
                    act.wait_ge(S["proj_qk"], n + 1)
                    if not (first and p < 1):
                        act.wait_ge(S["ss_done"], 2 * n - 2)
                    nc.scalar.activation(sq[:, p % 2, :, :], proj_ps[:, 0:2, :], ACT.Square).then_inc(S["sq_done"], 1)
                    v_unit(l, s, p, "b")
                if live(s, p, LAG_NORM, first):
                    m = n - LAG_NORM
                    act.wait_ge(S["guard_done"], 2 * m + 2)
                    nc.scalar.activation(inv_norm[:, :, :], inv_norm[:, :, :], ACT.Ln, scale=LN_SCALE)\
                      .then_inc(S["log_done"], 1)
                    act.wait_ge(S["log_done"], m + 1)
                    nc.scalar.activation(inv_norm[:, :, :], inv_norm[:, :, :], ACT.Exp, scale=-0.5,
                                         bias=ln_shift[:, 0:1]).then_inc(S["inv_done"], 1)
                if live(s, p, LAG_VALUE, first):
                    m = n - LAG_VALUE
                    act.wait_ge(S["tr_done"], 2 * m + 2)
                    if not (first and p == LAG_VALUE):
                        act.wait_ge(S["pv_done"], m)
                    nc.scalar.activation(probs_t[0:KEYS, 1, :, :, :], score_bank[1][0:KEYS, :], ACT.Copy)\
                      .then_inc(S["pt1"], 1)
                if full:
                    v_unit(l, s, p, "c")
                if live(s, p, LAG_SCORE, first):
                    m = n - LAG_SCORE
                    if not (first and p < LAG_SCORE + 1):
                        act.wait_ge(S["tr_done"], 2 * m - 2)
                    for h in range(2):
                        act.wait_ge(S["max_done"], 2 * m + (h + 1))
                        for b in range(h * HALF, (h + 1) * HALF):
                            at = (b - h * HALF) * KEYS
                            last = nc.scalar.activation(probs[:, p % 2, b, :], score_bank[h][:, at:at + KEYS], ACT.Exp,
                                                        scale=-1.0, bias=neg_max[:, p % 2, b:b + 1],
                                                        accum_out=den[:, p % 2, b:b + 1])
                        last.then_inc(S["exp_done"], 1)
                if live(s, p, LAG_VALUE, first):
                    m = n - LAG_VALUE
                    act.wait_ge(S["pv_done"], m + 1)
                    if (p - LAG_VALUE) % PAIRS == 0 and not first:
                        act.wait_ge(S["wo_done"], l * NSEQ + s)
                    nc.scalar.activation(y_t[:, (p - LAG_VALUE) % PAIRS, :], misc_bank[:, :], ACT.Copy)\
                      .then_inc(S["y_done"], 1)

            def ffn_norm(f, par):
                act.wait_ge(S["f_xc"], f + 1)
                nc.scalar.activation(fsq[:, :], xc[:, :], ACT.Square).then_inc(S["f_sq"], 1)
                act.wait_ge(S["f_var"], f + 1)
                nc.scalar.activation(rstd[:, :], ss_bank[:, :], ACT.Sqrt, bias=eps[:, 0:1]).then_inc(S["f_std"], 1)
                act.wait_ge(S["f_xn"], f + 1)
                nc.scalar.activation(xa[:, par, :], xc[:, :], ACT.Identity, scale=ln_g, bias=ln_b)\
                  .then_inc(S["f_xa"], 1)

            def ffn_gate(f):
                for c, (_, m) in enumerate(CHUNKS):
                    act.wait_ge(S["f_up"], f * NC + (c + 1))
                    nc.scalar.activation(gate[0:m, c, :], up_bank[c][1][0:m, :], ACT.Gelu,
                                         bias=vec[0:m, 2 + NC + c:3 + NC + c]).then_inc(S["f_gate"], 1)

            with act.Fori(0, depth) as l:
                steps(act, l, step)
                act.wait_ge(S["ffn_w"], l * (16 * N_FFN_DMA) + 16 * N_FFN_DMA)
                ffn_norm(l * NSEQ, 0)
                ffn_norm(l * NSEQ + 1, 1)
                ffn_gate(l * NSEQ)
                with act.Fori(1, NSEQ // 2) as s2:
                    for par in range(2):
                        f = l * NSEQ + s2 * 2 + par
                        ffn_norm(f, par)
                        ffn_gate(f - 1)
                ffn_gate(l * NSEQ + NSEQ - 1)

        @block.vector
        def _(dve):
            dve.wait_ge(S["const_in"], 48)
            nc.vector.tensor_copy(ident_b[:, :], ident[:, :]).then_inc(S["cast"], 1)
            nc.vector.tensor_copy(band_b[:, :], by_cos[:, :, :].rearrange("p a t -> p (a t)")[:, 0:NBLK * KEYS])\
              .then_inc(S["cast"], 1)
            dve.wait_ge(S["consts"], 4)
            dve.wait_ge(S["cast"], 2)

            def step(l, s, p, first):
                n = pair_no(l, s, p)
                if not first and p == WO_STEP:
                    r = l * NSEQ + s
                    dve.wait_ge(S["wo_done"], r)
                    nc.vector.tensor_tensor(seq_of(u_sb, s - 1), misc_bank[:, :], seq_of(u_sb, s - 1), ALU.add)\
                      .then_inc(S["attn_res"], 1)
                if live(s, p, 0, first):
                    dve.wait_ge(S["proj_rot"], n + 1)
                    if not (first and p == 0):
                        dve.wait_ge(S["add_done"], n)
                    nc.vector.tensor_tensor(by_sin[:, :, :], proj_ps[:, 2:4, :], rot_sin[:, :, :], ALU.mult)\
                      .then_inc(S["rot_done"], 1)
                    dve.wait_ge(S["sq_done"], n + 1)
                    nc.vector.tensor_tensor(by_cos[:, :, :], proj_ps[:, 0:2, :], rot_cos[:, :, :], ALU.mult)\
                      .then_inc(S["cos_done"], 1)
                if live(s, p, LAG_NORM, first):
                    m = n - LAG_NORM
                    if not (first and p == LAG_NORM):
                        dve.wait_ge(S["norm_done"], m)
                    for i in range(2):
                        dve.wait_ge(S["ss_done"], 2 * m + (i + 1))
                        nc.vector.tensor_scalar(inv_norm[:, i, :], ss_bank[:, :], NORM_FLOOR, None, ALU.max)\
                          .then_inc(S["guard_done"], 1)
                if live(s, p, LAG_VALUE, first):
                    m = n - LAG_VALUE
                    dve.wait_ge(S["tr_done"], 2 * m + 1)
                    if not (first and p == LAG_VALUE):
                        dve.wait_ge(S["pv_done"], m)
                    nc.vector.tensor_copy(probs_t[0:KEYS, 0, :, :, :], score_bank[0][0:KEYS, :]).then_inc(S["pt0"], 1)
                if live(s, p, LAG_NORM, first):
                    m = n - LAG_NORM
                    par = (p - LAG_NORM) % 2
                    dve.wait_ge(S["inv_done"], m + 1)
                    dve.wait_ge(S["add_done"], m + 1)
                    if not (first and p < LAG_NORM + 1):
                        dve.wait_ge(S["score_done"], 2 * m - 2)
                    nc.vector.tensor_tensor(k_t[:, par, WIN:WIN + SEQ], rotated[:, par, 1, :], inv_norm[:, 1, :], ALU.mult)
                    for h in range(2):
                        rows = slice(HD * h, HD * (h + 1))
                        last = nc.vector.tensor_tensor(
                            q_diag[rows, par, :, h, :],
                            rotated[rows, par, 0, :].rearrange("p (b q) -> p b q", q=BLK),
                            inv_norm[rows, 0, :].rearrange("p (b q) -> p b q", q=BLK), ALU.mult)
                    last.then_inc(S["norm_done"], 1)
                if live(s, p, LAG_SCORE, first):
                    m = n - LAG_SCORE
                    for h in range(2):
                        dve.wait_ge(S["score_done"], 2 * m + (h + 1))
                        nc.vector.tensor_reduce(neg_max[:, p % 2, h * HALF:(h + 1) * HALF],
                                                score_bank[h][:, 0:HALF * KEYS].rearrange("p (b k) -> p b k", k=KEYS),
                                                AX, ALU.min).then_inc(S["max_done"], 1)
                    for h in range(2):
                        dve.wait_ge(S["exp_done"], 2 * m + (h + 1))
                        blk = slice(h * HALF, (h + 1) * HALF)
                        nc.vector.reciprocal(rden[:, p % 2, blk], den[:, p % 2, blk]).then_inc(S["rden_done"], 1)

            def ffn_norm(f, first=False):
                dve.wait_ge(S["f_mean"], f + 1)
                if not first:
                    dve.wait_ge(S["f_xa"], f)
                nc.vector.tensor_tensor(xc[:, :], xf[:, :], ss_bank[:, :], ALU.subtract).then_inc(S["f_xc"], 1)
                dve.wait_ge(S["f_std"], f + 1)
                nc.vector.reciprocal(rstd[:, :], rstd[:, :]).then_inc(S["f_rstd"], 1)
                dve.wait_ge(S["f_rstd"], f + 1)
                nc.vector.tensor_tensor(xc[:, :], xc[:, :], rstd[:, :], ALU.mult).then_inc(S["f_xn"], 1)

            def ffn_hidden(l, s):
                f = l * NSEQ + s
                for c, (_, m) in enumerate(CHUNKS):
                    dve.wait_ge(S["f_gate"], f * NC + (c + 1))
                    nc.vector.scalar_tensor_tensor(hid[0:m, c, :], up_bank[c][0][0:m, :], vec[0:m, 2 + c:3 + c],
                                                   gate[0:m, c, :], ALU.add, ALU.mult).then_inc(S["f_hid"], 1)
                dve.wait_ge(S["f_down"], f + 1)
                nc.vector.scalar_tensor_tensor(seq_of(u_sb, s), misc_bank[:, :], b2, seq_of(u_sb, s),
                                               ALU.add, ALU.add).then_inc(S["ffn_res"], 1)

            with dve.Fori(0, depth) as l:
                dve.wait_ge(S["attn_w"], l * (16 * N_ATTN_DMA) + 16 * N_ATTN_DMA)
                for i in range(2):
                    for t, col in ((rot_cos, i), (rot_sin, 2 + i)):
                        nc.vector.tensor_scalar(t[:, i, :], t[:, i, :], qk_scale[:, col:col + 1], None, ALU.mult)\
                          .then_inc(S["tables"], 1)
                dve.wait_ge(S["tables"], l * 4 + 4)
                steps(dve, l, step)
                dve.wait_ge(S["ffn_w"], l * (16 * N_FFN_DMA) + 16 * N_FFN_DMA)
                ffn_norm(l * NSEQ, True)
                with dve.Fori(1, NSEQ) as s:
                    ffn_norm(l * NSEQ + s)
                    ffn_hidden(l, s - 1)
                ffn_hidden(l, NSEQ - 1)
            dve.wait_ge(S["ffn_res"], depth * NSEQ)
            nc.vector.tensor_tensor(res_sb[:, :], res_sb[:, :], u_sb[:, :], ALU.add).then_inc(S["sum_done"], 1)

        @block.tensor
        def _(pe):
            pe.wait_ge(S["const_in"], 48)
            pe.wait_ge(S["consts"], 4)
            pe.wait_ge(S["cast"], 2)

            def v_unit(l, s, p, slot, first):
                q = V_SLOTS[p].get(slot)
                if q is None:
                    return
                half, j = V_UNITS[q]
                done = (l * NSEQ + s) * len(V_UNITS) + q
                if p > 0 and q == min(V_SLOTS[p].values()):
                    if p == WO_STEP and not first:
                        pe.wait_ge(S["attn_res"], l * NSEQ + s)
                    elif first and p <= LAG_VALUE:
                        pe.wait_ge(S["v_done"], done)
                    else:
                        pe.wait_ge(S["y_done"], pair_no(l, s, p) - LAG_VALUE)
                elif p == 0 and q == 0:
                    if not first:
                        pe.wait_ge(S["y_done"], pair_no(l, s, p) - LAG_VALUE)
                else:
                    pe.wait_ge(S["v_done"], done)
                nc.tensor.matmul(misc_bank[0:KEYS, :], xs[:, j * BLK:j * BLK + KEYS],
                                 wv[:, half * (INNER // 2):(half + 1) * (INNER // 2)], start=True, stop=True)\
                  .then_inc(S["v_mm"], 1)

            def step(l, s, p, first):
                n = pair_no(l, s, p)
                full = live(s, p, 0, first)
                if full and p == 0:
                    pe.wait_ge(S["xs_in"], (l * NSEQ + s) * 32 + 32)
                if full:
                    v_unit(l, s, p, "a", first)
                if not first and p == WO_STEP:
                    pe.wait_ge(S["y_done"], pair_no(l, s, 0))
                    for a in range(PAIRS):
                        last = nc.tensor.matmul(misc_bank[:, :], wo[:, a, :], y_t[:, a, :],
                                                start=(a == 0), stop=(a == PAIRS - 1))
                    last.then_inc(S["wo_done"], 1)
                if full:
                    if not (first and p == 0):
                        pe.wait_ge(S["cos_done"], n)
                    for i in range(4):
                        last = nc.tensor.matmul(proj_ps[:, i, :], wqk[:, p, i, :], xs[:, WIN:WIN + SEQ],
                                                start=True, stop=True)
                        if i == 1:
                            last.then_inc(S["proj_qk"], 1)
                    last.then_inc(S["proj_rot"], 1)
                    v_unit(l, s, p, "b", first)
                if live(s, p, LAG_NORM, first):
                    m = n - LAG_NORM
                    pe.wait_ge(S["sq_done"], m + 1)
                    for i in range(2):
                        if not (first and p == LAG_NORM and i == 0):
                            pe.wait_ge(S["guard_done"], 2 * m + i)
                        nc.tensor.matmul(ss_bank[:, :], same_head[:, :], sq[:, (p - LAG_NORM) % 2, i, :],
                                         start=True, stop=True).then_inc(S["ss_done"], 1)
                if live(s, p, LAG_VALUE, first):
                    m = n - LAG_VALUE
                    for h in range(2):
                        pe.wait_ge(S["probs_done"], 2 * m + (h + 1))
                        for b in range(HALF):
                            last = nc.tensor.transpose(score_bank[h][0:KEYS, b * P:(b + 1) * P],
                                                       probs[:, (p - LAG_VALUE) % 2, h * HALF + b, :], ident[:, :])
                        last.then_inc(S["tr_done"], 1)
                if full:
                    v_unit(l, s, p, "c", first)
                if live(s, p, LAG_SCORE, first):
                    m = n - LAG_SCORE
                    pe.wait_ge(S["norm_done"], m + 1)
                    for h in range(2):
                        if not (first and p == LAG_SCORE):
                            pe.wait_ge(S["pt0"] if h == 0 else S["pt1"], m)
                        nc.tensor.matmul(score_bank[h][:, 0:HALF * KEYS], ident_b[:, :],
                                         band_b[:, h * HALF * KEYS:(h + 1) * HALF * KEYS],
                                         start=True, stop=False, skip_group_check=True)
                        for b in range(HALF):
                            j = h * HALF + b
                            last = nc.tensor.matmul(
                                score_bank[h][:, b * KEYS:(b + 1) * KEYS],
                                q_diag[:, p % 2, j, :, :].rearrange("p h q -> p (h q)"),
                                k_t[:, p % 2, j * BLK:j * BLK + KEYS], start=False, stop=(b == HALF - 1),
                                skip_group_check=True)
                        last.then_inc(S["score_done"], 1)
                if live(s, p, LAG_VALUE, first):
                    m = n - LAG_VALUE
                    pair = (p - LAG_VALUE) % PAIRS
                    of = l * NSEQ + s - (1 if p < LAG_VALUE else 0)
                    half = pair // (PAIRS // 2)
                    pe.wait_ge(S["pt0"], m + 1)
                    pe.wait_ge(S["pt1"], m + 1)
                    if p < LAG_VALUE and not full:
                        pe.wait_ge(S["y_done"], m)
                    elif V_SLOTS[p]:
                        pe.wait_ge(S["v_done"], (l * NSEQ + s) * len(V_UNITS) + max(V_SLOTS[p].values()) + 1)
                    else:
                        pe.wait_ge(S["y_done"], m)
                    for b in range(NBLK):
                        for h in range(2):
                            at = ((pair % (PAIRS // 2)) * 2 + h) * HD
                            last = nc.tensor.matmul(
                                misc_bank[HD * h:HD * (h + 1), b * BLK:(b + 1) * BLK], v[0:KEYS, half, b, at:at + HD],
                                probs_t[0:KEYS, b // HALF, b % HALF, h, :], start=True, stop=True,
                                tile_position=(0, HD * h))
                    last.then_inc(S["pv_done"], 1)

            def ffn_mean(f, first=False):
                pe.wait_ge(S["xf_in"], f * 32 + 32)
                if not first:
                    pe.wait_ge(S["f_std"], f)
                nc.tensor.matmul(ss_bank[:, :], mean_w[:, :], xf[:, :], start=True, stop=True).then_inc(S["f_mean"], 1)

            def ffn_var(f):
                pe.wait_ge(S["f_sq"], f + 1)
                nc.tensor.matmul(ss_bank[:, :], mean_w[:, :], fsq[:, :], start=True, stop=True).then_inc(S["f_var"], 1)

            def ffn_up(f, par, c):
                at, m = CHUNKS[c]
                if c == 0:
                    pe.wait_ge(S["f_xa"], f + 1)
                for i in range(2):
                    last = nc.tensor.matmul(up_bank[c][i][0:m, :], w1[:, i * DIM_INNER + at:i * DIM_INNER + at + m],
                                            xa[:, par, :], start=True, stop=True)
                last.then_inc(S["f_up"], 1)

            def ffn_down(f, first=False):
                if not first:
                    pe.wait_ge(S["ffn_res"], f)
                for c, (_, m) in enumerate(CHUNKS):
                    pe.wait_ge(S["f_hid"], f * NC + (c + 1))
                    last = nc.tensor.matmul(misc_bank[:, :], w2[0:m, c, :], hid[0:m, c, :],
                                            start=(c == 0), stop=(c == NC - 1))
                last.then_inc(S["f_down"], 1)

            with pe.Fori(0, depth) as l:
                pe.wait_ge(S["attn_w"], l * (16 * N_ATTN_DMA) + 16 * N_ATTN_DMA)
                steps(pe, l, step)
                pe.wait_ge(S["ffn_w"], l * (16 * N_FFN_DMA) + 16 * N_FFN_DMA)
                pe.wait_ge(S["attn_res"], l * NSEQ + NSEQ)
                ffn_mean(l * NSEQ, True)
                ffn_var(l * NSEQ)

                def ffn_step(f, par, first=False):
                    ffn_mean(f)
                    ffn_up(f - 1, 1 - par, 0)
                    ffn_var(f)
                    for c in range(1, NC):
                        ffn_up(f - 1, 1 - par, c)
                    ffn_down(f - 1, first)

                ffn_step(l * NSEQ + 1, 1, True)
                with pe.Fori(1, NSEQ // 2) as s2:
                    for par in range(2):
                        ffn_step(l * NSEQ + s2 * 2 + par, par)
                for c in range(NC):
                    ffn_up(l * NSEQ + NSEQ - 1, 1, c)
                ffn_down(l * NSEQ + NSEQ - 1)


def program(nc, d, out, depth=DEPTH):
    with ExitStack() as ctx:
        res_sb = ctx.enter_context(nc.sbuf_tensor("res", [P, TOK], F32))
        u_sb = ctx.enter_context(nc.sbuf_tensor("u", [P, TOK], F32))
        build_stage1(nc, d, res_sb, u_sb)
        build_stage2(nc, d, res_sb, u_sb, out, depth)


def shape_constants():
    f32 = np.float32
    half = np.arange(0, HD, 2, dtype=f32)
    inv_freq = (f32(1.0) / np.power(f32(10000.0), half / f32(HD))).astype(f32)
    t = np.arange(SEQ, dtype=f32)
    angle = (t[:, None] * inv_freq[None, :]).astype(f32).astype(np.float64)
    base = ((half + f32(0.4 * HD)) / f32(1.4 * HD)).astype(f32)
    power = ((t - SEQ // 2) / f32(WIN // 2)).astype(f32)
    scale = np.power(base[None, :].astype(np.float64), power[:, None].astype(np.float64))
    cos, sin = np.cos(angle), np.sin(angle)

    def table(a, sign):
        return np.concatenate([sign * a.T, a.T] * 2, axis=0)

    rot_cos = np.stack([-QK_SCALE * table(cos * scale, 1), table(cos / scale, 1)], axis=1).astype(f32)
    rot_sin = np.stack([-QK_SCALE * table(sin * scale, -1), table(sin / scale, -1)], axis=1).astype(f32)
    causal = np.where(np.arange(P)[None, :] > np.arange(P)[:, None], f32(MASKED), f32(0))
    q, k = np.arange(BLK)[:, None], np.arange(KEYS)[None, :]
    band = np.where((k >= q) & (k <= q + WIN), f32(0), f32(MASKED))
    band = np.tile(band[None, :, None, :], (2, 1, NBLK, 1))
    band[:, :, 0, :WIN] = MASKED
    heads = np.arange(P) // HD
    return {
        "c_ident": np.eye(P, dtype=f32), "c_causal": causal.astype(f32),
        "c_band": band.reshape(P, NBLK * KEYS).astype(f32), "c_cos": rot_cos, "c_sin": rot_sin,
        "c_same_head": (heads[:, None] == heads[None, :]).astype(f32),
    }


def lay_out(i):
    def pad_heads(w):
        w = np.asarray(w)
        w = w.reshape(w.shape[:-1] + (HEADS, HD1))
        return np.pad(w, [(0, 0)] * (w.ndim - 1) + [(0, PADH - HD1)]).reshape(w.shape[:-2] + (HEADS * PADH,))

    wo = pad_heads(np.asarray(i["L0_attn_Wo"]).T).T
    qkv = np.asarray(i["L0_ffn_Wqkv"]).reshape(DEPTH, DIM, 3, PAIRS, 2, 2, HD // 2)
    qk = qkv[:, :, 0:2].transpose(0, 1, 3, 2, 4, 5, 6)
    qk_all = np.stack([qk, qk[:, :, :, :, :, ::-1]], axis=3)
    q_scale, k_scale = np.asarray(i["L0_ffn_q_scale"]), np.asarray(i["L0_ffn_k_scale"])

    def both(s):
        return np.concatenate([s, s], axis=1)

    def swapped(s):
        return np.concatenate([s[:, HD // 2:], s[:, :HD // 2]], axis=1)

    b1 = np.asarray(i["L0_ffn_b1"]).reshape(DEPTH, 2, DIM_INNER)
    b1 = np.pad(b1, ((0, 0), (0, 0), (0, NC * P - DIM_INNER))).reshape(DEPTH, 2 * NC, P)
    w2 = np.pad(np.asarray(i["L0_ffn_W2"]), ((0, 0), (0, NC * P - DIM_INNER), (0, 0)))
    arrays = {
        "x": np.asarray(i["L0_attn_x"]).reshape(TOK, DIM).T,
        "a_wq": pad_heads(i["L0_attn_Wq"]), "a_wk": pad_heads(i["L0_attn_Wk"]), "a_wv": pad_heads(i["L0_attn_Wv"]),
        "a_wo": wo.reshape(GROUPS, P, DIM).transpose(1, 0, 2),
        "a_bq": pad_heads(i["L0_attn_bq"]).reshape(GROUPS, P).T,
        "a_bk": pad_heads(i["L0_attn_bk"]).reshape(GROUPS, P).T,
        "a_bv": pad_heads(i["L0_attn_bv"]), "a_bo": np.asarray(i["L0_attn_bo"])[:, None],
        "f_wqk": qk_all.reshape(DEPTH, DIM, PAIRS * 4 * P),
        "f_wv": np.asarray(i["L0_ffn_Wqkv"])[:, :, 2 * INNER:],
        "f_wo": np.asarray(i["L0_ffn_Wo"]).reshape(DEPTH, PAIRS, P, DIM).transpose(0, 2, 1, 3)
        .reshape(DEPTH, P, PAIRS * DIM),
        "f_qk_scale": np.stack([both(q_scale), both(k_scale), both(swapped(q_scale)), both(swapped(k_scale))], axis=2),
        "f_w1": np.asarray(i["L0_ffn_W1"]),
        "f_w2": w2.reshape(DEPTH, NC, P, DIM).transpose(0, 2, 1, 3).reshape(DEPTH, P, NC * DIM),
        "f_vec": np.concatenate([np.asarray(i["L0_ffn_ln_g"])[:, :, None], np.asarray(i["L0_ffn_ln_b"])[:, :, None],
                                 b1.transpose(0, 2, 1), np.asarray(i["L0_ffn_b2"])[:, :, None]], axis=2),
    }
    arrays.update(shape_constants())
    return {k: np.ascontiguousarray(v) for k, v in arrays.items()}


def kernel(**inputs):
    import concourse.bacc as bacc
    from concourse.bass_utils import run_bass_kernel_spmd

    arrays = lay_out(inputs)
    nc = bacc.Bacc("TRN2", target_bir_lowering=False, num_devices=1)
    d = {k: nc.dram_tensor(k, a.shape, mybir.dt.from_np(a.dtype), kind="ExternalInput").ap() for k, a in arrays.items()}
    out = nc.dram_tensor("out", (P, TOK), F32, kind="ExternalOutput").ap()
    program(nc, d, out)
    r = run_bass_kernel_spmd(nc, [arrays], core_ids=[0])
    return np.ascontiguousarray(r.results[0]["out"].T).reshape(NSEQ, SEQ, DIM)
```

```python
from contextlib import ExitStack

import numpy as np

import concourse.bass as bass
from concourse import mybir

F32 = mybir.dt.float32
BF16 = mybir.dt.bfloat16
F32R = mybir.dt.float32r
ACT = mybir.ActivationFunctionType
ALU = mybir.AluOpType
AX = mybir.AxisListType.X

P = 128
NSEQ, SEQ, DIM = 8, 512, 128
TOK = NSEQ * SEQ
HEADS = 16
EPS = 1e-5

HD1, PADH = 8, 32
GROUPS = HEADS * PADH // P
HPG = P // PADH
QB = SEQ // P
UNITS = GROUPS * QB * HPG
SETS = UNITS // HPG
UNIT_LIST = [(g, b, i) for g in range(GROUPS) for b in range(QB) for i in range(HPG)]
TR_LAG, PV_LAG = 4, 6
N_PROBS = 8
WO_AT, RES_LN_AT, X_LN_AT, Q_AT, K_AT, V_AT, DIAG_AT = 8, 11, 17, 24, 27, 30, 42
V_STEP = 3

DEPTH, HD, WIN = 6, 64, 32
INNER = HEADS * HD
PAIRS = HEADS // 2
HALF_HD = HD // 2
QHEADS = P // HALF_HD
QUADS = HEADS // QHEADS
TOKS = SEQ // 2
STEPS = 2 * QUADS
BLK = 2 * WIN
KEYS = BLK + WIN
NBLK = SEQ // BLK
NB = TOKS // BLK
QK_SCALE = 8.0
DIM_INNER = int(DIM * 4 * 2 / 3)
CHUNKS = [(c, min(P, DIM_INNER - c)) for c in range(0, DIM_INNER, P)]
NC = len(CHUNKS)

MASKED = 1e30


def wait(eng, sem, value):
    if not (isinstance(value, int) and value <= 0):
        eng.wait_ge(sem, value)


def build_stage1(nc, d, res_sb, u_sb):
    with ExitStack() as st:
        def sb(name, shape, dt=F32):
            return st.enter_context(nc.sbuf_tensor(name, shape, dt))

        def sem(name):
            return st.enter_context(nc.semaphore(name))

        bank = [st.enter_context(nc.psum_tensor(f"s1_bank{i}", [P, 512], F32)) for i in range(8)]
        proj_bank, y_bank, tr_bank, score_bank = bank[0], bank[1], bank[2:4], bank[4:8]

        x_sb = sb("s1_x", [P, TOK])
        wq = sb("s1_wq", [P, P])
        wk = sb("s1_wk", [P, P])
        wv = sb("s1_wv", [P, GROUPS * P])
        wo = sb("s1_wo", [P, GROUPS, DIM])
        bq = sb("s1_bq", [P, 1])
        bk = sb("s1_bk", [P, 1])
        bv = sb("s1_bv", [P, GROUPS * P])
        bo = sb("s1_bo", [P, 1])
        mean_w = sb("s1_mean_w", [P, P])
        eps = sb("s1_eps", [P, 1])
        ident = sb("s1_ident", [P, P])
        ident_b = sb("s1_ident_b", [P, P], BF16)
        causal = sb("s1_causal", [P, P])
        causal_b = sb("s1_causal_b", [P, P], BF16)
        own_rows = sb("s1_own_rows", [P, HEADS])
        xc = sb("s1_xc", [P, SEQ])
        sq = sb("s1_sq", [P, SEQ])
        rstd = sb("s1_rstd", [P, SEQ])
        xn = sb("s1_xn", [P, SEQ])
        q_t = sb("s1_q", [P, SEQ])
        q_diag = sb("s1_q_diag", [P, 2, HEADS, SEQ])
        k_t = sb("s1_k", [P, 2, SEQ])
        v = sb("s1_v", [P, 2, QB, GROUPS * P])
        neg_max = sb("s1_neg_max", [P, UNITS])
        den = sb("s1_den", [P, UNITS])
        rden = sb("s1_rden", [P, UNITS])
        probs = sb("s1_probs", [P, N_PROBS, SEQ])
        probs_t = sb("s1_probs_t", [P, 2, HPG, QB, P])
        y_t = sb("s1_y", [P, GROUPS, SEQ])

        names = ("loaded const_ready mask_ready ln_mean ln_xc ln_sq ln_var ln_log ln_rstd ln_xn proj_done q_ready k_ready "
                 "v_ready diag_done score_done max_done exp_done rden_done probs_done tr_done pt_vector pt_scalar "
                 "pv_done y_ready wo_done res_done").split()
        S = {n: sem("s1_" + n) for n in names}

        loads = [(x_sb[:, :], d["x"]), (wq[:, :], d["a_wq"]), (wk[:, :], d["a_wk"]), (wv[:, :], d["a_wv"]),
                 (wo[:, :, :], d["a_wo"]), (bq[:, :], d["a_bq"]), (bk[:, :], d["a_bk"]),
                 (bv[:, :], d["a_bv"].partition_broadcast(P)), (bo[:, :], d["a_bo"]),
                 (ident[:, :], d["c_ident"]), (causal[:, :], d["c_causal"]), (own_rows[:, :], d["c_own_rows"])]
        n_loaded = 16 * len(loads)
        block = st.enter_context(nc.Block())

        def seq_of(t, s):
            return t[:, bass.ds(s * SEQ, SEQ)]

        def sequences(eng, prepare, unit, finish):
            def units(s, par, first=False, last=False):
                for t in range(UNITS):
                    unit(s, par, t, first, last)

            prepare(0, 0, 0)
            units(0, 0, first=True)
            with eng.Fori(0, NSEQ // 2 - 1) as pair:
                units(pair * 2 + 1, 1)
                units(pair * 2 + 2, 0)
            units(NSEQ - 1, 1, last=True)
            for t in range(UNITS, UNITS + HPG + PV_LAG):
                unit(NSEQ - 1, 1, t, False, True)
            finish(NSEQ - 1, 2 * NSEQ - 1)

        def behind(s, par, t, lag, first):
            u = t - lag
            if u >= UNITS or (u < 0 and first):
                return None
            return (s, par, u) if u >= 0 else (s - 1, 1 - par, UNITS + u)

        def on_vector(u):
            return u % HPG == 0

        def pt(u):
            return S["pt_vector"] if on_vector(u) else S["pt_scalar"]

        def pt_count(s, u):
            if on_vector(u):
                return s * SETS + (u // HPG + 1)
            return s * (SETS * (HPG - 1)) + (u // HPG * (HPG - 1) + u % HPG)

        @block.sync
        def _(sp):
            for dst, src in loads:
                sp.dma_start(dst, src).then_inc(S["loaded"], 16)

        @block.gpsimd
        def _(pool):
            pool.memset(mean_w[:, :], 1.0 / DIM).then_inc(S["const_ready"], 1)
            pool.memset(eps[:, :], EPS).then_inc(S["const_ready"], 1)

            def normalise(s, u):
                n = P * (UNIT_LIST[u][1] + 1)
                pool.wait_ge(S["rden_done"], s * UNITS + (u + 1))
                row = probs[:, u % N_PROBS, 0:n]
                nc.gpsimd.tensor_tensor(row, row, rden[:, u:u + 1].to_broadcast([P, n]), ALU.mult)\
                  .then_inc(S["probs_done"], 1)

            with pool.Fori(0, NSEQ) as s:
                for u in range(UNITS):
                    normalise(s, u)

        def copy_out(eng_wait, copy, s, u, first):
            nb, of_set = UNIT_LIST[u][1] + 1, u // HPG
            eng_wait(S["tr_done"], s * UNITS + (u + 1))
            if not (first and of_set < 2):
                eng_wait(S["pv_done"], s * SETS + (of_set - 1))
            return copy(probs_t[:, of_set % 2, u % HPG, 0:nb, :].rearrange("p b q -> p (b q)"),
                        tr_bank[u % 2][:, 0:nb * P])

        @block.scalar
        def _(act):
            act.wait_ge(S["const_ready"], 2)

            def square(k):
                act.wait_ge(S["ln_xc"], k + 1)
                nc.scalar.activation(sq[:, :], xc[:, :], ACT.Square).then_inc(S["ln_sq"], 1)

            def inverse_std(k):
                act.wait_ge(S["ln_var"], k + 1)
                nc.scalar.activation(rstd[:, :], proj_bank[:, :], ACT.Ln, bias=eps[:, 0:1]).then_inc(S["ln_log"], 1)
                act.wait_ge(S["ln_log"], k + 1)
                nc.scalar.activation(rstd[:, :], rstd[:, :], ACT.Exp, scale=-0.5).then_inc(S["ln_rstd"], 1)

            def keys(s, par):
                act.wait_ge(S["proj_done"], s * (2 + QB) + 2)
                nc.scalar.activation(k_t[:, par, :], proj_bank[:, :], ACT.Identity, bias=bk[:, 0:1])\
                  .then_inc(S["k_ready"], 1)

            def prepare(s, par, k):
                act.wait_ge(S["loaded"], n_loaded)
                act.preload_act_table_set("natural_log_exp_and_others")
                square(k)
                inverse_std(k)
                keys(s, par)

            def finish(s, k):
                square(k)
                inverse_std(k)

            def unit(s, par, t, first, last):
                if t == 0:
                    act.preload_act_table_set("natural_log_exp_and_others")
                if t < UNITS:
                    n = P * (UNIT_LIST[t][1] + 1)
                    act.wait_ge(S["max_done"], s * UNITS + (t + 1))
                    if not (first and t < N_PROBS):
                        act.wait_ge(S["tr_done"], s * UNITS + (t - N_PROBS + 1))
                    nc.scalar.activation(probs[:, t % N_PROBS, 0:n], score_bank[t % 4][:, 0:n], ACT.Exp, scale=-1.0,
                                         bias=neg_max[:, t:t + 1], accum_out=den[:, t:t + 1]).then_inc(S["exp_done"], 1)
                of = behind(s, par, t, TR_LAG, first)
                if of and not on_vector(of[2]):
                    copy_out(act.wait_ge, lambda o, i: nc.scalar.activation(o, i, ACT.Copy), of[0], of[2], first)\
                        .then_inc(S["pt_scalar"], 1)
                of = behind(s, par, t, PV_LAG + 1, first)
                if of and (of[2] + 1) % (QB * HPG) == 0:
                    g = of[2] // (QB * HPG)
                    act.wait_ge(S["pv_done"], of[0] * SETS + (of[2] + 1) // HPG)
                    if g == 0 and not first:
                        act.wait_ge(S["wo_done"], of[0])
                    nc.scalar.activation(y_t[:, g, :], y_bank[:, :], ACT.Copy).then_inc(S["y_ready"], 1)
                if t < UNITS and not first:
                    if t == RES_LN_AT + 1:
                        square(2 * s)
                    if t == RES_LN_AT + 4:
                        inverse_std(2 * s)
                if t < UNITS and not last:
                    if t == X_LN_AT + 1:
                        square(2 * s + 1)
                    if t == X_LN_AT + 4:
                        inverse_std(2 * s + 1)
                    if t == K_AT + 1:
                        keys(s + 1, 1 - par)

            sequences(act, prepare, unit, finish)

        @block.vector
        def _(dve):
            dve.wait_ge(S["loaded"], n_loaded)
            nc.vector.tensor_copy(ident_b[:, :], ident[:, :]).then_inc(S["mask_ready"], 1)
            nc.vector.tensor_copy(causal_b[:, :], causal[:, :]).then_inc(S["mask_ready"], 1)

            def centre(k, src):
                wait(dve, S["ln_xn"], k)
                dve.wait_ge(S["ln_mean"], k + 1)
                nc.vector.tensor_tensor(xc[:, :], src, proj_bank[:, :], ALU.subtract).then_inc(S["ln_xc"], 1)

            def divide(k, dst):
                dve.wait_ge(S["ln_rstd"], k + 1)
                nc.vector.tensor_tensor(dst, xc[:, :], rstd[:, :], ALU.mult).then_inc(S["ln_xn"], 1)

            def queries(s):
                dve.wait_ge(S["proj_done"], s * (2 + QB) + 1)
                nc.vector.tensor_scalar(q_t[:, :], proj_bank[:, :], bq[:, 0:1], -float(HD1) ** -0.5, ALU.add, ALU.mult)\
                  .then_inc(S["q_ready"], 1)

            def values(s, par, b):
                dve.wait_ge(S["proj_done"], s * (2 + QB) + (2 + b + 1))
                nc.vector.tensor_tensor(v[:, par, b, :], proj_bank[:, :], bv[:, :], ALU.add).then_inc(S["v_ready"], 1)

            def diag(s, par, h):
                dve.wait_ge(S["q_ready"], s + 1)
                nc.vector.tensor_scalar(q_diag[:, par, h, :], q_t[:, :], own_rows[:, h:h + 1], None, ALU.mult)\
                  .then_inc(S["diag_done"], 1)

            def residual(s):
                dve.wait_ge(S["wo_done"], s + 1)
                nc.vector.scalar_tensor_tensor(seq_of(res_sb, s), proj_bank[:, :], bo[:, 0:1], seq_of(x_sb, s),
                                               ALU.add, ALU.add).then_inc(S["res_done"], 1)

            def prepare(s, par, k):
                centre(k, seq_of(x_sb, s))
                divide(k, xn[:, :])
                queries(s)
                for b in range(QB):
                    values(s, par, b)
                for h in range(HEADS):
                    diag(s, par, h)

            def finish(s, k):
                residual(s)
                dve.wait_ge(S["res_done"], s + 1)
                centre(k, seq_of(res_sb, s))
                divide(k, seq_of(u_sb, s))

            def unit(s, par, t, first, last):
                if t < UNITS:
                    n = P * (UNIT_LIST[t][1] + 1)
                    dve.wait_ge(S["score_done"], s * UNITS + (t + 1))
                    nc.vector.tensor_reduce(neg_max[:, t:t + 1], score_bank[t % 4][:, 0:n], AX, ALU.min)\
                      .then_inc(S["max_done"], 1)
                of = behind(s, par, t, 1, first)
                if of:
                    u = of[2]
                    dve.wait_ge(S["exp_done"], of[0] * UNITS + (u + 1))
                    nc.vector.reciprocal(rden[:, u:u + 1], den[:, u:u + 1]).then_inc(S["rden_done"], 1)
                of = behind(s, par, t, TR_LAG, first)
                if of and on_vector(of[2]):
                    copy_out(dve.wait_ge, nc.vector.tensor_copy, of[0], of[2], first).then_inc(S["pt_vector"], 1)
                if t < UNITS and not first:
                    if t == WO_AT:
                        residual(s - 1)
                    if t == RES_LN_AT:
                        dve.wait_ge(S["res_done"], s)
                        centre(2 * s, seq_of(res_sb, s - 1))
                    if t == RES_LN_AT + 5:
                        divide(2 * s, seq_of(u_sb, s - 1))
                if t < UNITS and not last:
                    if t == X_LN_AT:
                        centre(2 * s + 1, seq_of(x_sb, s + 1))
                    if t == X_LN_AT + 5:
                        divide(2 * s + 1, xn[:, :])
                    if t == Q_AT:
                        queries(s + 1)
                    if t >= V_AT and (t - V_AT) % V_STEP == 0 and (t - V_AT) // V_STEP < QB:
                        values(s + 1, 1 - par, (t - V_AT) // V_STEP)
                    if DIAG_AT <= t < DIAG_AT + HEADS:
                        diag(s + 1, 1 - par, t - DIAG_AT)

            sequences(dve, prepare, unit, finish)

        @block.tensor
        def _(pe):
            pe.wait_ge(S["loaded"], n_loaded)
            pe.wait_ge(S["const_ready"], 2)
            pe.wait_ge(S["mask_ready"], 2)

            def mean(src):
                nc.tensor.matmul(proj_bank[:, :], mean_w[:, :], src, start=True, stop=True).then_inc(S["ln_mean"], 1)

            def var(k):
                pe.wait_ge(S["ln_sq"], k + 1)
                nc.tensor.matmul(proj_bank[:, :], mean_w[:, :], sq[:, :], start=True, stop=True).then_inc(S["ln_var"], 1)

            def project(w, ready, count):
                pe.wait_ge(ready, count)
                nc.tensor.matmul(proj_bank[:, :], w[:, :], xn[:, :], start=True, stop=True).then_inc(S["proj_done"], 1)

            def values(s, b):
                if b == 0:
                    pe.wait_ge(S["k_ready"], s + 1)
                else:
                    pe.wait_ge(S["v_ready"], s * QB + b)
                nc.tensor.matmul(proj_bank[:, :], xn[:, b * P:(b + 1) * P], wv[:, :], start=True, stop=True)\
                  .then_inc(S["proj_done"], 1)

            def output(s):
                pe.wait_ge(S["y_ready"], s * GROUPS + GROUPS)
                for g in range(GROUPS):
                    last = nc.tensor.matmul(proj_bank[:, :], wo[:, g, :], y_t[:, g, :],
                                            start=(g == 0), stop=(g == GROUPS - 1))
                last.then_inc(S["wo_done"], 1)

            def prepare(s, par, k):
                mean(seq_of(x_sb, s))
                var(k)
                project(wq, S["ln_xn"], k + 1)
                project(wk, S["q_ready"], s + 1)
                for b in range(QB):
                    values(s, b)

            def finish(s, k):
                output(s)
                pe.wait_ge(S["res_done"], s + 1)
                mean(seq_of(res_sb, s))
                var(k)
                pe.wait_ge(S["ln_xn"], k + 1)

            def unit(s, par, t, first, last):
                if t == 0:
                    pe.wait_ge(S["diag_done"], s * HEADS + HEADS)
                    pe.wait_ge(S["k_ready"], s + 1)
                if t < UNITS:
                    g, b, i = UNIT_LIST[t]
                    n = P * (b + 1)
                    if not (first and t < 4):
                        pe.wait_ge(S["exp_done"], s * UNITS + (t - 3))
                    nc.tensor.matmul(score_bank[t % 4][:, 0:n], q_diag[:, par, g * HPG + i, b * P:(b + 1) * P],
                                     k_t[:, par, 0:n], start=True, stop=False, skip_group_check=True)
                    nc.tensor.matmul(score_bank[t % 4][:, n - P:n], ident_b[:, :], causal_b[:, :],
                                     start=False, stop=True, skip_group_check=True).then_inc(S["score_done"], 1)
                of = behind(s, par, t, TR_LAG, first)
                if of:
                    us, _, u = of
                    pe.wait_ge(S["probs_done"], us * UNITS + (u + 1))
                    if u >= 2:
                        pe.wait_ge(pt(u - 2), pt_count(us, u - 2))
                    elif not (first and u >= 0):
                        pe.wait_ge(pt(UNITS + u - 2), pt_count(us - 1, UNITS + u - 2))
                    for kb in range(UNIT_LIST[u][1] + 1):
                        done = nc.tensor.transpose(tr_bank[u % 2][:, kb * P:(kb + 1) * P],
                                                   probs[:, u % N_PROBS, kb * P:(kb + 1) * P], ident[:, :])
                    done.then_inc(S["tr_done"], 1)
                of = behind(s, par, t, PV_LAG, first)
                if of and (of[2] + 1) % HPG == 0:
                    us, upar, u = of
                    g, b, _ = UNIT_LIST[u]
                    of_set = u // HPG
                    pe.wait_ge(S["pt_vector"], us * SETS + (of_set + 1))
                    pe.wait_ge(S["pt_scalar"], (us * SETS + (of_set + 1)) * (HPG - 1))
                    if of_set == 0:
                        pe.wait_ge(S["v_ready"], us * QB + QB)
                    if b == 0 and not (first and g == 0):
                        pe.wait_ge(S["y_ready"], us * GROUPS + g)
                    for kb in range(b + 1):
                        for i in range(HPG):
                            done = nc.tensor.matmul(
                                y_bank[PADH * i:PADH * (i + 1), b * P:(b + 1) * P],
                                v[:, upar, kb, g * P + PADH * i:g * P + PADH * (i + 1)],
                                probs_t[:, of_set % 2, i, kb, :],
                                start=(kb == 0), stop=(kb == b), tile_position=(0, PADH * i))
                    done.then_inc(S["pv_done"], 1)
                if t < UNITS and not first:
                    if t == WO_AT:
                        output(s - 1)
                    if t == RES_LN_AT:
                        pe.wait_ge(S["res_done"], s)
                        mean(seq_of(res_sb, s - 1))
                    if t == RES_LN_AT + 3:
                        var(2 * s)
                if t < UNITS and not last:
                    if t == X_LN_AT:
                        if first:
                            pe.wait_ge(S["v_ready"], QB)
                        else:
                            pe.wait_ge(S["ln_log"], 2 * s + 1)
                        mean(seq_of(x_sb, s + 1))
                    if t == X_LN_AT + 3:
                        var(2 * s + 1)
                    if t == Q_AT:
                        project(wq, S["ln_xn"], 2 * s + 2)
                    if t == K_AT:
                        project(wk, S["q_ready"], s + 2)
                    if t >= V_AT and (t - V_AT) % V_STEP == 0 and (t - V_AT) // V_STEP < QB:
                        values(s + 1, (t - V_AT) // V_STEP)

            sequences(pe, prepare, unit, finish)


V_UNITS = [(half, j) for half in range(2) for j in range(NBLK)]
V_PER_STEP = len(V_UNITS) // STEPS
LAG_MIX, LAG_NORM, LAG_SCORE, LAG_VALUE = 1, 2, 3, 4
WO_STEP = LAG_VALUE
LN_STEP = WO_STEP + 1
POOL_Q = [(head, head // 2) for head in range(1, QHEADS)]
VECTOR_Q = [(0, 0)] + [(head, 1 - head // 2) for head in range(QHEADS)]
LN_SCALE = 2.0 ** 16
NORM_FLOOR = 1e-24


def build_stage2(nc, d, res_sb, u_sb, out, depth):
    with ExitStack() as st:
        def sb(name, shape, dt=F32):
            return st.enter_context(nc.sbuf_tensor(name, shape, dt))

        def sem(name):
            return st.enter_context(nc.semaphore(name))

        proj_ps = st.enter_context(nc.psum_tensor("s2_proj", [P, 2, 2, TOKS], F32))
        bank = [st.enter_context(nc.psum_tensor(f"s2_bank{i}", [P, 512], F32)) for i in range(2, 8)]
        ss_bank, score_bank, v_bank, y_bank = bank[0], bank[1:3], bank[3:5], bank[5]
        up_bank = [tuple(proj_ps[:, i, :, :].rearrange("p a t -> p (a t)") for i in range(2)),
                   (v_bank[0][:, :], v_bank[1][:, :]), (score_bank[0][:, :], score_bank[1][:, :])]

        w_high = sb("s2_w_high", [P, QUADS * 4 * P + INNER], F32R)
        w_rest = sb("s2_w_rest", [P, QUADS * 4 * P + INNER], F32R)
        wqk = [w[:, 0:QUADS * 4 * P].rearrange("p (a b n) -> p a b n", a=QUADS, b=4) for w in (w_high, w_rest)]
        wv = [w[:, QUADS * 4 * P:] for w in (w_high, w_rest)]
        wo = sb("s2_wo", [P, PAIRS, DIM])
        qk_scale = sb("s2_qk_scale", [P, 4])
        w1 = sb("s2_w1", [P, 2 * DIM_INNER])
        w2 = sb("s2_w2", [P, NC, DIM])
        vec = sb("s2_vec", [P, 2 + 2 * NC + 1])
        ln_g, ln_b, b2 = vec[:, 0:1], vec[:, 1:2], vec[:, 2 + 2 * NC:3 + 2 * NC]
        rot_cos = sb("s2_cos", [P, 2, 2, SEQ])
        rot_sin = sb("s2_sin", [P, 2, 2, SEQ])
        ident = sb("s2_ident", [P, P])
        ident_b = sb("s2_ident_b", [P, P], BF16)
        band_b = sb("s2_band_b", [P, 2, NB * KEYS], BF16)
        same_head = sb("s2_same_head", [P, P])
        mean_w = sb("s2_mean_w", [P, P])
        eps = sb("s2_eps", [P, 1])
        ln_shift = sb("s2_ln_shift", [P, 1])
        xs_raw = sb("s2_xs_raw", [P, WIN + SEQ])
        xs_high = sb("s2_xs_high", [P, WIN + SEQ], F32R)
        xs_rest = sb("s2_xs_rest", [P, WIN + SEQ], F32R)
        v = sb("s2_v", [P, 2, NBLK, INNER // 2])
        sq = sb("s2_sq", [P, 2, 2, TOKS])
        by_sin = sb("s2_by_sin", [P, 2, 2, TOKS])
        rotated = sb("s2_rotated", [P, 2, 2, 2, TOKS])
        inv_norm = sb("s2_inv_norm", [P, 2, 2, TOKS])
        q_diag = sb("s2_q_diag", [P, 2, 2, NB, 2, BLK])
        k_t = sb("s2_k", [P, 2, 2, WIN + SEQ])
        neg_max = sb("s2_neg_max", [P, 2, 2, NB])
        den = sb("s2_den", [P, 2, 2, NB])
        rden = sb("s2_rden", [P, 2, 2, NB])
        probs = sb("s2_probs", [P, 2, 2, NB, KEYS])
        probs_t = sb("s2_probs_t", [P, 2, NB, 2, BLK])
        y_t = sb("s2_y", [P, PAIRS, SEQ])
        w_raw = y_t[:, :, :].rearrange("p a t -> p (a t)")[:, 0:QUADS * 4 * P + INNER]
        xf = sb("s2_xf", [P, SEQ])
        xc = sb("s2_xc", [P, SEQ])
        rstd = sb("s2_rstd", [P, SEQ])
        xa = sb("s2_xa", [P, TOK])
        v_flat = v[:, :, :, :].rearrange("p a b n -> p (a b n)")
        gate = [v_flat[:, c * SEQ:(c + 1) * SEQ] for c in range(NC)]
        hid = [[v_flat[:, c * SEQ:(c + 1) * SEQ] for c in range((par + 1) * NC, (par + 2) * NC)] for par in range(2)]

        names = ("const_in consts cast zeroed attn_w ffn_w tables w_high w_rest xs_in xs_high xs_rest proj_done sq_done sqadd_done prod_done "
                 "add_done ss_done guard_done log_done inv_done norm_done qd_done score_done max_done exp_done "
                 "rden_done probs_done tr_done pt_done v_mm v_done pv_done y_done wo_done attn_res "
                 "xf_in f_mean f_xc f_sq f_var f_log f_rstd f_xn f_xa f_up f_gate f_hid f_down ffn_res "
                 "sum_done stored").split()
        S = {n: sem("s2_" + n) for n in names}
        N_ATTN_DMA, N_FFN_DMA = 6, 3
        NQP = len(POOL_Q)

        block = st.enter_context(nc.Block())

        def seq_of(t, s):
            return t[:, bass.ds(s * SEQ, SEQ)]

        def steps(eng, l, body):
            for p in range(STEPS):
                body(l, 0, p, True)
            with eng.Fori(1, NSEQ) as s:
                for p in range(STEPS):
                    body(l, s, p, False)
            for p in range(WO_STEP + 1):
                body(l, NSEQ, p, False)

        def live(s, p, lag, first):
            if first:
                return p >= lag
            return p < lag if isinstance(s, int) else True

        def step_no(l, s, p):
            return l * (NSEQ * STEPS) + s * STEPS + p

        def place(p, lag):
            m = (p - lag) % STEPS
            return m // 2, m % 2, m % 2

        @block.sync
        def _(sp):
            sp.dma_start(ident[:, :], d["c_ident"]).then_inc(S["const_in"], 16)
            sp.dma_start(by_sin[:, :, :, :].rearrange("p a b t -> p (a b t)")[:, 0:2 * NB * KEYS], d["c_band"])\
              .then_inc(S["const_in"], 16)
            sp.dma_start(same_head[:, :], d["c_same_head"]).then_inc(S["const_in"], 16)
            sp.wait_ge(S["zeroed"], 3)
            def layer(l, first):
                def of_layer(name):
                    a = d[name]
                    return (a[0:1] if first else a[bass.ds(l, 1)]).rearrange("o p n -> (o p) n")

                if not first:
                    sp.wait_ge(S["attn_res"], l * NSEQ)
                for dst, src in ((w_raw[:, 0:QUADS * 4 * P], of_layer("f_wqk")),
                                 (w_raw[:, QUADS * 4 * P:], of_layer("f_wv")),
                                 (wo[:, :, :].rearrange("p a n -> p (a n)"), of_layer("f_wo")),
                                 (qk_scale[:, :], of_layer("f_qk_scale")),
                                 (rot_cos[:, :, 0, :], d["c_cos"]), (rot_sin[:, :, 0, :], d["c_sin"])):
                    sp.dma_start(dst, src).then_inc(S["attn_w"], 16)

                def shifted(s):
                    at = s * SEQ if isinstance(s, int) else sp.snap(s * SEQ)
                    if not isinstance(s, int):
                        sp.wait_ge(S["xs_rest"], l * NSEQ + s)
                    sp.dma_start(xs_raw[0:64, WIN:WIN + SEQ], u_sb[0:64, bass.ds(at, SEQ)]).then_inc(S["xs_in"], 16)
                    sp.dma_start(xs_raw[64:128, WIN + 1:WIN + SEQ], u_sb[64:128, bass.ds(at, SEQ - 1)])\
                      .then_inc(S["xs_in"], 16)

                def shifted_ffn(s):
                    at = s * SEQ if isinstance(s, int) else sp.snap(s * SEQ)
                    sp.wait_ge(S["attn_res"], l * NSEQ + s + 1)
                    sp.dma_start(xf[0:64, :], u_sb[0:64, bass.ds(at, SEQ)]).then_inc(S["xf_in"], 16)
                    sp.dma_start(xf[64:128, 1:SEQ], u_sb[64:128, bass.ds(at, SEQ - 1)]).then_inc(S["xf_in"], 16)

                if not first:
                    sp.wait_ge(S["ffn_res"], (l - 1) * NSEQ + 1)
                shifted(0)
                if not first:
                    sp.wait_ge(S["ffn_res"], l * NSEQ)
                for dst, src in ((w1[:, :], of_layer("f_w1")),
                                 (w2[:, :, :].rearrange("p a n -> p (a n)"), of_layer("f_w2")),
                                 (vec[:, :], of_layer("f_vec"))):
                    sp.dma_start(dst, src).then_inc(S["ffn_w"], 16)
                with sp.Fori(1, NSEQ) as s:
                    shifted(s)
                    shifted_ffn(s - 1)
                shifted_ffn(NSEQ - 1)

            layer(0, True)
            if depth > 1:
                with sp.Fori(1, depth) as l:
                    layer(l, False)
            sp.wait_ge(S["sum_done"], 1)
            sp.dma_start(out, res_sb[:, :]).then_inc(S["stored"], 16)
            sp.wait_ge(S["stored"], 16)

        def write_q(eng, p, head, half):
            par = place(p, LAG_NORM)[2]
            src = slice(HALF_HD * head, HALF_HD * (head + 1))
            row = HD * half + HALF_HD * (head % 2)
            return eng.tensor_tensor(
                q_diag[row:row + HALF_HD, par, head // 2, :, head % 2, :],
                rotated[src, par, 0, half, :].rearrange("p (b q) -> p b q", q=BLK),
                inv_norm[src, par, 0, :].rearrange("p (b q) -> p b q", q=BLK), ALU.mult)

        def write_k(eng, p, pair, half):
            quad, toks, par = place(p, LAG_NORM)
            src, dst = slice(HD * pair, HD * (pair + 1)), slice(HD * half, HD * (half + 1))
            at = WIN + toks * TOKS
            return eng.tensor_tensor(k_t[dst, quad % 2, pair, at:at + TOKS], rotated[src, par, 1, half, :],
                                     inv_norm[src, par, 1, :], ALU.mult)

        def copy_out(eng_wait, copy, n, p, first):
            m = n - LAG_VALUE
            if not (first and p == LAG_VALUE):
                eng_wait(S["pv_done"], m)
            for h in range(2):
                eng_wait(S["tr_done"], 2 * m + (h + 1))
                copy(probs_t[0:KEYS, h, :, :, :].rearrange("p b h q -> p (b h q)"), score_bank[h][0:KEYS, :])\
                    .then_inc(S["pt_done"], 1)

        @block.gpsimd
        def _(pool):
            pool.memset(xs_raw[:, 0:WIN + 1], 0.0).then_inc(S["zeroed"], 1)
            pool.memset(xf[:, 0:1], 0.0).then_inc(S["zeroed"], 1)
            pool.memset(k_t[:, :, :, 0:WIN], 0.0).then_inc(S["zeroed"], 1)
            pool.memset(q_diag[:, :, :, :, :, :].rearrange("p a b c h q -> p (a b c h q)"), 0.0).then_inc(S["consts"], 1)
            pool.memset(mean_w[:, :], 1.0 / DIM).then_inc(S["consts"], 1)
            pool.memset(eps[:, :], EPS).then_inc(S["consts"], 1)
            pool.memset(ln_shift[:, :], 0.5 * float(np.log(LN_SCALE))).then_inc(S["consts"], 1)
            pool.wait_ge(S["consts"], 4)

            def step(l, s, p, first):
                n = step_no(l, s, p)

                def rotate(half):
                    par = place(p, LAG_MIX)[2]
                    nc.gpsimd.tensor_tensor(rotated[:, par, :, half, :], rotated[:, par, :, half, :],
                                            by_sin[:, :, 1 - half, :], (ALU.subtract, ALU.add)[half])\
                      .then_inc(S["add_done"], 1)

                def normalise(h, written):
                    m, par = n - LAG_SCORE, place(p, LAG_SCORE)[2]
                    if written is not None:
                        pool.wait_ge(S["qd_done"], written)
                    pool.wait_ge(S["rden_done"], 2 * m + (h + 1))
                    part = probs[:, par, h, :, :]
                    by = rden[:, par, h, :].unsqueeze(2).to_broadcast([P, NB, KEYS])
                    nc.gpsimd.tensor_tensor(part, part, by, ALU.mult).then_inc(S["probs_done"], 1)

                norm, score = live(s, p, LAG_NORM, first), live(s, p, LAG_SCORE, first)
                mix = live(s, p, LAG_MIX, first)
                if p == 0 and live(s, p, 0, first):
                    pool.wait_ge(S["xs_high"], l * NSEQ + s + 1)
                    nc.gpsimd.tensor_tensor(xs_rest[:, :], xs_raw[:, :], xs_high[:, :].bitcast(F32), ALU.subtract)\
                      .then_inc(S["xs_rest"], 1)
                written = NQP * (n - LAG_NORM + 1) if norm else None
                if mix:
                    m = n - LAG_MIX
                    pool.wait_ge(S["sq_done"], m + 1)
                    nc.gpsimd.tensor_tensor(sq[:, :, 0, :], sq[:, :, 0, :], sq[:, :, 1, :], ALU.add)\
                      .then_inc(S["sqadd_done"], 1)
                if norm:
                    m = n - LAG_NORM
                    pool.wait_ge(S["inv_done"], m + 1)
                    pool.wait_ge(S["add_done"], 2 * m + 2)
                    if not (first and p < LAG_NORM + 2):
                        pool.wait_ge(S["score_done"], 2 * m - 2)
                    pool.wait_ge(S["add_done"], 2 * m + 2)
                    if mix:
                        pool.wait_ge(S["sqadd_done"], m + 2)
                    else:
                        pool.wait_ge(S["probs_done"], 2 * (n - LAG_SCORE))
                    for i, (head, half) in enumerate(POOL_Q):
                        if i:
                            pool.wait_ge(S["qd_done"], NQP * m + i)
                        write_q(nc.gpsimd, p, head, half).then_inc(S["qd_done"], 1)
                if score:
                    normalise(0, written)
                    normalise(1, None)
                if mix:
                    if norm and not score:
                        pool.wait_ge(S["qd_done"], written)
                    m = n - LAG_MIX
                    pool.wait_ge(S["prod_done"], 2 * m + 2)
                    rotate(0)
                    rotate(1)

            with pool.Fori(0, depth) as l:
                pool.wait_ge(S["attn_w"], l * (16 * N_ATTN_DMA) + 16 * N_ATTN_DMA)
                for half in (1, 0):
                    for i in range(2):
                        by = qk_scale[:, 2 * i + half:2 * i + half + 1].to_broadcast([P, SEQ])
                        for t in (rot_cos, rot_sin):
                            nc.gpsimd.tensor_tensor(t[:, i, half, :], t[:, i, 0, :], by, ALU.mult)\
                              .then_inc(S["tables"], 1)
                    if half:
                        pool.wait_ge(S["tables"], l * 8 + 4)
                nc.gpsimd.tensor_copy(w_high[:, :], w_raw).then_inc(S["w_high"], 1)
                pool.wait_ge(S["w_high"], l + 1)
                nc.gpsimd.tensor_tensor(w_rest[:, :], w_raw, w_high[:, :].bitcast(F32), ALU.subtract)\
                  .then_inc(S["w_rest"], 1)
                steps(pool, l, step)

        @block.scalar
        def _(act):
            act.wait_ge(S["consts"], 4)

            def v_unit(l, s, p, i):
                q = p * V_PER_STEP + i
                half, j = V_UNITS[q]
                act.wait_ge(S["v_mm"], (l * NSEQ + s) * len(V_UNITS) + (q + 1))
                nc.scalar.activation(v[0:KEYS, half, j, :], v_bank[i][0:KEYS, :], ACT.Copy).then_inc(S["v_done"], 1)

            def centred_square(f):
                act.wait_ge(S["f_xc"], f + 1)
                nc.scalar.activation(rstd[:, :], xc[:, :], ACT.Square).then_inc(S["f_sq"], 1)

            def inverse_std(f):
                act.wait_ge(S["f_var"], f + 1)
                nc.scalar.activation(rstd[:, :], ss_bank[:, :], ACT.Ln, bias=eps[:, 0:1]).then_inc(S["f_log"], 1)
                act.wait_ge(S["f_log"], f + 1)
                nc.scalar.activation(rstd[:, :], rstd[:, :], ACT.Exp, scale=-0.5).then_inc(S["f_rstd"], 1)

            def step(l, s, p, first):
                n = step_no(l, s, p)
                full = live(s, p, 0, first)
                if p == 0:
                    act.preload_act_table_set("natural_log_exp_and_others")
                f = l * NSEQ + s - 1
                ln = full and not first
                if live(s, p, LAG_VALUE, first) and p > 0:
                    copy_out(act.wait_ge, lambda o, i: nc.scalar.activation(o, i, ACT.Copy), n, p, first)
                if full and p == 0:
                    act.wait_ge(S["xs_in"], (l * NSEQ + s) * 32 + 32)
                    if not first:
                        act.wait_ge(S["proj_done"], n)
                    nc.scalar.activation(xs_high[:, :], xs_raw[:, :], ACT.Copy).then_inc(S["xs_high"], 1)
                if full and p > 0:
                    v_unit(l, s, p, 0)
                if live(s, p, LAG_NORM, first):
                    m, par = n - LAG_NORM, place(p, LAG_NORM)[2]
                    act.wait_ge(S["guard_done"], m + 1)
                    nc.scalar.activation(inv_norm[:, par, :, :], inv_norm[:, par, :, :], ACT.Ln, scale=LN_SCALE)\
                      .then_inc(S["log_done"], 1)
                    act.wait_ge(S["log_done"], m + 1)
                    nc.scalar.activation(inv_norm[:, par, :, :], inv_norm[:, par, :, :], ACT.Exp, scale=-0.5,
                                         bias=ln_shift[:, 0:1]).then_inc(S["inv_done"], 1)
                if ln and p == LN_STEP + 1:
                    centred_square(f)
                if ln and p == LN_STEP + 2:
                    inverse_std(f)
                if live(s, p, LAG_SCORE, first):
                    m, par = n - LAG_SCORE, place(p, LAG_SCORE)[2]
                    if not (first and p < LAG_SCORE + 2):
                        act.wait_ge(S["tr_done"], 2 * m - 2)
                    for h in range(2):
                        act.wait_ge(S["max_done"], 2 * m + (h + 1))
                        for b in range(NB):
                            last = nc.scalar.activation(probs[:, par, h, b, :],
                                                        score_bank[h][:, b * KEYS:(b + 1) * KEYS], ACT.Exp,
                                                        scale=-1.0, bias=neg_max[:, par, h, b:b + 1],
                                                        accum_out=den[:, par, h, b:b + 1])
                        last.then_inc(S["exp_done"], 1)
                if full and p == 0:
                    v_unit(l, s, p, 0)
                if full:
                    v_unit(l, s, p, 1)
                if full:
                    act.wait_ge(S["proj_done"], n + 1)
                    if not (first and p == 0):
                        act.wait_ge(S["ss_done"], n)
                    nc.scalar.activation(sq[:, :, :, :], proj_ps[:, :, :, :], ACT.Square)\
                      .then_inc(S["sq_done"], 1)
                if live(s, p, LAG_VALUE, first):
                    m = n - LAG_VALUE
                    quad, half, _ = place(p, LAG_VALUE)
                    act.wait_ge(S["pv_done"], m + 1)
                    if p == LAG_VALUE and not first:
                        act.wait_ge(S["wo_done"], l * NSEQ + s)
                    nc.scalar.activation(y_t[:, 2 * quad:2 * quad + 2, half * TOKS:(half + 1) * TOKS],
                                         y_bank[:, :].rearrange("p (a t) -> p a t", a=2), ACT.Copy)\
                      .then_inc(S["y_done"], 1)

            def ffn_gate(f):
                for c, (_, m) in enumerate(CHUNKS):
                    act.wait_ge(S["f_up"], f * NC + (c + 1))
                    nc.scalar.activation(gate[c][0:m, :], up_bank[c][1][0:m, :], ACT.Gelu,
                                         bias=vec[0:m, 2 + NC + c:3 + NC + c]).then_inc(S["f_gate"], 1)

            with act.Fori(0, depth) as l:
                steps(act, l, step)
                act.wait_ge(S["ffn_w"], l * (16 * N_FFN_DMA) + 16 * N_FFN_DMA)
                f = l * NSEQ + NSEQ - 1
                ffn_gate(l * NSEQ)
                ffn_gate(l * NSEQ + 1)
                centred_square(f)
                ffn_gate(l * NSEQ + 2)
                inverse_std(f)
                ffn_gate(l * NSEQ + 3)
                with act.Fori(4, NSEQ) as s:
                    ffn_gate(l * NSEQ + s)

        @block.vector
        def _(dve):
            dve.wait_ge(S["const_in"], 48)
            nc.vector.tensor_copy(ident_b[:, :], ident[:, :]).then_inc(S["cast"], 1)
            nc.vector.tensor_copy(band_b[:, :, :].rearrange("p a k -> p (a k)"),
                                  by_sin[:, :, :, :].rearrange("p a b t -> p (a b t)")[:, 0:2 * NB * KEYS])\
              .then_inc(S["cast"], 1)
            dve.wait_ge(S["consts"], 4)
            dve.wait_ge(S["cast"], 2)

            def centre(f):
                dve.wait_ge(S["f_mean"], f + 1)
                nc.vector.tensor_tensor(xc[:, :], xf[:, :], ss_bank[:, :], ALU.subtract).then_inc(S["f_xc"], 1)

            def divide(l, s):
                f = l * NSEQ + s
                dve.wait_ge(S["f_rstd"], f + 1)
                nc.vector.tensor_tensor(xc[:, :], xc[:, :], rstd[:, :], ALU.mult).then_inc(S["f_xn"], 1)

            def scale_shift(l, s):
                f = l * NSEQ + s
                dve.wait_ge(S["ffn_w"], l * (16 * N_FFN_DMA) + 16 * N_FFN_DMA)
                dve.wait_ge(S["f_xn"], f + 1)
                nc.vector.tensor_scalar(seq_of(xa, s), xc[:, :], ln_g, ln_b, ALU.mult, ALU.add).then_inc(S["f_xa"], 1)

            def ffn_hidden(f, par):
                for c, (_, m) in enumerate(CHUNKS):
                    dve.wait_ge(S["f_gate"], f * NC + (c + 1))
                    nc.vector.scalar_tensor_tensor(hid[par][c][0:m, :], up_bank[c][0][0:m, :], vec[0:m, 2 + c:3 + c],
                                                   gate[c][0:m, :], ALU.add, ALU.mult).then_inc(S["f_hid"], 1)

            def step(l, s, p, first):
                n = step_no(l, s, p)
                ln = live(s, p, 0, first) and not first
                if ln and p == LN_STEP + 1:
                    centre(l * NSEQ + s - 1)
                norm, score = live(s, p, LAG_NORM, first), live(s, p, LAG_SCORE, first)

                def least(h):
                    m, par = n - LAG_SCORE, place(p, LAG_SCORE)[2]
                    dve.wait_ge(S["score_done"], 2 * m + (h + 1))
                    nc.vector.tensor_reduce(neg_max[:, par, h, :],
                                            score_bank[h][:, 0:NB * KEYS].rearrange("p (b k) -> p b k", k=KEYS),
                                            AX, ALU.min).then_inc(S["max_done"], 1)

                def inverse_sum(h):
                    m, par = n - LAG_SCORE, place(p, LAG_SCORE)[2]
                    dve.wait_ge(S["exp_done"], 2 * m + (h + 1))
                    nc.vector.reciprocal(rden[:, par, h, :], den[:, par, h, :]).then_inc(S["rden_done"], 1)

                if score:
                    least(0)
                if norm:
                    m = n - LAG_NORM
                    dve.wait_ge(S["inv_done"], m + 1)
                    dve.wait_ge(S["add_done"], 2 * m + 2)
                    if not (first and p < LAG_NORM + 2):
                        dve.wait_ge(S["score_done"], 2 * m - 2)
                    for c in range(2):
                        write_k(nc.vector, p, 0, c)
                if score:
                    least(1)
                if norm:
                    for c in range(2):
                        write_k(nc.vector, p, 1, c)
                if ln and p == LN_STEP + 2:
                    divide(l, s - 1)
                if score:
                    inverse_sum(0)
                if norm:
                    for head, c in VECTOR_Q[:2]:
                        write_q(nc.vector, p, head, c)
                if ln and p == LN_STEP + 2:
                    scale_shift(l, s - 1)
                if score:
                    inverse_sum(1)
                if norm:
                    for head, c in VECTOR_Q[2:]:
                        last = write_q(nc.vector, p, head, c)
                    last.then_inc(S["norm_done"], 1)
                if live(s, p, LAG_MIX, first):
                    m, par = n - LAG_MIX, place(p, LAG_MIX)[2]
                    dve.wait_ge(S["ss_done"], m + 1)
                    if not (first and p < LAG_MIX + 2):
                        dve.wait_ge(S["norm_done"], m - 1)
                        dve.wait_ge(S["qd_done"], NQP * (m - 1))
                    nc.vector.tensor_scalar(inv_norm[:, par, :, :].rearrange("p a t -> p (a t)"), ss_bank[:, :],
                                            NORM_FLOOR, None, ALU.max).then_inc(S["guard_done"], 1)
                if live(s, p, 0, first) and p == STEPS - 1:
                    copy_out(dve.wait_ge, nc.vector.tensor_copy, n + 1, 0, False)
                if live(s, p, 0, first):
                    _, half, par = place(p, 0)
                    toks = slice(half * TOKS, (half + 1) * TOKS)
                    dve.wait_ge(S["sq_done"], n + 1)
                    if not (first and p < 2):
                        dve.wait_ge(S["norm_done"], n - 1)
                        dve.wait_ge(S["qd_done"], NQP * (n - 1))
                    nc.vector.tensor_tensor(rotated[:, par, :, :, :], proj_ps[:, :, :, :], rot_cos[:, :, :, toks],
                                            ALU.mult).then_inc(S["prod_done"], 1)
                    if not (first and p == 0):
                        dve.wait_ge(S["add_done"], 2 * n)
                    nc.vector.tensor_tensor(by_sin[:, :, :, :], proj_ps[:, :, :, :], rot_sin[:, :, :, toks],
                                            ALU.mult).then_inc(S["prod_done"], 1)
                if s is NSEQ and p == WO_STEP:
                    ffn_hidden(l * NSEQ, 0)
                if not first and p == WO_STEP:
                    r = l * NSEQ + s
                    dve.wait_ge(S["wo_done"], r)
                    nc.vector.tensor_tensor(seq_of(u_sb, s - 1), y_bank[:, :], seq_of(u_sb, s - 1), ALU.add)\
                      .then_inc(S["attn_res"], 1)

            def ffn_add(f, s):
                dve.wait_ge(S["f_down"], f + 1)
                nc.vector.scalar_tensor_tensor(seq_of(u_sb, s), y_bank[:, :], b2, seq_of(u_sb, s),
                                               ALU.add, ALU.add).then_inc(S["ffn_res"], 1)

            with dve.Fori(0, depth) as l:
                dve.wait_ge(S["tables"], l * 8 + 8)
                steps(dve, l, step)
                ffn_hidden(l * NSEQ + 1, 1)
                ffn_add(l * NSEQ, 0)
                centre(l * NSEQ + NSEQ - 1)
                ffn_hidden(l * NSEQ + 2, 0)
                ffn_add(l * NSEQ + 1, 1)
                divide(l, NSEQ - 1)
                scale_shift(l, NSEQ - 1)
                ffn_hidden(l * NSEQ + 3, 1)
                ffn_add(l * NSEQ + 2, 2)
                with dve.Fori(2, NSEQ // 2) as s2:
                    for par in range(2):
                        f = l * NSEQ + s2 * 2 + par
                        ffn_hidden(f, par)
                        ffn_add(f - 1, s2 * 2 + par - 1)
                ffn_add(l * NSEQ + NSEQ - 1, NSEQ - 1)
            dve.wait_ge(S["ffn_res"], depth * NSEQ)
            nc.vector.tensor_tensor(res_sb[:, :], res_sb[:, :], u_sb[:, :], ALU.add).then_inc(S["sum_done"], 1)

        @block.tensor
        def _(pe):
            pe.wait_ge(S["const_in"], 48)
            pe.wait_ge(S["consts"], 4)
            pe.wait_ge(S["cast"], 2)

            def v_unit(l, s, p, i, first):
                q = p * V_PER_STEP + i
                half, j = V_UNITS[q]
                if not (first and p == 0):
                    pe.wait_ge(S["v_done"], (l * NSEQ + s) * len(V_UNITS) + (q - V_PER_STEP + 1))
                toks, cols = slice(j * BLK, j * BLK + KEYS), slice(half * (INNER // 2), (half + 1) * (INNER // 2))
                out_ps = v_bank[i][0:KEYS, :]
                nc.tensor.matmul(out_ps, xs_high[:, toks], wv[0][:, cols], start=True, stop=False)
                nc.tensor.matmul(out_ps, xs_high[:, toks], wv[1][:, cols], start=False, stop=False)
                nc.tensor.matmul(out_ps, xs_rest[:, toks], wv[0][:, cols], start=False, stop=True)\
                  .then_inc(S["v_mm"], 1)

            def ffn_mean(f):
                pe.wait_ge(S["xf_in"], f * 32 + 32)
                nc.tensor.matmul(ss_bank[:, :], mean_w[:, :], xf[:, :], start=True, stop=True).then_inc(S["f_mean"], 1)

            def ffn_var(f):
                pe.wait_ge(S["f_sq"], f + 1)
                nc.tensor.matmul(ss_bank[:, :], mean_w[:, :], rstd[:, :], start=True, stop=True)\
                  .then_inc(S["f_var"], 1)

            def ffn_up(f, s, c):
                at, m = CHUNKS[c]
                for i in range(2):
                    last = nc.tensor.matmul(up_bank[c][i][0:m, :], w1[:, i * DIM_INNER + at:i * DIM_INNER + at + m],
                                            seq_of(xa, s), start=True, stop=True)
                last.then_inc(S["f_up"], 1)

            def step(l, s, p, first):
                n = step_no(l, s, p)
                full = live(s, p, 0, first)
                if full and p > 0:
                    v_unit(l, s, p, 0, first)
                if live(s, p, LAG_SCORE, first):
                    m = n - LAG_SCORE
                    quad, half, par = place(p, LAG_SCORE)
                    pe.wait_ge(S["norm_done"], m + 1)
                    pe.wait_ge(S["qd_done"], NQP * (m + 1))
                    for h in range(2):
                        if not (first and p == LAG_SCORE):
                            pe.wait_ge(S["pt_done"], 2 * m + (h - 1))
                        nc.tensor.matmul(score_bank[h][:, 0:NB * KEYS], ident_b[:, :], band_b[:, half, :],
                                         start=True, stop=False, skip_group_check=True)
                        for b in range(NB):
                            at = half * TOKS + b * BLK
                            last = nc.tensor.matmul(
                                score_bank[h][:, b * KEYS:(b + 1) * KEYS],
                                q_diag[:, par, h, b, :, :].rearrange("p h q -> p (h q)"),
                                k_t[:, quad % 2, h, at:at + KEYS], start=False, stop=(b == NB - 1),
                                skip_group_check=True)
                        last.then_inc(S["score_done"], 1)
                if full and p == 0:
                    pe.wait_ge(S["xs_rest"], l * NSEQ + s + 1)
                    v_unit(l, s, p, 0, first)
                if full:
                    v_unit(l, s, p, 1, first)
                if live(s, p, LAG_MIX, first):
                    m = n - LAG_MIX
                    pe.wait_ge(S["sqadd_done"], m + 1)
                    if not (first and p == LAG_MIX):
                        pe.wait_ge(S["guard_done"], m)
                    if full and not first and p == LN_STEP + 1:
                        pe.wait_ge(S["f_xc"], l * NSEQ + s)
                    if full and not first and p == LN_STEP + 2:
                        pe.wait_ge(S["f_log"], l * NSEQ + s)
                    for i in range(2):
                        last = nc.tensor.matmul(ss_bank[:, i * TOKS:(i + 1) * TOKS], same_head[:, :],
                                                sq[:, i, 0, :], start=True, stop=True)
                    last.then_inc(S["ss_done"], 1)
                if full:
                    if not (first and p == 0):
                        pe.wait_ge(S["prod_done"], 2 * n)
                    quad, half, _ = place(p, 0)
                    at = WIN + half * TOKS
                    for i in range(2):
                        for c in range(2):
                            w = [part[:, quad, 2 * i + c, :] for part in wqk]
                            nc.tensor.matmul(proj_ps[:, i, c, :], w[0], xs_high[:, at:at + TOKS], start=True, stop=False)
                            nc.tensor.matmul(proj_ps[:, i, c, :], w[0], xs_rest[:, at:at + TOKS], start=False, stop=False)
                            last = nc.tensor.matmul(proj_ps[:, i, c, :], w[1], xs_high[:, at:at + TOKS],
                                                    start=False, stop=True)
                    last.then_inc(S["proj_done"], 1)
                def values():
                    if live(s, p, LAG_VALUE, first):
                        m = n - LAG_VALUE
                        quad, half, _ = place(p, LAG_VALUE)
                        of = l * NSEQ + s - (1 if p < LAG_VALUE else 0)
                        cols = quad // 2
                        pe.wait_ge(S["pt_done"], 2 * m + 2)
                        pe.wait_ge(S["v_done"], of * len(V_UNITS) + (cols * NBLK + (half + 1) * NB))
                        if p == WO_STEP and not first:
                            pe.wait_ge(S["attn_res"], l * NSEQ + s)
                        elif not (first and p == LAG_VALUE):
                            pe.wait_ge(S["y_done"], m)
                        for pair in range(2):
                            for b in range(NB):
                                for h in range(2):
                                    at = (((quad % 2) * 2 + pair) * 2 + h) * HD
                                    to = pair * TOKS + b * BLK
                                    last = nc.tensor.matmul(
                                        y_bank[HD * h:HD * (h + 1), to:to + BLK],
                                        v[0:KEYS, cols, half * NB + b, at:at + HD],
                                        probs_t[0:KEYS, pair, b, h, :], start=True, stop=True, tile_position=(0, HD * h))
                        last.then_inc(S["pv_done"], 1)

                def transposes():
                    if live(s, p, LAG_SCORE, first):
                        m, par = n - LAG_SCORE, place(p, LAG_SCORE)[2]
                        for h in range(2):
                            pe.wait_ge(S["probs_done"], 2 * m + (h + 1))
                            for b in range(NB):
                                last = nc.tensor.transpose(score_bank[h][0:KEYS, b * P:(b + 1) * P], probs[:, par, h, b, :],
                                                           ident[:, :])
                            last.then_inc(S["tr_done"], 1)

                if not first and p == WO_STEP:
                    if s is NSEQ:
                        ffn_up(l * NSEQ, 0, 2)
                    pe.wait_ge(S["y_done"], step_no(l, s, 0))
                    for a in range(PAIRS):
                        last = nc.tensor.matmul(y_bank[:, :], wo[:, a, :], y_t[:, a, :],
                                                start=(a == 0), stop=(a == PAIRS - 1))
                    last.then_inc(S["wo_done"], 1)
                    transposes()
                    values()
                else:
                    values()
                    if s is NSEQ and p < 2:
                        if p == 0:
                            pe.wait_ge(S["ffn_w"], l * (16 * N_FFN_DMA) + 16 * N_FFN_DMA)
                            pe.wait_ge(S["f_xa"], l * NSEQ + 1)
                            pe.wait_ge(S["prod_done"], 2 * n)
                        else:
                            pe.wait_ge(S["v_done"], (l * NSEQ + NSEQ) * len(V_UNITS))
                        ffn_up(l * NSEQ, 0, p)
                    transposes()
                if full and not first and p in (LN_STEP, LN_STEP + 1):
                    pe.wait_ge(S["guard_done"], n)
                    (ffn_mean if p == LN_STEP else ffn_var)(l * NSEQ + s - 1)

            def ffn_down(f, par, first=False):
                if first:
                    pe.wait_ge(S["attn_res"], f + NSEQ)
                else:
                    pe.wait_ge(S["ffn_res"], f)
                for c, (_, m) in enumerate(CHUNKS):
                    pe.wait_ge(S["f_hid"], f * NC + (c + 1))
                    last = nc.tensor.matmul(y_bank[:, :], w2[0:m, c, :], hid[par][c][0:m, :],
                                            start=(c == 0), stop=(c == NC - 1))
                last.then_inc(S["f_down"], 1)

            def ffn_step(f, s, par, first=False):
                pe.wait_ge(S["f_xa"], f + 1)
                for c in range(NC):
                    pe.wait_ge(S["f_hid"], (f - 1) * NC + (c + 1))
                    ffn_up(f, s, c)
                ffn_down(f - 1, 1 - par, first)

            with pe.Fori(0, depth) as l:
                pe.wait_ge(S["attn_w"], l * (16 * N_ATTN_DMA) + 16 * N_ATTN_DMA)
                pe.wait_ge(S["w_rest"], l + 1)
                steps(pe, l, step)
                f = l * NSEQ + NSEQ - 1
                ffn_step(l * NSEQ + 1, 1, 1, True)
                ffn_mean(f)
                ffn_step(l * NSEQ + 2, 2, 0)
                ffn_var(f)
                ffn_step(l * NSEQ + 3, 3, 1)
                with pe.Fori(2, NSEQ // 2) as s2:
                    for par in range(2):
                        ffn_step(l * NSEQ + s2 * 2 + par, s2 * 2 + par, par)
                ffn_down(l * NSEQ + NSEQ - 1, 1)


def program(nc, d, out, depth=DEPTH):
    with ExitStack() as ctx:
        res_sb = ctx.enter_context(nc.sbuf_tensor("res", [P, TOK], F32))
        u_sb = ctx.enter_context(nc.sbuf_tensor("u", [P, TOK], F32))
        build_stage1(nc, d, res_sb, u_sb)
        build_stage2(nc, d, res_sb, u_sb, out, depth)


def shape_constants():
    f32 = np.float32
    half = np.arange(0, HD, 2, dtype=f32)
    inv_freq = (f32(1.0) / np.power(f32(10000.0), half / f32(HD))).astype(f32)
    t = np.arange(SEQ, dtype=f32)
    angle = (t[:, None] * inv_freq[None, :]).astype(f32).astype(np.float64)
    base = ((half + f32(0.4 * HD)) / f32(1.4 * HD)).astype(f32)
    power = ((t - SEQ // 2) / f32(WIN // 2)).astype(f32)
    scale = np.power(base[None, :].astype(np.float64), power[:, None].astype(np.float64))
    cos, sin = np.cos(angle), np.sin(angle)

    def table(a):
        return np.concatenate([a.T] * QHEADS, axis=0)

    rot_cos = np.stack([-QK_SCALE * table(cos * scale), table(cos / scale)], axis=1).astype(f32)
    rot_sin = np.stack([-QK_SCALE * table(sin * scale), table(sin / scale)], axis=1).astype(f32)
    causal = np.where(np.arange(P)[None, :] > np.arange(P)[:, None], f32(MASKED), f32(0))
    q, k = np.arange(BLK)[:, None], np.arange(KEYS)[None, :]
    band = np.where((k >= q) & (k <= q + WIN), f32(0), f32(MASKED))
    band = np.tile(band[None, :, None, None, :], (2, 1, 2, NB, 1))
    band[:, :, 0, 0, :WIN] = MASKED
    heads = np.arange(P) // HALF_HD
    return {
        "c_ident": np.eye(P, dtype=f32), "c_causal": causal.astype(f32),
        "c_band": band.reshape(P, 2 * NB * KEYS).astype(f32), "c_cos": rot_cos, "c_sin": rot_sin,
        "c_own_rows": (np.arange(P)[:, None] // HD1 == np.arange(HEADS)[None, :]).astype(f32),
        "c_same_head": (heads[:, None] == heads[None, :]).astype(f32),
    }


def lay_out(i):
    def pad_heads(w):
        w = np.asarray(w)
        w = w.reshape(w.shape[:-1] + (HEADS, HD1))
        return np.pad(w, [(0, 0)] * (w.ndim - 1) + [(0, PADH - HD1)]).reshape(w.shape[:-2] + (HEADS * PADH,))

    wo = pad_heads(np.asarray(i["L0_attn_Wo"]).T).T
    qkv = np.asarray(i["L0_ffn_Wqkv"]).reshape(DEPTH, DIM, 3, QUADS, QHEADS, 2, HALF_HD)
    qk_all = qkv[:, :, 0:2].transpose(0, 1, 3, 2, 5, 4, 6)
    q_scale, k_scale = np.asarray(i["L0_ffn_q_scale"]), np.asarray(i["L0_ffn_k_scale"])

    def four(s, half):
        return np.tile(s[:, half * HALF_HD:(half + 1) * HALF_HD], (1, QHEADS))

    b1 = np.asarray(i["L0_ffn_b1"]).reshape(DEPTH, 2, DIM_INNER)
    b1 = np.pad(b1, ((0, 0), (0, 0), (0, NC * P - DIM_INNER))).reshape(DEPTH, 2 * NC, P)
    w2 = np.pad(np.asarray(i["L0_ffn_W2"]), ((0, 0), (0, NC * P - DIM_INNER), (0, 0)))
    arrays = {
        "x": np.asarray(i["L0_attn_x"]).reshape(TOK, DIM).T,
        "a_wq": np.asarray(i["L0_attn_Wq"]), "a_wk": np.asarray(i["L0_attn_Wk"]), "a_wv": pad_heads(i["L0_attn_Wv"]),
        "a_wo": wo.reshape(GROUPS, P, DIM).transpose(1, 0, 2),
        "a_bq": np.asarray(i["L0_attn_bq"])[:, None], "a_bk": np.asarray(i["L0_attn_bk"])[:, None],
        "a_bv": pad_heads(i["L0_attn_bv"]), "a_bo": np.asarray(i["L0_attn_bo"])[:, None],
        "f_wqk": qk_all.reshape(DEPTH, DIM, QUADS * 4 * P),
        "f_wv": np.asarray(i["L0_ffn_Wqkv"])[:, :, 2 * INNER:],
        "f_wo": np.asarray(i["L0_ffn_Wo"]).reshape(DEPTH, PAIRS, P, DIM).transpose(0, 2, 1, 3)
        .reshape(DEPTH, P, PAIRS * DIM),
        "f_qk_scale": np.stack([four(s, half) for s in (q_scale, k_scale) for half in range(2)], axis=2),
        "f_w1": np.asarray(i["L0_ffn_W1"]),
        "f_w2": w2.reshape(DEPTH, NC, P, DIM).transpose(0, 2, 1, 3).reshape(DEPTH, P, NC * DIM),
        "f_vec": np.concatenate([np.asarray(i["L0_ffn_ln_g"])[:, :, None], np.asarray(i["L0_ffn_ln_b"])[:, :, None],
                                 b1.transpose(0, 2, 1), np.asarray(i["L0_ffn_b2"])[:, :, None]], axis=2),
    }
    arrays.update(shape_constants())
    return {k: np.ascontiguousarray(v) for k, v in arrays.items()}


def kernel(**inputs):
    import concourse.bacc as bacc
    from concourse.bass_utils import run_bass_kernel_spmd

    arrays = lay_out(inputs)
    nc = bacc.Bacc("TRN2", target_bir_lowering=False, num_devices=1)
    d = {k: nc.dram_tensor(k, a.shape, mybir.dt.from_np(a.dtype), kind="ExternalInput").ap() for k, a in arrays.items()}
    out = nc.dram_tensor("out", (P, TOK), F32, kind="ExternalOutput").ap()
    program(nc, d, out)
    r = run_bass_kernel_spmd(nc, [arrays], core_ids=[0])
    return np.ascontiguousarray(r.results[0]["out"].T).reshape(NSEQ, SEQ, DIM)
```

```python
from contextlib import ExitStack

import numpy as np

import concourse.bass as bass
from concourse import mybir

F32 = mybir.dt.float32
BF16 = mybir.dt.bfloat16
F32R = mybir.dt.float32r
ACT = mybir.ActivationFunctionType
ALU = mybir.AluOpType
AX = mybir.AxisListType.X

P = 128
NSEQ, SEQ, DIM = 8, 512, 128
TOK = NSEQ * SEQ
HEADS = 16
EPS = 1e-5

HD1, PADH = 8, 32
GROUPS = HEADS * PADH // P
HPG = P // PADH
QB = SEQ // P
UNITS = GROUPS * QB * HPG
SETS = UNITS // HPG
UNIT_LIST = [(g, b, i) for g in range(GROUPS) for b in range(QB) for i in range(HPG)]
TR_LAG, PV_LAG = 4, 7
N_PROBS = 8
WO_AT, RES_LN_AT, X_LN_AT, PREP_AT = 9, 12, 18, 24
PREP_STEP = 3
FIRST_AT, FIRST_STEP = 0, 2
QUERIES, KEYS_OF, VALUES = range(3)
PROJECTIONS = 3 * GROUPS
DIAG_VECTOR, DIAG_POOL = (0, 1, 2), (3,)

DEPTH, HD, WIN = 6, 64, 32
INNER = HEADS * HD
PAIRS = HEADS // 2
HALF_HD = HD // 2
QHEADS = P // HALF_HD
QUADS = HEADS // QHEADS
TOKS = SEQ // 2
STEPS = 2 * QUADS
BLK = 2 * WIN
KEYS = BLK + WIN
NBLK = SEQ // BLK
NB = TOKS // BLK
QK_SCALE = 8.0
DIM_INNER = int(DIM * 4 * 2 / 3)
CHUNKS = [(c, min(P, DIM_INNER - c)) for c in range(0, DIM_INNER, P)]
NC = len(CHUNKS)

MASKED = 1e30


def wait(eng, sem, value):
    if not (isinstance(value, int) and value <= 0):
        eng.wait_ge(sem, value)


def build_stage1(nc, d, res_sb, u_sb):
    with ExitStack() as st:
        def sb(name, shape, dt=F32):
            return st.enter_context(nc.sbuf_tensor(name, shape, dt))

        def sem(name):
            return st.enter_context(nc.semaphore(name))

        bank = [st.enter_context(nc.psum_tensor(f"s1_bank{i}", [P, 512], F32)) for i in range(8)]
        proj_bank, y_bank, tr_bank, score_bank = bank[0], bank[1], bank[2:4], bank[4:8]

        wq = sb("s1_wq", [P, GROUPS * P])
        wk = sb("s1_wk", [P, GROUPS * P])
        wv = sb("s1_wv", [P, GROUPS * P])
        wo = sb("s1_wo", [P, GROUPS, DIM])
        bq = sb("s1_bq", [P, GROUPS])
        bk = sb("s1_bk", [P, GROUPS])
        bv = sb("s1_bv", [P, GROUPS * P])
        bo = sb("s1_bo", [P, 1])
        mean_w = sb("s1_mean_w", [P, P])
        eps = sb("s1_eps", [P, 1])
        ident = sb("s1_ident", [P, P])
        ident_b = sb("s1_ident_b", [P, P], BF16)
        causal = sb("s1_causal", [P, P])
        causal_b = sb("s1_causal_b", [P, P], BF16)
        own_rows = sb("s1_own_rows", [P, HPG])
        xc = sb("s1_xc", [P, SEQ])
        sq = sb("s1_sq", [P, SEQ])
        rstd = sb("s1_rstd", [P, SEQ])
        xn = sb("s1_xn", [P, SEQ])
        q_t = sb("s1_q", [P, SEQ])
        q_split = sb("s1_q_split", [P, SEQ], F32R)
        k_raw = sb("s1_k_raw", [P, SEQ])
        k_t = sb("s1_k", [P, 2, GROUPS, SEQ], F32R)
        q_diag = sb("s1_q_diag", [P, 2, HEADS, SEQ], F32R)
        v = sb("s1_v", [P, 2, QB, GROUPS * P])
        neg_max = sb("s1_neg_max", [P, UNITS])
        den = sb("s1_den", [P, UNITS])
        rden = sb("s1_rden", [P, UNITS])
        probs = sb("s1_probs", [P, N_PROBS, SEQ])
        probs_t = sb("s1_probs_t", [P, 2, HPG, QB, P])
        y_t = sb("s1_y", [P, GROUPS, SEQ])

        names = ("loaded others_loaded const_ready mask_ready ln_mean ln_xc ln_sq ln_var ln_log ln_rstd ln_xn proj_done q_ready "
                 "q_split k_ready k_split "
                 "v_ready diag_vector diag_pool score_done max_done exp_done rden_done probs_done tr_done pt_vector pt_scalar "
                 "pv_done y_ready wo_done res_done").split()
        S = {n: sem("s1_" + n) for n in names}

        loads = [(res_sb[:, 0:SEQ], d["x"][:, 0:SEQ]), (wq[:, :], d["a_wq"]), (wk[:, :], d["a_wk"]), (wv[:, :], d["a_wv"]),
                 (wo[:, :, :], d["a_wo"]), (bq[:, :], d["a_bq"]), (bk[:, :], d["a_bk"]),
                 (bv[:, :], d["a_bv"].partition_broadcast(P)), (bo[:, :], d["a_bo"]),
                 (ident[:, :], d["c_ident"]), (causal[:, :], d["c_causal"]), (own_rows[:, :], d["c_own_rows"])]
        n_loaded = 16 * len(loads)
        block = st.enter_context(nc.Block())

        def seq_of(t, s):
            return t[:, bass.ds(s * SEQ, SEQ)]

        def sequences(eng, prepare, unit, finish):
            def units(s, par, first=False, last=False):
                for t in range(UNITS):
                    unit(s, par, t, first, last)

            prepare(0, 0, 0)
            units(0, 0, first=True)
            with eng.Fori(0, NSEQ // 2 - 1) as pair:
                units(pair * 2 + 1, 1)
                units(pair * 2 + 2, 0)
            units(NSEQ - 1, 1, last=True)
            for t in range(UNITS, UNITS + HPG + PV_LAG):
                unit(NSEQ - 1, 1, t, False, True)
            finish(NSEQ - 1, 2 * NSEQ - 1)

        def event(s, par, t, kind, first):
            early = first and t < PREP_AT
            i, n = divmod(t - (FIRST_AT if early else PREP_AT), FIRST_STEP if early else PREP_STEP)
            g = i // 3 + (1 if early else 0)
            if n or i < 0 or g >= GROUPS or i % 3 != kind:
                return None
            return (s, par, g) if early else (s + 1, 1 - par, g)

        def behind(s, par, t, lag, first):
            u = t - lag
            if u >= UNITS or (u < 0 and first):
                return None
            return (s, par, u) if u >= 0 else (s - 1, 1 - par, UNITS + u)

        def on_vector(u):
            return u % HPG == 0

        def pt(u):
            return S["pt_vector"] if on_vector(u) else S["pt_scalar"]

        def pt_count(s, u):
            if on_vector(u):
                return s * SETS + (u // HPG + 1)
            return s * (SETS * (HPG - 1)) + (u // HPG * (HPG - 1) + u % HPG)

        @block.sync
        def _(sp):
            for dst, src in loads:
                sp.dma_start(dst, src).then_inc(S["loaded"], 16)
            sp.dma_start(res_sb[:, SEQ:], d["x"][:, SEQ:]).then_inc(S["others_loaded"], 16)

        @block.gpsimd
        def _(pool):
            pool.memset(mean_w[:, :], 1.0 / DIM).then_inc(S["const_ready"], 1)
            pool.memset(eps[:, :], EPS).then_inc(S["const_ready"], 1)

            def normalise(s, u):
                n = P * (UNIT_LIST[u][1] + 1)
                pool.wait_ge(S["rden_done"], s * UNITS + (u + 1))
                row = probs[:, u % N_PROBS, 0:n]
                nc.gpsimd.tensor_tensor(row, row, rden[:, u:u + 1].to_broadcast([P, n]), ALU.mult)\
                  .then_inc(S["probs_done"], 1)

            def diag(s, par, h):
                pool.wait_ge(S["q_split"], s * GROUPS + (h // HPG + 1))
                rows = own_rows[:, h % HPG:h % HPG + 1].to_broadcast([P, SEQ])
                nc.gpsimd.tensor_tensor(q_diag[:, par, h, :], q_split[:, :].bitcast(F32), rows, ALU.mult)\
                  .then_inc(S["diag_pool"], 1)

            def prepare(s, par, k):
                pool.wait_ge(S["loaded"], n_loaded)
                for i in DIAG_POOL:
                    diag(s, par, i)

            def unit(s, par, t, first, last):
                if t < UNITS:
                    normalise(s, t)
                if t < UNITS and not last:
                    for n, i in enumerate(DIAG_POOL):
                        of = event(s, par, t - 2 - 2 * n, QUERIES, first)
                        if of:
                            diag(of[0], of[1], of[2] * HPG + i)

            sequences(pool, prepare, unit, lambda s, k: None)

        def copy_out(eng_wait, copy, s, u, first):
            nb, of_set = UNIT_LIST[u][1] + 1, u // HPG
            eng_wait(S["tr_done"], s * UNITS + (u + 1))
            if not (first and of_set < 2):
                eng_wait(S["pv_done"], s * SETS + (of_set - 1))
            return copy(probs_t[:, of_set % 2, u % HPG, 0:nb, :].rearrange("p b q -> p (b q)"),
                        tr_bank[u % 2][:, 0:nb * P])

        @block.scalar
        def _(act):
            act.wait_ge(S["const_ready"], 2)

            def square(k):
                act.wait_ge(S["ln_xc"], k + 1)
                nc.scalar.activation(sq[:, :], xc[:, :], ACT.Square).then_inc(S["ln_sq"], 1)

            def inverse_std(k):
                act.wait_ge(S["ln_var"], k + 1)
                nc.scalar.activation(rstd[:, :], proj_bank[:, :], ACT.Ln, bias=eps[:, 0:1]).then_inc(S["ln_log"], 1)
                act.wait_ge(S["ln_log"], k + 1)
                nc.scalar.activation(rstd[:, :], rstd[:, :], ACT.Exp, scale=-0.5).then_inc(S["ln_rstd"], 1)

            def keys(s, par, g):
                wait(act, S["k_split"], s * GROUPS + g)
                act.wait_ge(S["proj_done"], s * PROJECTIONS + (3 * g + 2))
                for dst in (k_raw[:, :], k_t[:, par, g, :]):
                    last = nc.scalar.activation(dst, proj_bank[:, :], ACT.Identity, bias=bk[:, g:g + 1])
                last.then_inc(S["k_ready"], 1)

            def prepare(s, par, k):
                act.wait_ge(S["loaded"], n_loaded)
                act.preload_act_table_set("natural_log_exp_and_others")
                square(k)
                inverse_std(k)
                keys(s, par, 0)

            def finish(s, k):
                square(k)
                inverse_std(k)

            def unit(s, par, t, first, last):
                if t == 0:
                    act.preload_act_table_set("natural_log_exp_and_others")
                of = behind(s, par, t, TR_LAG, first)
                if of and not on_vector(of[2]):
                    copy_out(act.wait_ge, lambda o, i: nc.scalar.activation(o, i, ACT.Copy), of[0], of[2], first)\
                        .then_inc(S["pt_scalar"], 1)
                if t < UNITS:
                    n = P * (UNIT_LIST[t][1] + 1)
                    act.wait_ge(S["max_done"], s * UNITS + (t + 1))
                    if not (first and t < N_PROBS):
                        act.wait_ge(S["tr_done"], s * UNITS + (t - N_PROBS + 1))
                    nc.scalar.activation(probs[:, t % N_PROBS, 0:n], score_bank[t % 4][:, 0:n], ACT.Exp, scale=-1.0,
                                         bias=neg_max[:, t:t + 1], accum_out=den[:, t:t + 1]).then_inc(S["exp_done"], 1)
                of = behind(s, par, t, PV_LAG + 1, first)
                if of and (of[2] + 1) % (QB * HPG) == 0:
                    g = of[2] // (QB * HPG)
                    act.wait_ge(S["pv_done"], of[0] * SETS + (of[2] + 1) // HPG)
                    if g == 0 and not first:
                        act.wait_ge(S["wo_done"], of[0])
                    nc.scalar.activation(y_t[:, g, :], y_bank[:, :], ACT.Copy).then_inc(S["y_ready"], 1)
                if t < UNITS and not first:
                    if t == RES_LN_AT + 1:
                        square(2 * s)
                    if t == RES_LN_AT + 4:
                        inverse_std(2 * s)
                if t < UNITS and not last:
                    if t == X_LN_AT + 1:
                        square(2 * s + 1)
                    if t == X_LN_AT + 4:
                        inverse_std(2 * s + 1)
                    of = event(s, par, t, KEYS_OF, first)
                    if of:
                        keys(*of)

            sequences(act, prepare, unit, finish)

        @block.vector
        def _(dve):
            dve.wait_ge(S["loaded"], n_loaded)
            nc.vector.tensor_copy(ident_b[:, :], ident[:, :]).then_inc(S["mask_ready"], 1)
            nc.vector.tensor_copy(causal_b[:, :], causal[:, :]).then_inc(S["mask_ready"], 1)

            def centre(k, src):
                wait(dve, S["ln_xn"], k)
                dve.wait_ge(S["ln_mean"], k + 1)
                nc.vector.tensor_tensor(xc[:, :], src, proj_bank[:, :], ALU.subtract).then_inc(S["ln_xc"], 1)

            def divide(k, dst):
                dve.wait_ge(S["ln_rstd"], k + 1)
                nc.vector.tensor_tensor(dst, xc[:, :], rstd[:, :], ALU.mult).then_inc(S["ln_xn"], 1)

            def queries(s, g):
                wait(dve, S["q_split"], s * GROUPS + g)
                dve.wait_ge(S["proj_done"], s * PROJECTIONS + (3 * g + 1))
                wait(dve, S["diag_vector"], (s * GROUPS + g) * len(DIAG_VECTOR))
                wait(dve, S["diag_pool"], (s * GROUPS + g) * len(DIAG_POOL))
                for dst in (q_t[:, :], q_split[:, :]):
                    last = nc.vector.tensor_scalar(dst, proj_bank[:, :], bq[:, g:g + 1], -float(HD1) ** -0.5,
                                                   ALU.add, ALU.mult)
                last.then_inc(S["q_ready"], 1)

            def query_rest(s, g):
                dve.wait_ge(S["q_ready"], s * GROUPS + (g + 1))
                rows = slice(2 * PADH, 3 * PADH)
                nc.vector.tensor_tensor(q_split[rows, :], q_t[rows, :], q_split[rows, :].bitcast(F32), ALU.subtract)\
                  .then_inc(S["q_split"], 1)

            def key_rest(s, par, g):
                dve.wait_ge(S["k_ready"], s * GROUPS + (g + 1))
                rows = slice(PADH, 2 * PADH)
                nc.vector.tensor_tensor(k_t[rows, par, g, :], k_raw[rows, :], k_t[rows, par, g, :].bitcast(F32),
                                        ALU.subtract).then_inc(S["k_split"], 1)

            def values(s, par, b):
                dve.wait_ge(S["proj_done"], s * PROJECTIONS + (3 * b + 3))
                nc.vector.tensor_tensor(v[:, par, b, :], proj_bank[:, :], bv[:, :], ALU.add).then_inc(S["v_ready"], 1)

            def diag(s, par, h):
                dve.wait_ge(S["q_split"], s * GROUPS + (h // HPG + 1))
                nc.vector.tensor_scalar(q_diag[:, par, h, :], q_split[:, :].bitcast(F32),
                                        own_rows[:, h % HPG:h % HPG + 1], None, ALU.mult)\
                  .then_inc(S["diag_vector"], 1)

            def residual(s):
                dve.wait_ge(S["wo_done"], s + 1)
                nc.vector.scalar_tensor_tensor(seq_of(res_sb, s), proj_bank[:, :], bo[:, 0:1], seq_of(res_sb, s),
                                               ALU.add, ALU.add).then_inc(S["res_done"], 1)

            def prepare(s, par, k):
                centre(k, seq_of(res_sb, s))
                divide(k, xn[:, :])
                queries(s, 0)
                query_rest(s, 0)
                for i in DIAG_VECTOR:
                    diag(s, par, i)
                key_rest(s, par, 0)
                values(s, par, 0)

            def finish(s, k):
                residual(s)
                dve.wait_ge(S["res_done"], s + 1)
                centre(k, seq_of(res_sb, s))
                divide(k, seq_of(u_sb, s))

            def unit(s, par, t, first, last):
                if t < UNITS:
                    n = P * (UNIT_LIST[t][1] + 1)
                    dve.wait_ge(S["score_done"], s * UNITS + (t + 1))
                    nc.vector.tensor_reduce(neg_max[:, t:t + 1], score_bank[t % 4][:, 0:n], AX, ALU.min)\
                      .then_inc(S["max_done"], 1)
                of = behind(s, par, t, TR_LAG, first)
                if of and on_vector(of[2]):
                    copy_out(dve.wait_ge, nc.vector.tensor_copy, of[0], of[2], first).then_inc(S["pt_vector"], 1)
                of = behind(s, par, t, 1, first)
                if of:
                    u = of[2]
                    dve.wait_ge(S["exp_done"], of[0] * UNITS + (u + 1))
                    nc.vector.reciprocal(rden[:, u:u + 1], den[:, u:u + 1]).then_inc(S["rden_done"], 1)
                if t < UNITS and not first:
                    if t == WO_AT:
                        residual(s - 1)
                    if t == RES_LN_AT:
                        dve.wait_ge(S["res_done"], s)
                        centre(2 * s, seq_of(res_sb, s - 1))
                    if t == RES_LN_AT + 5:
                        divide(2 * s, seq_of(u_sb, s - 1))
                if t < UNITS and not last:
                    if t == X_LN_AT:
                        dve.wait_ge(S["others_loaded"], 16)
                        centre(2 * s + 1, seq_of(res_sb, s + 1))
                    if t == X_LN_AT + 5:
                        divide(2 * s + 1, xn[:, :])
                    of = event(s, par, t - 1, QUERIES, first)
                    if of:
                        queries(of[0], of[2])
                    of = event(s, par, t - 2, QUERIES, first)
                    if of:
                        query_rest(of[0], of[2])
                    for n, i in enumerate(DIAG_VECTOR):
                        of = event(s, par, t - 3 - n, QUERIES, first)
                        if of:
                            diag(of[0], of[1], of[2] * HPG + i)
                    of = event(s, par, t - 3, KEYS_OF, first)
                    if of:
                        key_rest(*of)
                    of = event(s, par, t - 1, VALUES, first)
                    if of:
                        values(*of)

            sequences(dve, prepare, unit, finish)

        @block.tensor
        def _(pe):
            pe.wait_ge(S["loaded"], n_loaded)
            pe.wait_ge(S["const_ready"], 2)
            pe.wait_ge(S["mask_ready"], 2)

            def mean(src):
                nc.tensor.matmul(proj_bank[:, :], mean_w[:, :], src, start=True, stop=True).then_inc(S["ln_mean"], 1)

            def var(k):
                pe.wait_ge(S["ln_sq"], k + 1)
                nc.tensor.matmul(proj_bank[:, :], mean_w[:, :], sq[:, :], start=True, stop=True).then_inc(S["ln_var"], 1)

            def project(w, g, ready, count):
                pe.wait_ge(ready, count)
                nc.tensor.matmul(proj_bank[:, :], w[:, g * P:(g + 1) * P], xn[:, :], start=True, stop=True)\
                  .then_inc(S["proj_done"], 1)

            def queries(s, k, g):
                if g == 0:
                    project(wq, g, S["ln_xn"], k + 1)
                else:
                    project(wq, g, S["v_ready"], s * QB + g)

            def keys(s, g):
                project(wk, g, S["q_ready"], s * GROUPS + (g + 1))

            def values(s, b):
                pe.wait_ge(S["k_ready"], s * GROUPS + (b + 1))
                nc.tensor.matmul(proj_bank[:, :], xn[:, b * P:(b + 1) * P], wv[:, :], start=True, stop=True)\
                  .then_inc(S["proj_done"], 1)

            def output(s):
                pe.wait_ge(S["y_ready"], s * GROUPS + GROUPS)
                for g in range(GROUPS):
                    last = nc.tensor.matmul(proj_bank[:, :], wo[:, g, :], y_t[:, g, :],
                                            start=(g == 0), stop=(g == GROUPS - 1))
                last.then_inc(S["wo_done"], 1)

            def prepare(s, par, k):
                mean(seq_of(res_sb, s))
                var(k)
                queries(s, k, 0)
                keys(s, 0)
                values(s, 0)

            def finish(s, k):
                output(s)
                pe.wait_ge(S["res_done"], s + 1)
                mean(seq_of(res_sb, s))
                var(k)
                pe.wait_ge(S["ln_xn"], k + 1)

            def unit(s, par, t, first, last):
                if t < UNITS:
                    g, b, i = UNIT_LIST[t]
                    if b == 0 and i == 0:
                        pe.wait_ge(S["diag_vector"], (s * GROUPS + (g + 1)) * len(DIAG_VECTOR))
                        pe.wait_ge(S["diag_pool"], (s * GROUPS + (g + 1)) * len(DIAG_POOL))
                        pe.wait_ge(S["k_split"], s * GROUPS + (g + 1))
                    n = P * (b + 1)
                    if not (first and t < 4):
                        pe.wait_ge(S["exp_done"], s * UNITS + (t - 3))
                    nc.tensor.matmul(score_bank[t % 4][:, 0:n], q_diag[:, par, g * HPG + i, b * P:(b + 1) * P],
                                     k_t[:, par, g, 0:n], start=True, stop=False, skip_group_check=True)
                    nc.tensor.matmul(score_bank[t % 4][:, n - P:n], ident_b[:, :], causal_b[:, :],
                                     start=False, stop=True, skip_group_check=True).then_inc(S["score_done"], 1)
                of = behind(s, par, t, TR_LAG, first)
                if of:
                    us, _, u = of
                    pe.wait_ge(S["probs_done"], us * UNITS + (u + 1))
                    if u >= 2:
                        pe.wait_ge(pt(u - 2), pt_count(us, u - 2))
                    elif not (first and u >= 0):
                        pe.wait_ge(pt(UNITS + u - 2), pt_count(us - 1, UNITS + u - 2))
                    for kb in range(UNIT_LIST[u][1] + 1):
                        done = nc.tensor.transpose(tr_bank[u % 2][:, kb * P:(kb + 1) * P],
                                                   probs[:, u % N_PROBS, kb * P:(kb + 1) * P], ident[:, :])
                    done.then_inc(S["tr_done"], 1)
                of = behind(s, par, t, PV_LAG, first)
                if of and (of[2] + 1) % HPG == 0:
                    us, upar, u = of
                    g, b, _ = UNIT_LIST[u]
                    of_set = u // HPG
                    pe.wait_ge(S["pt_vector"], us * SETS + (of_set + 1))
                    pe.wait_ge(S["pt_scalar"], (us * SETS + (of_set + 1)) * (HPG - 1))
                    if g == 0:
                        pe.wait_ge(S["v_ready"], us * QB + (b + 1))
                    if b == 0 and not (first and g == 0):
                        pe.wait_ge(S["y_ready"], us * GROUPS + g)
                    for kb in range(b + 1):
                        for i in range(HPG):
                            done = nc.tensor.matmul(
                                y_bank[PADH * i:PADH * (i + 1), b * P:(b + 1) * P],
                                v[:, upar, kb, g * P + PADH * i:g * P + PADH * (i + 1)],
                                probs_t[:, of_set % 2, i, kb, :],
                                start=(kb == 0), stop=(kb == b), tile_position=(0, PADH * i))
                    done.then_inc(S["pv_done"], 1)
                if t < UNITS and not first:
                    if t == WO_AT:
                        output(s - 1)
                    if t == RES_LN_AT:
                        pe.wait_ge(S["res_done"], s)
                        mean(seq_of(res_sb, s - 1))
                    if t == RES_LN_AT + 3:
                        var(2 * s)
                if t < UNITS and not last:
                    if t == X_LN_AT:
                        if first:
                            pe.wait_ge(S["v_ready"], QB)
                        else:
                            pe.wait_ge(S["ln_log"], 2 * s + 1)
                        pe.wait_ge(S["others_loaded"], 16)
                        mean(seq_of(res_sb, s + 1))
                    if t == X_LN_AT + 3:
                        var(2 * s + 1)
                    of = event(s, par, t, QUERIES, first)
                    if of:
                        queries(of[0], 2 * s + 1, of[2])
                    of = event(s, par, t, KEYS_OF, first)
                    if of:
                        keys(of[0], of[2])
                    of = event(s, par, t, VALUES, first)
                    if of:
                        values(of[0], of[2])

            sequences(pe, prepare, unit, finish)


V_UNITS = [(half, j) for half in range(2) for j in range(NBLK)]
V_PER_STEP = len(V_UNITS) // STEPS
LAG_MIX, LAG_NORM, LAG_SCORE, LAG_VALUE = 1, 2, 3, 4
WO_STEP = LAG_VALUE
LN_STEP = WO_STEP + 1
POOL_Q = [(head, head // 2) for head in range(1, QHEADS)]
VECTOR_Q = [(0, 0)] + [(head, 1 - head // 2) for head in range(QHEADS)]
LN_SCALE = 2.0 ** 16
NORM_FLOOR = 1e-24


def build_stage2(nc, d, res_sb, u_sb, out, depth):
    with ExitStack() as st:
        def sb(name, shape, dt=F32):
            return st.enter_context(nc.sbuf_tensor(name, shape, dt))

        def sem(name):
            return st.enter_context(nc.semaphore(name))

        proj_ps = st.enter_context(nc.psum_tensor("s2_proj", [P, 2, 2, TOKS], F32))
        bank = [st.enter_context(nc.psum_tensor(f"s2_bank{i}", [P, 512], F32)) for i in range(2, 8)]
        ss_bank, score_bank, v_bank, y_bank = bank[0], bank[1:3], bank[3:5], bank[5]
        up_bank = [tuple(proj_ps[:, i, :, :].rearrange("p a t -> p (a t)") for i in range(2)),
                   (v_bank[0][:, :], v_bank[1][:, :]), (score_bank[0][:, :], score_bank[1][:, :])]

        w_high = sb("s2_w_high", [P, QUADS * 4 * P + INNER], F32R)
        w_rest = sb("s2_w_rest", [P, QUADS * 4 * P + INNER], F32R)
        wqk = [w[:, 0:QUADS * 4 * P].rearrange("p (a b n) -> p a b n", a=QUADS, b=4) for w in (w_high, w_rest)]
        wv = [w[:, QUADS * 4 * P:] for w in (w_high, w_rest)]
        wo = sb("s2_wo", [P, PAIRS, DIM])
        qk_scale = sb("s2_qk_scale", [P, 4])
        w1 = sb("s2_w1", [P, 2 * DIM_INNER])
        w2 = sb("s2_w2", [P, NC, DIM])
        vec = sb("s2_vec", [P, 2 + 2 * NC + 1])
        ln_g, ln_b, b2 = vec[:, 0:1], vec[:, 1:2], vec[:, 2 + 2 * NC:3 + 2 * NC]
        rot_cos = sb("s2_cos", [P, 2, 2, SEQ])
        rot_sin = sb("s2_sin", [P, 2, 2, SEQ])
        ident = sb("s2_ident", [P, P])
        ident_b = sb("s2_ident_b", [P, P], BF16)
        band_b = sb("s2_band_b", [P, 2, NB * KEYS], BF16)
        same_head = sb("s2_same_head", [P, P])
        mean_w = sb("s2_mean_w", [P, P])
        eps = sb("s2_eps", [P, 1])
        ln_shift = sb("s2_ln_shift", [P, 1])
        xs_raw = sb("s2_xs_raw", [P, WIN + SEQ])
        xs_high = sb("s2_xs_high", [P, WIN + SEQ], F32R)
        xs_rest = sb("s2_xs_rest", [P, WIN + SEQ], F32R)
        v = sb("s2_v", [P, 2, NBLK, INNER // 2])
        sq = sb("s2_sq", [P, 2, 2, TOKS])
        by_sin = sb("s2_by_sin", [P, 2, 2, TOKS])
        rotated = sb("s2_rotated", [P, 2, 2, 2, TOKS])
        inv_norm = sb("s2_inv_norm", [P, 2, 2, TOKS])
        q_diag = sb("s2_q_diag", [P, 2, 2, NB, 2, BLK])
        k_t = sb("s2_k", [P, 2, 2, WIN + SEQ])
        neg_max = sb("s2_neg_max", [P, 2, 2, NB])
        den = sb("s2_den", [P, 2, 2, NB])
        rden = sb("s2_rden", [P, 2, 2, NB])
        probs = sb("s2_probs", [P, 2, 2, NB, KEYS])
        probs_t = sb("s2_probs_t", [P, 2, NB, 2, BLK])
        y_t = sb("s2_y", [P, PAIRS, SEQ])
        w_raw = y_t[:, :, :].rearrange("p a t -> p (a t)")[:, 0:QUADS * 4 * P + INNER]
        xf = sb("s2_xf", [P, SEQ])
        xc = sb("s2_xc", [P, SEQ])
        rstd = sb("s2_rstd", [P, SEQ])
        xa = sb("s2_xa", [P, TOK])
        v_flat = v[:, :, :, :].rearrange("p a b n -> p (a b n)")
        gate = [v_flat[:, c * SEQ:(c + 1) * SEQ] for c in range(NC)]
        hid = [[v_flat[:, c * SEQ:(c + 1) * SEQ] for c in range((par + 1) * NC, (par + 2) * NC)] for par in range(2)]

        names = ("const_in consts cast zeroed attn_w ffn_w tables w_high w_rest xs_in xs_high xs_rest proj_done sq_done sqadd_done prod_done "
                 "add_done ss_done guard_done log_done inv_done norm_done qd_done score_done max_done exp_done "
                 "rden_done probs_done tr_done pt_done v_mm v_done pv_done y_done wo_done attn_res "
                 "xf_in f_mean f_xc f_sq f_var f_log f_rstd f_xn f_xa f_up f_gate f_hid f_down ffn_res "
                 "sum_done stored").split()
        S = {n: sem("s2_" + n) for n in names}
        N_ATTN_DMA, N_FFN_DMA = 6, 3
        NQP = len(POOL_Q)

        block = st.enter_context(nc.Block())

        def seq_of(t, s):
            return t[:, bass.ds(s * SEQ, SEQ)]

        def steps(eng, l, body):
            for p in range(STEPS):
                body(l, 0, p, True)
            with eng.Fori(1, NSEQ) as s:
                for p in range(STEPS):
                    body(l, s, p, False)
            for p in range(WO_STEP + 1):
                body(l, NSEQ, p, False)

        def live(s, p, lag, first):
            if first:
                return p >= lag
            return p < lag if isinstance(s, int) else True

        def step_no(l, s, p):
            return l * (NSEQ * STEPS) + s * STEPS + p

        def place(p, lag):
            m = (p - lag) % STEPS
            return m // 2, m % 2, m % 2

        @block.sync
        def _(sp):
            sp.dma_start(ident[:, :], d["c_ident"]).then_inc(S["const_in"], 16)
            sp.dma_start(by_sin[:, :, :, :].rearrange("p a b t -> p (a b t)")[:, 0:2 * NB * KEYS], d["c_band"])\
              .then_inc(S["const_in"], 16)
            sp.dma_start(same_head[:, :], d["c_same_head"]).then_inc(S["const_in"], 16)
            sp.wait_ge(S["zeroed"], 3)
            def layer(l, first):
                def of_layer(name):
                    a = d[name]
                    return (a[0:1] if first else a[bass.ds(l, 1)]).rearrange("o p n -> (o p) n")

                if not first:
                    sp.wait_ge(S["attn_res"], l * NSEQ)
                for dst, src in ((w_raw[:, 0:QUADS * 4 * P], of_layer("f_wqk")),
                                 (w_raw[:, QUADS * 4 * P:], of_layer("f_wv")),
                                 (wo[:, :, :].rearrange("p a n -> p (a n)"), of_layer("f_wo")),
                                 (qk_scale[:, :], of_layer("f_qk_scale")),
                                 (rot_cos[:, :, 0, :], d["c_cos"]), (rot_sin[:, :, 0, :], d["c_sin"])):
                    sp.dma_start(dst, src).then_inc(S["attn_w"], 16)

                def shifted(s):
                    at = s * SEQ if isinstance(s, int) else sp.snap(s * SEQ)
                    if not isinstance(s, int):
                        sp.wait_ge(S["xs_rest"], l * NSEQ + s)
                    sp.dma_start(xs_raw[0:64, WIN:WIN + SEQ], u_sb[0:64, bass.ds(at, SEQ)]).then_inc(S["xs_in"], 16)
                    sp.dma_start(xs_raw[64:128, WIN + 1:WIN + SEQ], u_sb[64:128, bass.ds(at, SEQ - 1)])\
                      .then_inc(S["xs_in"], 16)

                def shifted_ffn(s):
                    at = s * SEQ if isinstance(s, int) else sp.snap(s * SEQ)
                    sp.wait_ge(S["attn_res"], l * NSEQ + s + 1)
                    sp.dma_start(xf[0:64, :], u_sb[0:64, bass.ds(at, SEQ)]).then_inc(S["xf_in"], 16)
                    sp.dma_start(xf[64:128, 1:SEQ], u_sb[64:128, bass.ds(at, SEQ - 1)]).then_inc(S["xf_in"], 16)

                if not first:
                    sp.wait_ge(S["ffn_res"], (l - 1) * NSEQ + 1)
                shifted(0)
                if not first:
                    sp.wait_ge(S["ffn_res"], l * NSEQ)
                for dst, src in ((w1[:, :], of_layer("f_w1")),
                                 (w2[:, :, :].rearrange("p a n -> p (a n)"), of_layer("f_w2")),
                                 (vec[:, :], of_layer("f_vec"))):
                    sp.dma_start(dst, src).then_inc(S["ffn_w"], 16)
                with sp.Fori(1, NSEQ) as s:
                    shifted(s)
                    shifted_ffn(s - 1)
                shifted_ffn(NSEQ - 1)

            layer(0, True)
            if depth > 1:
                with sp.Fori(1, depth) as l:
                    layer(l, False)
            sp.wait_ge(S["sum_done"], 1)
            sp.dma_start(out, res_sb[:, :]).then_inc(S["stored"], 16)
            sp.wait_ge(S["stored"], 16)

        def write_q(eng, p, head, half):
            par = place(p, LAG_NORM)[2]
            src = slice(HALF_HD * head, HALF_HD * (head + 1))
            row = HD * half + HALF_HD * (head % 2)
            return eng.tensor_tensor(
                q_diag[row:row + HALF_HD, par, head // 2, :, head % 2, :],
                rotated[src, par, 0, half, :].rearrange("p (b q) -> p b q", q=BLK),
                inv_norm[src, par, 0, :].rearrange("p (b q) -> p b q", q=BLK), ALU.mult)

        def write_k(eng, p, pair, half):
            quad, toks, par = place(p, LAG_NORM)
            src, dst = slice(HD * pair, HD * (pair + 1)), slice(HD * half, HD * (half + 1))
            at = WIN + toks * TOKS
            return eng.tensor_tensor(k_t[dst, quad % 2, pair, at:at + TOKS], rotated[src, par, 1, half, :],
                                     inv_norm[src, par, 1, :], ALU.mult)

        def copy_out(eng_wait, copy, n, p, first):
            m = n - LAG_VALUE
            if not (first and p == LAG_VALUE):
                eng_wait(S["pv_done"], m)
            for h in range(2):
                eng_wait(S["tr_done"], 2 * m + (h + 1))
                copy(probs_t[0:KEYS, h, :, :, :].rearrange("p b h q -> p (b h q)"), score_bank[h][0:KEYS, :])\
                    .then_inc(S["pt_done"], 1)

        @block.gpsimd
        def _(pool):
            pool.memset(xs_raw[:, 0:WIN + 1], 0.0).then_inc(S["zeroed"], 1)
            pool.memset(xf[:, 0:1], 0.0).then_inc(S["zeroed"], 1)
            pool.memset(k_t[:, :, :, 0:WIN], 0.0).then_inc(S["zeroed"], 1)
            pool.memset(q_diag[:, :, :, :, :, :].rearrange("p a b c h q -> p (a b c h q)"), 0.0).then_inc(S["consts"], 1)
            pool.memset(mean_w[:, :], 1.0 / DIM).then_inc(S["consts"], 1)
            pool.memset(eps[:, :], EPS).then_inc(S["consts"], 1)
            pool.memset(ln_shift[:, :], 0.5 * float(np.log(LN_SCALE))).then_inc(S["consts"], 1)
            pool.wait_ge(S["consts"], 4)

            def step(l, s, p, first):
                n = step_no(l, s, p)

                def rotate(half):
                    par = place(p, LAG_MIX)[2]
                    nc.gpsimd.tensor_tensor(rotated[:, par, :, half, :], rotated[:, par, :, half, :],
                                            by_sin[:, :, 1 - half, :], (ALU.subtract, ALU.add)[half])\
                      .then_inc(S["add_done"], 1)

                def normalise(h, written):
                    m, par = n - LAG_SCORE, place(p, LAG_SCORE)[2]
                    if written is not None:
                        pool.wait_ge(S["qd_done"], written)
                    pool.wait_ge(S["rden_done"], 2 * m + (h + 1))
                    part = probs[:, par, h, :, :]
                    by = rden[:, par, h, :].unsqueeze(2).to_broadcast([P, NB, KEYS])
                    nc.gpsimd.tensor_tensor(part, part, by, ALU.mult).then_inc(S["probs_done"], 1)

                norm, score = live(s, p, LAG_NORM, first), live(s, p, LAG_SCORE, first)
                mix = live(s, p, LAG_MIX, first)
                if p == 0 and live(s, p, 0, first):
                    pool.wait_ge(S["xs_high"], l * NSEQ + s + 1)
                    nc.gpsimd.tensor_tensor(xs_rest[:, :], xs_raw[:, :], xs_high[:, :].bitcast(F32), ALU.subtract)\
                      .then_inc(S["xs_rest"], 1)
                written = NQP * (n - LAG_NORM + 1) if norm else None
                if mix:
                    m = n - LAG_MIX
                    pool.wait_ge(S["sq_done"], m + 1)
                    nc.gpsimd.tensor_tensor(sq[:, :, 0, :], sq[:, :, 0, :], sq[:, :, 1, :], ALU.add)\
                      .then_inc(S["sqadd_done"], 1)
                if norm:
                    m = n - LAG_NORM
                    pool.wait_ge(S["inv_done"], m + 1)
                    pool.wait_ge(S["add_done"], 2 * m + 2)
                    if not (first and p < LAG_NORM + 2):
                        pool.wait_ge(S["score_done"], 2 * m - 2)
                    pool.wait_ge(S["add_done"], 2 * m + 2)
                    if mix:
                        pool.wait_ge(S["sqadd_done"], m + 2)
                    else:
                        pool.wait_ge(S["probs_done"], 2 * (n - LAG_SCORE))
                    for i, (head, half) in enumerate(POOL_Q):
                        if i:
                            pool.wait_ge(S["qd_done"], NQP * m + i)
                        write_q(nc.gpsimd, p, head, half).then_inc(S["qd_done"], 1)
                if score:
                    normalise(0, written)
                    normalise(1, None)
                if mix:
                    if norm and not score:
                        pool.wait_ge(S["qd_done"], written)
                    m = n - LAG_MIX
                    pool.wait_ge(S["prod_done"], 2 * m + 2)
                    rotate(0)
                    rotate(1)

            def tables(l):
                pool.wait_ge(S["attn_w"], l * (16 * N_ATTN_DMA) + 16 * N_ATTN_DMA)
                for half in (1, 0):
                    for i in range(2):
                        by = qk_scale[:, 2 * i + half:2 * i + half + 1].to_broadcast([P, SEQ])
                        for t in (rot_cos, rot_sin):
                            nc.gpsimd.tensor_tensor(t[:, i, half, :], t[:, i, 0, :], by, ALU.mult)\
                              .then_inc(S["tables"], 1)
                    if half:
                        pool.wait_ge(S["tables"], l * 8 + 4)

            tables(0)
            if depth > 1:
                with pool.Fori(0, depth - 1) as l:
                    steps(pool, l, step)
                    tables(l + 1)
                    nc.gpsimd.tensor_copy(w_high[:, :], w_raw).then_inc(S["w_high"], 1)
                    pool.wait_ge(S["w_high"], l + 2)
                    nc.gpsimd.tensor_tensor(w_rest[:, :], w_raw, w_high[:, :].bitcast(F32), ALU.subtract)\
                      .then_inc(S["w_rest"], 1)
            steps(pool, depth - 1, step)

        @block.scalar
        def _(act):
            act.wait_ge(S["consts"], 4)

            def v_unit(l, s, p, i):
                q = p * V_PER_STEP + i
                half, j = V_UNITS[q]
                act.wait_ge(S["v_mm"], (l * NSEQ + s) * len(V_UNITS) + (q + 1))
                nc.scalar.activation(v[0:KEYS, half, j, :], v_bank[i][0:KEYS, :], ACT.Copy).then_inc(S["v_done"], 1)

            def centred_square(f):
                act.wait_ge(S["f_xc"], f + 1)
                nc.scalar.activation(rstd[:, :], xc[:, :], ACT.Square).then_inc(S["f_sq"], 1)

            def inverse_std(f):
                act.wait_ge(S["f_var"], f + 1)
                nc.scalar.activation(rstd[:, :], ss_bank[:, :], ACT.Ln, bias=eps[:, 0:1]).then_inc(S["f_log"], 1)
                act.wait_ge(S["f_log"], f + 1)
                nc.scalar.activation(rstd[:, :], rstd[:, :], ACT.Exp, scale=-0.5).then_inc(S["f_rstd"], 1)

            def step(l, s, p, first):
                n = step_no(l, s, p)
                full = live(s, p, 0, first)
                if p == 0:
                    act.preload_act_table_set("natural_log_exp_and_others")
                f = l * NSEQ + s - 1
                ln = full and not first
                if live(s, p, LAG_VALUE, first) and p > 0:
                    copy_out(act.wait_ge, lambda o, i: nc.scalar.activation(o, i, ACT.Copy), n, p, first)
                if full and p == 0:
                    act.wait_ge(S["xs_in"], (l * NSEQ + s) * 32 + 32)
                    if not first:
                        act.wait_ge(S["proj_done"], n)
                    nc.scalar.activation(xs_high[:, :], xs_raw[:, :], ACT.Copy).then_inc(S["xs_high"], 1)
                if full and p > 0:
                    v_unit(l, s, p, 0)
                if live(s, p, LAG_NORM, first):
                    m, par = n - LAG_NORM, place(p, LAG_NORM)[2]
                    act.wait_ge(S["guard_done"], m + 1)
                    nc.scalar.activation(inv_norm[:, par, :, :], inv_norm[:, par, :, :], ACT.Ln, scale=LN_SCALE)\
                      .then_inc(S["log_done"], 1)
                    act.wait_ge(S["log_done"], m + 1)
                    nc.scalar.activation(inv_norm[:, par, :, :], inv_norm[:, par, :, :], ACT.Exp, scale=-0.5,
                                         bias=ln_shift[:, 0:1]).then_inc(S["inv_done"], 1)
                if ln and p == LN_STEP + 1:
                    centred_square(f)
                if ln and p == LN_STEP + 2:
                    inverse_std(f)
                if live(s, p, LAG_SCORE, first):
                    m, par = n - LAG_SCORE, place(p, LAG_SCORE)[2]
                    if not (first and p < LAG_SCORE + 2):
                        act.wait_ge(S["tr_done"], 2 * m - 2)
                    for h in range(2):
                        act.wait_ge(S["max_done"], 2 * m + (h + 1))
                        for b in range(NB):
                            last = nc.scalar.activation(probs[:, par, h, b, :],
                                                        score_bank[h][:, b * KEYS:(b + 1) * KEYS], ACT.Exp,
                                                        scale=-1.0, bias=neg_max[:, par, h, b:b + 1],
                                                        accum_out=den[:, par, h, b:b + 1])
                        last.then_inc(S["exp_done"], 1)
                if full and p == 0:
                    v_unit(l, s, p, 0)
                if full:
                    v_unit(l, s, p, 1)
                if full:
                    act.wait_ge(S["proj_done"], n + 1)
                    if not (first and p == 0):
                        act.wait_ge(S["ss_done"], n)
                    nc.scalar.activation(sq[:, :, :, :], proj_ps[:, :, :, :], ACT.Square)\
                      .then_inc(S["sq_done"], 1)
                if live(s, p, LAG_VALUE, first):
                    m = n - LAG_VALUE
                    quad, half, _ = place(p, LAG_VALUE)
                    act.wait_ge(S["pv_done"], m + 1)
                    if p == LAG_VALUE and not first:
                        act.wait_ge(S["wo_done"], l * NSEQ + s)
                    nc.scalar.activation(y_t[:, 2 * quad:2 * quad + 2, half * TOKS:(half + 1) * TOKS],
                                         y_bank[:, :].rearrange("p (a t) -> p a t", a=2), ACT.Copy)\
                      .then_inc(S["y_done"], 1)

            def ffn_gate(f):
                for c, (_, m) in enumerate(CHUNKS):
                    act.wait_ge(S["f_up"], f * NC + (c + 1))
                    nc.scalar.activation(gate[c][0:m, :], up_bank[c][1][0:m, :], ACT.Gelu,
                                         bias=vec[0:m, 2 + NC + c:3 + NC + c]).then_inc(S["f_gate"], 1)

            act.wait_ge(S["attn_w"], 16 * N_ATTN_DMA)
            nc.scalar.activation(w_high[:, :], w_raw, ACT.Copy).then_inc(S["w_high"], 1)
            with act.Fori(0, depth) as l:
                steps(act, l, step)
                act.wait_ge(S["ffn_w"], l * (16 * N_FFN_DMA) + 16 * N_FFN_DMA)
                f = l * NSEQ + NSEQ - 1
                ffn_gate(l * NSEQ)
                ffn_gate(l * NSEQ + 1)
                centred_square(f)
                ffn_gate(l * NSEQ + 2)
                inverse_std(f)
                ffn_gate(l * NSEQ + 3)
                with act.Fori(4, NSEQ) as s:
                    ffn_gate(l * NSEQ + s)

        @block.vector
        def _(dve):
            dve.wait_ge(S["const_in"], 48)
            nc.vector.tensor_copy(ident_b[:, :], ident[:, :]).then_inc(S["cast"], 1)
            nc.vector.tensor_copy(band_b[:, :, :].rearrange("p a k -> p (a k)"),
                                  by_sin[:, :, :, :].rearrange("p a b t -> p (a b t)")[:, 0:2 * NB * KEYS])\
              .then_inc(S["cast"], 1)
            dve.wait_ge(S["consts"], 4)
            dve.wait_ge(S["cast"], 2)

            def centre(f):
                dve.wait_ge(S["f_mean"], f + 1)
                nc.vector.tensor_tensor(xc[:, :], xf[:, :], ss_bank[:, :], ALU.subtract).then_inc(S["f_xc"], 1)

            def divide(l, s):
                f = l * NSEQ + s
                dve.wait_ge(S["f_rstd"], f + 1)
                nc.vector.tensor_tensor(xc[:, :], xc[:, :], rstd[:, :], ALU.mult).then_inc(S["f_xn"], 1)

            def scale_shift(l, s):
                f = l * NSEQ + s
                dve.wait_ge(S["ffn_w"], l * (16 * N_FFN_DMA) + 16 * N_FFN_DMA)
                dve.wait_ge(S["f_xn"], f + 1)
                nc.vector.tensor_scalar(seq_of(xa, s), xc[:, :], ln_g, ln_b, ALU.mult, ALU.add).then_inc(S["f_xa"], 1)

            def ffn_hidden(f, par):
                for c, (_, m) in enumerate(CHUNKS):
                    dve.wait_ge(S["f_gate"], f * NC + (c + 1))
                    nc.vector.scalar_tensor_tensor(hid[par][c][0:m, :], up_bank[c][0][0:m, :], vec[0:m, 2 + c:3 + c],
                                                   gate[c][0:m, :], ALU.add, ALU.mult).then_inc(S["f_hid"], 1)

            def step(l, s, p, first):
                n = step_no(l, s, p)
                ln = live(s, p, 0, first) and not first
                if ln and p == LN_STEP + 1:
                    centre(l * NSEQ + s - 1)
                norm, score = live(s, p, LAG_NORM, first), live(s, p, LAG_SCORE, first)

                def least(h):
                    m, par = n - LAG_SCORE, place(p, LAG_SCORE)[2]
                    dve.wait_ge(S["score_done"], 2 * m + (h + 1))
                    nc.vector.tensor_reduce(neg_max[:, par, h, :],
                                            score_bank[h][:, 0:NB * KEYS].rearrange("p (b k) -> p b k", k=KEYS),
                                            AX, ALU.min).then_inc(S["max_done"], 1)

                def inverse_sum(h):
                    m, par = n - LAG_SCORE, place(p, LAG_SCORE)[2]
                    dve.wait_ge(S["exp_done"], 2 * m + (h + 1))
                    nc.vector.reciprocal(rden[:, par, h, :], den[:, par, h, :]).then_inc(S["rden_done"], 1)

                if score:
                    least(0)
                if norm:
                    m = n - LAG_NORM
                    dve.wait_ge(S["inv_done"], m + 1)
                    dve.wait_ge(S["add_done"], 2 * m + 2)
                    if not (first and p < LAG_NORM + 2):
                        dve.wait_ge(S["score_done"], 2 * m - 2)
                    for c in range(2):
                        write_k(nc.vector, p, 0, c)
                if score:
                    least(1)
                if norm:
                    for c in range(2):
                        write_k(nc.vector, p, 1, c)
                if ln and p == LN_STEP + 2:
                    divide(l, s - 1)
                if score:
                    inverse_sum(0)
                if norm:
                    for head, c in VECTOR_Q[:2]:
                        write_q(nc.vector, p, head, c)
                if ln and p == LN_STEP + 2:
                    scale_shift(l, s - 1)
                if score:
                    inverse_sum(1)
                if norm:
                    for head, c in VECTOR_Q[2:]:
                        last = write_q(nc.vector, p, head, c)
                    last.then_inc(S["norm_done"], 1)
                if live(s, p, LAG_MIX, first):
                    m, par = n - LAG_MIX, place(p, LAG_MIX)[2]
                    dve.wait_ge(S["ss_done"], m + 1)
                    if not (first and p < LAG_MIX + 2):
                        dve.wait_ge(S["norm_done"], m - 1)
                        dve.wait_ge(S["qd_done"], NQP * (m - 1))
                    nc.vector.tensor_scalar(inv_norm[:, par, :, :].rearrange("p a t -> p (a t)"), ss_bank[:, :],
                                            NORM_FLOOR, None, ALU.max).then_inc(S["guard_done"], 1)
                if live(s, p, 0, first) and p == STEPS - 1:
                    copy_out(dve.wait_ge, nc.vector.tensor_copy, n + 1, 0, False)
                if live(s, p, 0, first):
                    _, half, par = place(p, 0)
                    toks = slice(half * TOKS, (half + 1) * TOKS)
                    dve.wait_ge(S["sq_done"], n + 1)
                    if not (first and p < 2):
                        dve.wait_ge(S["norm_done"], n - 1)
                        dve.wait_ge(S["qd_done"], NQP * (n - 1))
                    nc.vector.tensor_tensor(rotated[:, par, :, :, :], proj_ps[:, :, :, :], rot_cos[:, :, :, toks],
                                            ALU.mult).then_inc(S["prod_done"], 1)
                    if not (first and p == 0):
                        dve.wait_ge(S["add_done"], 2 * n)
                    nc.vector.tensor_tensor(by_sin[:, :, :, :], proj_ps[:, :, :, :], rot_sin[:, :, :, toks],
                                            ALU.mult).then_inc(S["prod_done"], 1)
                if s is NSEQ and p == WO_STEP:
                    ffn_hidden(l * NSEQ, 0)
                if not first and p == WO_STEP:
                    r = l * NSEQ + s
                    dve.wait_ge(S["wo_done"], r)
                    nc.vector.tensor_tensor(seq_of(u_sb, s - 1), y_bank[:, :], seq_of(u_sb, s - 1), ALU.add)\
                      .then_inc(S["attn_res"], 1)

            def ffn_add(f, s):
                dve.wait_ge(S["f_down"], f + 1)
                nc.vector.scalar_tensor_tensor(seq_of(u_sb, s), y_bank[:, :], b2, seq_of(u_sb, s),
                                               ALU.add, ALU.add).then_inc(S["ffn_res"], 1)

            dve.wait_ge(S["attn_w"], 16 * N_ATTN_DMA)
            dve.wait_ge(S["w_high"], 1)
            nc.vector.tensor_tensor(w_rest[:, :], w_raw, w_high[:, :].bitcast(F32), ALU.subtract)\
              .then_inc(S["w_rest"], 1)
            with dve.Fori(0, depth) as l:
                dve.wait_ge(S["tables"], l * 8 + 8)
                steps(dve, l, step)
                ffn_hidden(l * NSEQ + 1, 1)
                ffn_add(l * NSEQ, 0)
                centre(l * NSEQ + NSEQ - 1)
                ffn_hidden(l * NSEQ + 2, 0)
                ffn_add(l * NSEQ + 1, 1)
                divide(l, NSEQ - 1)
                scale_shift(l, NSEQ - 1)
                ffn_hidden(l * NSEQ + 3, 1)
                ffn_add(l * NSEQ + 2, 2)
                with dve.Fori(2, NSEQ // 2) as s2:
                    for par in range(2):
                        f = l * NSEQ + s2 * 2 + par
                        ffn_hidden(f, par)
                        ffn_add(f - 1, s2 * 2 + par - 1)
                ffn_add(l * NSEQ + NSEQ - 1, NSEQ - 1)
            dve.wait_ge(S["ffn_res"], depth * NSEQ)
            nc.vector.tensor_tensor(res_sb[:, :], res_sb[:, :], u_sb[:, :], ALU.add).then_inc(S["sum_done"], 1)

        @block.tensor
        def _(pe):
            pe.wait_ge(S["const_in"], 48)
            pe.wait_ge(S["consts"], 4)
            pe.wait_ge(S["cast"], 2)

            def v_unit(l, s, p, i, first):
                q = p * V_PER_STEP + i
                half, j = V_UNITS[q]
                if not (first and p == 0):
                    pe.wait_ge(S["v_done"], (l * NSEQ + s) * len(V_UNITS) + (q - V_PER_STEP + 1))
                toks, cols = slice(j * BLK, j * BLK + KEYS), slice(half * (INNER // 2), (half + 1) * (INNER // 2))
                out_ps = v_bank[i][0:KEYS, :]
                nc.tensor.matmul(out_ps, xs_high[:, toks], wv[0][:, cols], start=True, stop=False)
                nc.tensor.matmul(out_ps, xs_high[:, toks], wv[1][:, cols], start=False, stop=False)
                nc.tensor.matmul(out_ps, xs_rest[:, toks], wv[0][:, cols], start=False, stop=True)\
                  .then_inc(S["v_mm"], 1)

            def ffn_mean(f):
                pe.wait_ge(S["xf_in"], f * 32 + 32)
                nc.tensor.matmul(ss_bank[:, :], mean_w[:, :], xf[:, :], start=True, stop=True).then_inc(S["f_mean"], 1)

            def ffn_var(f):
                pe.wait_ge(S["f_sq"], f + 1)
                nc.tensor.matmul(ss_bank[:, :], mean_w[:, :], rstd[:, :], start=True, stop=True)\
                  .then_inc(S["f_var"], 1)

            def ffn_up(f, s, c):
                at, m = CHUNKS[c]
                for i in range(2):
                    last = nc.tensor.matmul(up_bank[c][i][0:m, :], w1[:, i * DIM_INNER + at:i * DIM_INNER + at + m],
                                            seq_of(xa, s), start=True, stop=True)
                last.then_inc(S["f_up"], 1)

            def step(l, s, p, first):
                n = step_no(l, s, p)
                full = live(s, p, 0, first)
                if full and p > 0:
                    v_unit(l, s, p, 0, first)
                if live(s, p, LAG_SCORE, first):
                    m = n - LAG_SCORE
                    quad, half, par = place(p, LAG_SCORE)
                    pe.wait_ge(S["norm_done"], m + 1)
                    pe.wait_ge(S["qd_done"], NQP * (m + 1))
                    for h in range(2):
                        if not (first and p == LAG_SCORE):
                            pe.wait_ge(S["pt_done"], 2 * m + (h - 1))
                        nc.tensor.matmul(score_bank[h][:, 0:NB * KEYS], ident_b[:, :], band_b[:, half, :],
                                         start=True, stop=False, skip_group_check=True)
                        for b in range(NB):
                            at = half * TOKS + b * BLK
                            last = nc.tensor.matmul(
                                score_bank[h][:, b * KEYS:(b + 1) * KEYS],
                                q_diag[:, par, h, b, :, :].rearrange("p h q -> p (h q)"),
                                k_t[:, quad % 2, h, at:at + KEYS], start=False, stop=(b == NB - 1),
                                skip_group_check=True)
                        last.then_inc(S["score_done"], 1)
                if full and p == 0:
                    pe.wait_ge(S["xs_rest"], l * NSEQ + s + 1)
                    v_unit(l, s, p, 0, first)
                if full:
                    v_unit(l, s, p, 1, first)
                if live(s, p, LAG_MIX, first):
                    m = n - LAG_MIX
                    pe.wait_ge(S["sqadd_done"], m + 1)
                    if not (first and p == LAG_MIX):
                        pe.wait_ge(S["guard_done"], m)
                    if full and not first and p == LN_STEP + 1:
                        pe.wait_ge(S["f_xc"], l * NSEQ + s)
                    if full and not first and p == LN_STEP + 2:
                        pe.wait_ge(S["f_log"], l * NSEQ + s)
                    for i in range(2):
                        last = nc.tensor.matmul(ss_bank[:, i * TOKS:(i + 1) * TOKS], same_head[:, :],
                                                sq[:, i, 0, :], start=True, stop=True)
                    last.then_inc(S["ss_done"], 1)
                if full:
                    if not (first and p == 0):
                        pe.wait_ge(S["prod_done"], 2 * n)
                    quad, half, _ = place(p, 0)
                    at = WIN + half * TOKS
                    for i in range(2):
                        for c in range(2):
                            w = [part[:, quad, 2 * i + c, :] for part in wqk]
                            nc.tensor.matmul(proj_ps[:, i, c, :], w[0], xs_high[:, at:at + TOKS], start=True, stop=False)
                            nc.tensor.matmul(proj_ps[:, i, c, :], w[0], xs_rest[:, at:at + TOKS], start=False, stop=False)
                            last = nc.tensor.matmul(proj_ps[:, i, c, :], w[1], xs_high[:, at:at + TOKS],
                                                    start=False, stop=True)
                    last.then_inc(S["proj_done"], 1)
                def values():
                    if live(s, p, LAG_VALUE, first):
                        m = n - LAG_VALUE
                        quad, half, _ = place(p, LAG_VALUE)
                        of = l * NSEQ + s - (1 if p < LAG_VALUE else 0)
                        cols = quad // 2
                        pe.wait_ge(S["pt_done"], 2 * m + 2)
                        pe.wait_ge(S["v_done"], of * len(V_UNITS) + (cols * NBLK + (half + 1) * NB))
                        if p == WO_STEP and not first:
                            pe.wait_ge(S["attn_res"], l * NSEQ + s)
                        elif not (first and p == LAG_VALUE):
                            pe.wait_ge(S["y_done"], m)
                        for pair in range(2):
                            for b in range(NB):
                                for h in range(2):
                                    at = (((quad % 2) * 2 + pair) * 2 + h) * HD
                                    to = pair * TOKS + b * BLK
                                    last = nc.tensor.matmul(
                                        y_bank[HD * h:HD * (h + 1), to:to + BLK],
                                        v[0:KEYS, cols, half * NB + b, at:at + HD],
                                        probs_t[0:KEYS, pair, b, h, :], start=True, stop=True, tile_position=(0, HD * h))
                        last.then_inc(S["pv_done"], 1)

                def transposes():
                    if live(s, p, LAG_SCORE, first):
                        m, par = n - LAG_SCORE, place(p, LAG_SCORE)[2]
                        for h in range(2):
                            pe.wait_ge(S["probs_done"], 2 * m + (h + 1))
                            for b in range(NB):
                                last = nc.tensor.transpose(score_bank[h][0:KEYS, b * P:(b + 1) * P], probs[:, par, h, b, :],
                                                           ident[:, :])
                            last.then_inc(S["tr_done"], 1)

                if not first and p == WO_STEP:
                    if s is NSEQ:
                        ffn_up(l * NSEQ, 0, 2)
                    pe.wait_ge(S["y_done"], step_no(l, s, 0))
                    for a in range(PAIRS):
                        last = nc.tensor.matmul(y_bank[:, :], wo[:, a, :], y_t[:, a, :],
                                                start=(a == 0), stop=(a == PAIRS - 1))
                    last.then_inc(S["wo_done"], 1)
                    transposes()
                    values()
                else:
                    values()
                    if s is NSEQ and p < 2:
                        if p == 0:
                            pe.wait_ge(S["ffn_w"], l * (16 * N_FFN_DMA) + 16 * N_FFN_DMA)
                            pe.wait_ge(S["f_xa"], l * NSEQ + 1)
                            pe.wait_ge(S["prod_done"], 2 * n)
                        else:
                            pe.wait_ge(S["v_done"], (l * NSEQ + NSEQ) * len(V_UNITS))
                        ffn_up(l * NSEQ, 0, p)
                    transposes()
                if full and not first and p in (LN_STEP, LN_STEP + 1):
                    pe.wait_ge(S["guard_done"], n)
                    (ffn_mean if p == LN_STEP else ffn_var)(l * NSEQ + s - 1)

            def ffn_down(f, par, first=False):
                if first:
                    pe.wait_ge(S["attn_res"], f + NSEQ)
                else:
                    pe.wait_ge(S["ffn_res"], f)
                for c, (_, m) in enumerate(CHUNKS):
                    pe.wait_ge(S["f_hid"], f * NC + (c + 1))
                    last = nc.tensor.matmul(y_bank[:, :], w2[0:m, c, :], hid[par][c][0:m, :],
                                            start=(c == 0), stop=(c == NC - 1))
                last.then_inc(S["f_down"], 1)

            def ffn_step(f, s, par, first=False):
                pe.wait_ge(S["f_xa"], f + 1)
                for c in range(NC):
                    pe.wait_ge(S["f_hid"], (f - 1) * NC + (c + 1))
                    ffn_up(f, s, c)
                ffn_down(f - 1, 1 - par, first)

            with pe.Fori(0, depth) as l:
                pe.wait_ge(S["attn_w"], l * (16 * N_ATTN_DMA) + 16 * N_ATTN_DMA)
                pe.wait_ge(S["w_rest"], l + 1)
                steps(pe, l, step)
                f = l * NSEQ + NSEQ - 1
                ffn_step(l * NSEQ + 1, 1, 1, True)
                ffn_mean(f)
                ffn_step(l * NSEQ + 2, 2, 0)
                ffn_var(f)
                ffn_step(l * NSEQ + 3, 3, 1)
                with pe.Fori(2, NSEQ // 2) as s2:
                    for par in range(2):
                        ffn_step(l * NSEQ + s2 * 2 + par, s2 * 2 + par, par)
                ffn_down(l * NSEQ + NSEQ - 1, 1)


def program(nc, d, out, depth=DEPTH):
    with ExitStack() as ctx:
        res_sb = ctx.enter_context(nc.sbuf_tensor("res", [P, TOK], F32))
        u_sb = ctx.enter_context(nc.sbuf_tensor("u", [P, TOK], F32))
        build_stage1(nc, d, res_sb, u_sb)
        build_stage2(nc, d, res_sb, u_sb, out, depth)


def shape_constants():
    f32 = np.float32
    half = np.arange(0, HD, 2, dtype=f32)
    inv_freq = (f32(1.0) / np.power(f32(10000.0), half / f32(HD))).astype(f32)
    t = np.arange(SEQ, dtype=f32)
    angle = (t[:, None] * inv_freq[None, :]).astype(f32).astype(np.float64)
    base = ((half + f32(0.4 * HD)) / f32(1.4 * HD)).astype(f32)
    power = ((t - SEQ // 2) / f32(WIN // 2)).astype(f32)
    scale = np.power(base[None, :].astype(np.float64), power[:, None].astype(np.float64))
    cos, sin = np.cos(angle), np.sin(angle)

    def table(a):
        return np.concatenate([a.T] * QHEADS, axis=0)

    rot_cos = np.stack([-QK_SCALE * table(cos * scale), table(cos / scale)], axis=1).astype(f32)
    rot_sin = np.stack([-QK_SCALE * table(sin * scale), table(sin / scale)], axis=1).astype(f32)
    causal = np.where(np.arange(P)[None, :] > np.arange(P)[:, None], f32(MASKED), f32(0))
    q, k = np.arange(BLK)[:, None], np.arange(KEYS)[None, :]
    band = np.where((k >= q) & (k <= q + WIN), f32(0), f32(MASKED))
    band = np.tile(band[None, :, None, None, :], (2, 1, 2, NB, 1))
    band[:, :, 0, 0, :WIN] = MASKED
    heads = np.arange(P) // HALF_HD
    return {
        "c_ident": np.eye(P, dtype=f32), "c_causal": causal.astype(f32),
        "c_band": band.reshape(P, 2 * NB * KEYS).astype(f32), "c_cos": rot_cos, "c_sin": rot_sin,
        "c_own_rows": ((np.arange(P)[:, None] % PADH // HD1 == np.arange(HPG)[None, :])
                       & (np.arange(P)[:, None] < 3 * PADH)).astype(f32),
        "c_same_head": (heads[:, None] == heads[None, :]).astype(f32),
    }


def lay_out(i):
    def pad_heads(w):
        w = np.asarray(w)
        w = w.reshape(w.shape[:-1] + (HEADS, HD1))
        return np.pad(w, [(0, 0)] * (w.ndim - 1) + [(0, PADH - HD1)]).reshape(w.shape[:-2] + (HEADS * PADH,))

    def four_times(w):
        w = w.reshape(w.shape[0], GROUPS, 1, HPG * HD1)
        return np.tile(w, (1, 1, P // (HPG * HD1), 1)).reshape(w.shape[0], GROUPS * P)

    wo = pad_heads(np.asarray(i["L0_attn_Wo"]).T).T
    qkv = np.asarray(i["L0_ffn_Wqkv"]).reshape(DEPTH, DIM, 3, QUADS, QHEADS, 2, HALF_HD)
    qk_all = qkv[:, :, 0:2].transpose(0, 1, 3, 2, 5, 4, 6)
    q_scale, k_scale = np.asarray(i["L0_ffn_q_scale"]), np.asarray(i["L0_ffn_k_scale"])

    def four(s, half):
        return np.tile(s[:, half * HALF_HD:(half + 1) * HALF_HD], (1, QHEADS))

    b1 = np.asarray(i["L0_ffn_b1"]).reshape(DEPTH, 2, DIM_INNER)
    b1 = np.pad(b1, ((0, 0), (0, 0), (0, NC * P - DIM_INNER))).reshape(DEPTH, 2 * NC, P)
    w2 = np.pad(np.asarray(i["L0_ffn_W2"]), ((0, 0), (0, NC * P - DIM_INNER), (0, 0)))
    arrays = {
        "x": np.asarray(i["L0_attn_x"]).reshape(TOK, DIM).T,
        "a_wq": four_times(np.asarray(i["L0_attn_Wq"])), "a_wk": four_times(np.asarray(i["L0_attn_Wk"])), "a_wv": pad_heads(i["L0_attn_Wv"]),
        "a_wo": wo.reshape(GROUPS, P, DIM).transpose(1, 0, 2),
        "a_bq": four_times(np.asarray(i["L0_attn_bq"])[None]).reshape(GROUPS, P).T,
        "a_bk": four_times(np.asarray(i["L0_attn_bk"])[None]).reshape(GROUPS, P).T,
        "a_bv": pad_heads(i["L0_attn_bv"]), "a_bo": np.asarray(i["L0_attn_bo"])[:, None],
        "f_wqk": qk_all.reshape(DEPTH, DIM, QUADS * 4 * P),
        "f_wv": np.asarray(i["L0_ffn_Wqkv"])[:, :, 2 * INNER:],
        "f_wo": np.asarray(i["L0_ffn_Wo"]).reshape(DEPTH, PAIRS, P, DIM).transpose(0, 2, 1, 3)
        .reshape(DEPTH, P, PAIRS * DIM),
        "f_qk_scale": np.stack([four(s, half) for s in (q_scale, k_scale) for half in range(2)], axis=2),
        "f_w1": np.asarray(i["L0_ffn_W1"]),
        "f_w2": w2.reshape(DEPTH, NC, P, DIM).transpose(0, 2, 1, 3).reshape(DEPTH, P, NC * DIM),
        "f_vec": np.concatenate([np.asarray(i["L0_ffn_ln_g"])[:, :, None], np.asarray(i["L0_ffn_ln_b"])[:, :, None],
                                 b1.transpose(0, 2, 1), np.asarray(i["L0_ffn_b2"])[:, :, None]], axis=2),
    }
    arrays.update(shape_constants())
    return {k: np.ascontiguousarray(v) for k, v in arrays.items()}


def kernel(**inputs):
    import concourse.bacc as bacc
    from concourse.bass_utils import run_bass_kernel_spmd

    arrays = lay_out(inputs)
    nc = bacc.Bacc("TRN2", target_bir_lowering=False, num_devices=1)
    d = {k: nc.dram_tensor(k, a.shape, mybir.dt.from_np(a.dtype), kind="ExternalInput").ap() for k, a in arrays.items()}
    out = nc.dram_tensor("out", (P, TOK), F32, kind="ExternalOutput").ap()
    program(nc, d, out)
    r = run_bass_kernel_spmd(nc, [arrays], core_ids=[0])
    return np.ascontiguousarray(r.results[0]["out"].T).reshape(NSEQ, SEQ, DIM)
```
